# Optimizing a Trainium2 kernel written in Bass

```python
import numpy as np
import jax
import jax.numpy as jnp

def _softmax(x, axis=-1):
    return jax.nn.softmax(x, axis=axis)

def _gelu(x):
    return jax.nn.gelu(x, approximate=True)

def _silu(x):
    return jax.nn.silu(x)

def _sigmoid(x):
    return jax.nn.sigmoid(x)

def _layernorm(x, axis=-1, eps=1e-05):
    m = jnp.mean(x, axis=axis, keepdims=True)
    v = jnp.var(x, axis=axis, keepdims=True)
    return (x - m) / jnp.sqrt(v + eps)

def _scatter_add(tgt, idx, src, axis=0):
    return tgt.at[idx].add(src)

def _segment_sum(src, seg, n):
    return jax.ops.segment_sum(src, seg, n)
kernel_name = 'mk_perceiver_d1_seqx_r2_0cf77b'

def setup_inputs(seed: int=0):
    np.random.seed(seed)
    _w = jnp.asarray

    def _rec_inputs():
        import jax
        import jax.numpy as jnp
        _rk = jax.random.key(seed)
        x = -0.0002928 + 1 * jax.random.normal(jax.random.fold_in(_rk, 1), (64, 32, 512), jnp.float32)
        _lenS = 32 - jax.random.randint(jax.random.fold_in(_rk, 7), (64,), 0, max(1, 32 // 4) + 1, jnp.int32)
        _lenS2 = 257 - jax.random.randint(jax.random.fold_in(_rk, 8), (64,), 0, max(1, 257 // 4) + 1, jnp.int32)
        _ctx_1024P = jax.random.normal(jax.random.fold_in(_rk, 11), (64, 16, 512), jnp.float32)
        _ctx_1024c = jax.random.dirichlet(jax.random.fold_in(_rk, 511), 0.3 * jnp.ones((16,), jnp.float32), (64, 257))
        _ctx_1024t = jnp.einsum('bsk,bkd->bsd', _ctx_1024c, _ctx_1024P)
        _ctx_1024t = _ctx_1024t * jax.lax.rsqrt(jnp.mean(jnp.square(_ctx_1024t)) + 1e-12) * 0.953939
        ctx_1024 = 2.81802e-05 + 1.00001 * (_ctx_1024t + 0.3 * jax.random.normal(jax.random.fold_in(_rk, 611), (64, 257, 512), jnp.float32))
        return (x, ctx_1024)
    x, ctx_1024 = _rec_inputs()

    def _L0_xattn_setup():
        import jax, jax.numpy as jnp
        import numpy as np
        DIM = 512
        NUM_HEADS = 16
        HEAD_DIM = DIM // NUM_HEADS
        ROPE_BASE = 10000.0
        SCALE = 1.0 / np.sqrt(HEAD_DIM)

        def _rotate_half(x):
            x1, x2 = jnp.split(x, 2, axis=-1)
            return jnp.concatenate([-x2, x1], axis=-1)

        def _rope(x, seq_len):
            inv_freq = 1.0 / ROPE_BASE ** (jnp.arange(0, HEAD_DIM, 2, dtype=jnp.float32) / HEAD_DIM)
            t = jnp.arange(seq_len, dtype=jnp.float32)
            freqs = jnp.outer(t, inv_freq)
            emb = jnp.concatenate([freqs, freqs], -1)
            cos = jnp.cos(emb)[None, None]
            sin = jnp.sin(emb)[None, None]
            return x * cos + _rotate_half(x) * sin
        key = jax.random.key(seed)
        ks = jax.random.split(key, 6)
        B, T_q, T_k = (4, 512, 2048)
        s = 1.0 / np.sqrt(DIM)
        return {'x_query': jax.random.normal(ks[0], (B, T_q, DIM), jnp.float32), 'x_kv': jax.random.normal(ks[1], (B, T_k, DIM), jnp.float32), 'Wq': jax.random.normal(ks[2], (DIM, DIM), jnp.float32) * s, 'Wk': jax.random.normal(ks[3], (DIM, DIM), jnp.float32) * s, 'Wv': jax.random.normal(ks[4], (DIM, DIM), jnp.float32) * s, 'Wo': jax.random.normal(ks[5], (DIM, DIM), jnp.float32) * s}
    _L0_xattn_all = _L0_xattn_setup()
    _L0_xattn_in = {k: v for k, v in _L0_xattn_all.items() if k in ('Wq', 'Wk', 'Wv', 'Wo')}
    del _L0_xattn_all

    def _L0_attn_setup():
        import jax, jax.numpy as jnp
        import numpy as np
        import math
        NUM_HEADS = 8
        D_HEAD = 128
        DEPTH = 1
        LAMBDA_INIT = 0.8 - 0.6 * math.exp(-0.3 * DEPTH)
        EPS = 1e-05
        key = jax.random.key(seed)
        ks = jax.random.split(key, 10)
        B, N, D = (2, 1024, 512)
        s = 0.02
        return {'X': jax.random.normal(ks[0], (B, N, D), jnp.float32), 'Wq': jax.random.normal(ks[1], (2 * D_HEAD * NUM_HEADS, D), jnp.float32) * s, 'Wk': jax.random.normal(ks[2], (2 * D_HEAD * NUM_HEADS, D), jnp.float32) * s, 'Wv': jax.random.normal(ks[3], (2 * D_HEAD * NUM_HEADS, D), jnp.float32) * s, 'Wo': jax.random.normal(ks[4], (D, 2 * D_HEAD * NUM_HEADS), jnp.float32) * s, 'lambda_q1': jax.random.normal(ks[5], (NUM_HEADS, D_HEAD), jnp.float32) * 0.1, 'lambda_k1': jax.random.normal(ks[6], (NUM_HEADS, D_HEAD), jnp.float32) * 0.1, 'lambda_q2': jax.random.normal(ks[7], (NUM_HEADS, D_HEAD), jnp.float32) * 0.1, 'lambda_k2': jax.random.normal(ks[8], (NUM_HEADS, D_HEAD), jnp.float32) * 0.1, 'rms_scale': jnp.ones((2 * D_HEAD,), jnp.float32)}
    _L0_attn_all = _L0_attn_setup()
    _L0_attn_in = {k: v for k, v in _L0_attn_all.items() if k in ('Wq', 'Wk', 'Wv', 'Wo', 'lambda_q1', 'lambda_k1', 'lambda_q2', 'lambda_k2', 'rms_scale')}
    del _L0_attn_all

    def _L0_ffn_setup():
        import jax, jax.numpy as jnp
        import numpy as np
        D_MODEL = 512
        HIDDEN = 2048
        N_ROUTING = 2
        key = jax.random.key(seed)
        ks = jax.random.split(key, 10)
        s = 0.02
        x = jax.random.normal(ks[0], (4, 2048, D_MODEL), dtype=jnp.float32)
        gate_w = jax.random.normal(ks[1], (N_ROUTING, D_MODEL), dtype=jnp.float32) * s
        w1 = jax.random.normal(ks[2], (N_ROUTING, D_MODEL, HIDDEN), dtype=jnp.float32) * s
        b1 = jax.random.normal(ks[3], (N_ROUTING, HIDDEN), dtype=jnp.float32) * s
        w2 = jax.random.normal(ks[4], (N_ROUTING, HIDDEN, D_MODEL), dtype=jnp.float32) * s
        b2 = jax.random.normal(ks[5], (N_ROUTING, D_MODEL), dtype=jnp.float32) * s
        sw1 = jax.random.normal(ks[6], (D_MODEL, HIDDEN), dtype=jnp.float32) * s
        sb1 = jax.random.normal(ks[7], (HIDDEN,), dtype=jnp.float32) * s
        sw2 = jax.random.normal(ks[8], (HIDDEN, D_MODEL), dtype=jnp.float32) * s
        sb2 = jax.random.normal(ks[9], (D_MODEL,), dtype=jnp.float32) * s
        return {'x': x, 'gate_w': gate_w, 'w1': w1, 'b1': b1, 'w2': w2, 'b2': b2, 'sw1': sw1, 'sb1': sb1, 'sw2': sw2, 'sb2': sb2}
    _L0_ffn_all = _L0_ffn_setup()
    _L0_ffn_in = {k: v for k, v in _L0_ffn_all.items() if k in ('gate_w', 'w1', 'b1', 'w2', 'b2', 'sw1', 'sb1', 'sw2', 'sb2')}
    del _L0_ffn_all
    return {'x': x, 'ctx_1024': ctx_1024, 'L0_xattn_Wq': _L0_xattn_in['Wq'], 'L0_xattn_Wk': _L0_xattn_in['Wk'], 'L0_xattn_Wv': _L0_xattn_in['Wv'], 'L0_xattn_Wo': _L0_xattn_in['Wo'], 'L0_attn_Wq': _L0_attn_in['Wq'], 'L0_attn_Wk': _L0_attn_in['Wk'], 'L0_attn_Wv': _L0_attn_in['Wv'], 'L0_attn_Wo': _L0_attn_in['Wo'], 'L0_attn_lambda_q1': _L0_attn_in['lambda_q1'], 'L0_attn_lambda_k1': _L0_attn_in['lambda_k1'], 'L0_attn_lambda_q2': _L0_attn_in['lambda_q2'], 'L0_attn_lambda_k2': _L0_attn_in['lambda_k2'], 'L0_attn_rms_scale': _L0_attn_in['rms_scale'], 'L0_ffn_gate_w': _L0_ffn_in['gate_w'], 'L0_ffn_w1': _L0_ffn_in['w1'], 'L0_ffn_b1': _L0_ffn_in['b1'], 'L0_ffn_w2': _L0_ffn_in['w2'], 'L0_ffn_b2': _L0_ffn_in['b2'], 'L0_ffn_sw1': _L0_ffn_in['sw1'], 'L0_ffn_sb1': _L0_ffn_in['sb1'], 'L0_ffn_sw2': _L0_ffn_in['sw2'], 'L0_ffn_sb2': _L0_ffn_in['sb2']}

def reference(x, ctx_1024, L0_xattn_Wq, L0_xattn_Wk, L0_xattn_Wv, L0_xattn_Wo, L0_attn_Wq, L0_attn_Wk, L0_attn_Wv, L0_attn_Wo, L0_attn_lambda_q1, L0_attn_lambda_k1, L0_attn_lambda_q2, L0_attn_lambda_k2, L0_attn_rms_scale, L0_ffn_gate_w, L0_ffn_w1, L0_ffn_b1, L0_ffn_w2, L0_ffn_b2, L0_ffn_sw1, L0_ffn_sb1, L0_ffn_sw2, L0_ffn_sb2):
    import jax
    import jax.numpy as jnp

    def _L0_xattn_ref(x_query, x_kv, Wq, Wk, Wv, Wo):
        import jax, jax.numpy as jnp
        import numpy as np
        DIM = 512
        NUM_HEADS = 16
        HEAD_DIM = DIM // NUM_HEADS
        ROPE_BASE = 10000.0
        SCALE = 1.0 / np.sqrt(HEAD_DIM)

        def _rotate_half(x):
            x1, x2 = jnp.split(x, 2, axis=-1)
            return jnp.concatenate([-x2, x1], axis=-1)

        def _rope(x, seq_len):
            inv_freq = 1.0 / ROPE_BASE ** (jnp.arange(0, HEAD_DIM, 2, dtype=jnp.float32) / HEAD_DIM)
            t = jnp.arange(seq_len, dtype=jnp.float32)
            freqs = jnp.outer(t, inv_freq)
            emb = jnp.concatenate([freqs, freqs], -1)
            cos = jnp.cos(emb)[None, None]
            sin = jnp.sin(emb)[None, None]
            return x * cos + _rotate_half(x) * sin
        B, T_q, _ = x_query.shape
        T_k = x_kv.shape[1]
        h, d = (NUM_HEADS, HEAD_DIM)
        q = (x_query @ Wq.T).reshape(B, T_q, h, d).transpose(0, 2, 1, 3)
        k = (x_kv @ Wk.T).reshape(B, T_k, h, d).transpose(0, 2, 1, 3)
        v = (x_kv @ Wv.T).reshape(B, T_k, h, d).transpose(0, 2, 1, 3)
        q = _rope(q, T_q)
        k = _rope(k, T_k)
        attn = jnp.einsum('bhqd,bhkd->bhqk', q, k) * SCALE
        attn = jax.nn.softmax(attn, axis=-1)
        out = jnp.einsum('bhqk,bhkd->bhqd', attn, v)
        out = out.transpose(0, 2, 1, 3).reshape(B, T_q, DIM)
        return out @ Wo.T

    def _L0_attn_ref(X, Wq, Wk, Wv, Wo, lambda_q1, lambda_k1, lambda_q2, lambda_k2, rms_scale):
        import jax, jax.numpy as jnp
        import numpy as np
        import math
        NUM_HEADS = 8
        D_HEAD = 128
        DEPTH = 1
        LAMBDA_INIT = 0.8 - 0.6 * math.exp(-0.3 * DEPTH)
        EPS = 1e-05
        B, N, D = X.shape
        H, dh = (NUM_HEADS, D_HEAD)

        def proj(W):
            y = jnp.einsum('bnd,ed->bne', X, W)
            return y.reshape(B, N, H, 2 * dh).transpose(0, 2, 1, 3)
        Q = proj(Wq)
        K = proj(Wk)
        V = proj(Wv)
        Q1, Q2 = (Q[..., :dh], Q[..., dh:])
        K1, K2 = (K[..., :dh], K[..., dh:])
        lam1 = jnp.exp(jnp.sum(lambda_q1 * lambda_k1, axis=-1))
        lam2 = jnp.exp(jnp.sum(lambda_q2 * lambda_k2, axis=-1))
        lam = (lam1 - lam2 + LAMBDA_INIT)[None, :, None, None]
        scaling = 1.0 / math.sqrt(dh)
        A1 = jnp.einsum('bhqd,bhkd->bhqk', Q1, K1) * scaling
        A2 = jnp.einsum('bhqd,bhkd->bhqk', Q2, K2) * scaling
        attn = jax.nn.softmax(A1, axis=-1) - lam * jax.nn.softmax(A2, axis=-1)
        O = jnp.einsum('bhqk,bhkd->bhqd', attn, V)
        rms = jnp.sqrt(jnp.mean(O * O, axis=-1, keepdims=True) + EPS)
        O = O / rms * rms_scale
        O = O * (1.0 - LAMBDA_INIT)
        O = O.transpose(0, 2, 1, 3).reshape(B, N, H * 2 * dh)
        return jnp.einsum('bne,de->bnd', O, Wo)

    def _L0_ffn_ref(x, gate_w, w1, b1, w2, b2, sw1, sb1, sw2, sb2):
        import jax, jax.numpy as jnp
        import numpy as np
        D_MODEL = 512
        HIDDEN = 2048
        N_ROUTING = 2
        B, S, D = x.shape
        xf = x.reshape(-1, D)
        gate_scores = xf @ gate_w.T
        gate_probs = jax.nn.softmax(gate_scores, axis=-1)
        top1 = jnp.argmax(gate_probs, axis=-1)
        one_hot = jax.nn.one_hot(top1, N_ROUTING, dtype=xf.dtype)
        masked = xf[None, :, :] * one_hot.T[:, :, None]
        h = jax.nn.relu(jnp.einsum('end,edh->enh', masked, w1) + b1[:, None, :])
        expert_out = jnp.einsum('enh,ehd->end', h, w2) + b2[:, None, :]
        routing_output = expert_out.sum(axis=0)
        shared = jax.nn.relu(xf @ sw1 + sb1) @ sw2 + sb2
        return (routing_output + shared).reshape(B, S, D)
    x = x + _L0_xattn_ref(_layernorm(x, axis=-1), ctx_1024, L0_xattn_Wq, L0_xattn_Wk, L0_xattn_Wv, L0_xattn_Wo)
    x = x + _L0_attn_ref(_layernorm(x, axis=-1), L0_attn_Wq, L0_attn_Wk, L0_attn_Wv, L0_attn_Wo, L0_attn_lambda_q1, L0_attn_lambda_k1, L0_attn_lambda_q2, L0_attn_lambda_k2, L0_attn_rms_scale)
    x = x + _L0_ffn_ref(_layernorm(x, axis=-1), L0_ffn_gate_w, L0_ffn_w1, L0_ffn_b1, L0_ffn_w2, L0_ffn_b2, L0_ffn_sw1, L0_ffn_sb1, L0_ffn_sw2, L0_ffn_sb2)
    return x

_drawn_inputs = setup_inputs


def setup_inputs(seed=0):
    import zlib

    import numpy as np

    out = dict(_drawn_inputs(seed))
    spreads = {'L0_attn_rms_scale': (1.0, 0.2)}
    factors = {'L0_attn_lambda_k1': 4.238,
     'L0_attn_lambda_k2': 5.275,
     'L0_ffn_b1': 4.506,
     'L0_ffn_sb1': 6.043,
     'L0_ffn_sb2': 3.86}
    for name, (base, spread) in spreads.items():
        noise = np.random.default_rng([zlib.crc32(name.encode()), seed]).standard_normal(out[name].shape)
        drawn = base * np.exp(spread * noise) if base else spread * noise
        out[name] = jnp.asarray(drawn.astype(out[name].dtype))
    for name, factor in factors.items():
        out[name] = (out[name] * factor).astype(out[name].dtype)
    return out
```

```python
from contextlib import ExitStack
import math

import concourse.bass as bass
from concourse import mybir

ALU = mybir.AluOpType
ACT = mybir.ActivationFunctionType
AX = mybir.AxisListType
F32 = mybir.dt.float32
F32R = mybir.dt.float32r
BF16 = mybir.dt.bfloat16

P = 128
D = 512
KT = D // P
BATCH = 64
TQ = 32
TK = 257
TKM = TK - 1
TOKENS = BATCH * TQ
TILES = TOKENS // P
GROUP = 512
GROUPS = TOKENS // GROUP
GT = GROUP // P
PAIRS = BATCH // 2
X_HEAD = 32
X_SCALE = 1.0 / math.sqrt(X_HEAD)
HEADS = 8
DH = 128
D_SCALE = 1.0 / math.sqrt(DH)
LAMBDA_INIT = 0.8 - 0.6 * math.exp(-0.3 * 1)
EPS = 1e-5
HIDDEN = 2048
EXPERTS = 3
HC = 512
HT = HC // P
CHUNKS = EXPERTS * HIDDEN // HC
CHUNKS_PER_EXPERT = HIDDEN // HC
MASKED = -(2.0 ** 100)
SHUFFLE_HALVES = [(j + X_HEAD // 2) % X_HEAD for j in range(X_HEAD)]
CONSTS = 3
BN = 6


def f32(ap):
    return ap.bitcast(F32)


def three_pass(pe, out, terms, start=True, stop=True):
    passes = [(a, b) for (a_hi, a_lo), (b_hi, b_lo) in terms for a, b in ((a_hi, b_hi), (a_hi, b_lo), (a_lo, b_hi))]
    for n, (a, b) in enumerate(passes):
        mm = pe.matmul(out, a, b, start=start and n == 0, stop=stop and n == len(passes) - 1)
    return mm


class Norm:

    CHAIN = 4

    def __init__(self, name, sb, pb, sem, x, ident):
        self.x, self.ident = x, ident
        self.stats = sb(name + "_stats", [P, GT, BN])
        self.mean_sum = sb(name + "_mean_sum", [P, GT])
        self.mean_gap = sb(name + "_mean_gap", [P, GT])
        self.mean = sb(name + "_mean", [P, GT])
        self.gap_sq = sb(name + "_gap_sq", [P, GT])
        self.var_sum = sb(name + "_var_sum", [P, GT])
        self.sd = sb(name + "_sd", [P, GT])
        self.rstd = sb(name + "_rstd", [P, GT])
        self.eps = sb(name + "_eps", [P, 1])
        self.xn = sb(name + "_xn", [P, GT, D])
        self.turned = [pb(f"{name}_turned{i}", [P, KT, P]) for i in range(2)]
        self.chain = sem(name + "_chain")
        self.eps_set = sem(name + "_eps_set")
        self.var_ready = sem(name + "_var_ready")
        self.sd_ready = sem(name + "_sd_ready")
        self.xn_ready = sem(name + "_xn_ready")
        self.turn_done = sem(name + "_turn_done")
        self.hi_ready = sem(name + "_hi_ready")
        self.lo_ready = sem(name + "_lo_ready")

    def start(self, dve):
        dve.memset(self.eps[:, :], EPS).then_inc(self.eps_set, 1)

    def vector_stats(self, dve, g):
        for s in range(GT):
            ins = dve.bn_stats(self.stats[:, s, :], self.x[:, bass.ds(g * GT + s, 1), :].rearrange("p a d -> p (a d)"))
        ins.then_inc(self.chain, 1)
        dve.wait_ge(self.chain, g * self.CHAIN + 1)
        dve.tensor_tensor(self.mean_sum[:, :], self.stats[:, :, 1], self.stats[:, :, 4], ALU.add)
        dve.tensor_tensor(self.mean_gap[:, :], self.stats[:, :, 1], self.stats[:, :, 4], ALU.subtract)
        dve.tensor_tensor(self.var_sum[:, :], self.stats[:, :, 2], self.stats[:, :, 5], ALU.add).then_inc(self.chain, 1)
        dve.wait_ge(self.chain, g * self.CHAIN + 2)
        dve.tensor_scalar(self.mean[:, :], self.mean_sum[:, :], 0.5, None, ALU.mult)
        dve.tensor_tensor(self.gap_sq[:, :], self.mean_gap[:, :], self.mean_gap[:, :], ALU.mult).then_inc(self.chain, 1)
        dve.wait_ge(self.chain, g * self.CHAIN + 3)
        dve.scalar_tensor_tensor(self.var_sum[:, :], self.gap_sq[:, :], D / 4.0, self.var_sum[:, :], ALU.mult, ALU.add)\
            .then_inc(self.var_ready, 1)
        dve.wait_ge(self.sd_ready, g + 1)
        dve.reciprocal(self.rstd[:, :], self.sd[:, :]).then_inc(self.chain, 1)
        dve.wait_ge(self.chain, g * self.CHAIN + 4)
        for s in range(GT):
            ins = dve.tensor_scalar(self.xn[:, s, :], self.x[:, bass.ds(g * GT + s, 1), :].rearrange("p a d -> p (a d)"),
                                    self.mean[:, s:s + 1], self.rstd[:, s:s + 1], ALU.subtract, ALU.mult)
        ins.then_inc(self.xn_ready, 1)

    def scalar_sd(self, act, g):
        act.wait_ge(self.var_ready, g + 1)
        act.activation(self.sd[:, :], self.var_sum[:, :], ACT.Sqrt, bias=self.eps[:, :], scale=1.0 / D).then_inc(self.sd_ready, 1)

    def tensor_turn(self, pe, g):
        pe.wait_ge(self.xn_ready, g + 1)
        for s in range(GT):
            if s >= 2:
                pe.wait_ge(self.lo_ready, g * GT + s - 1)
            for k in range(KT):
                mm = pe.transpose(self.turned[s % 2][:, k, :], self.xn[:, s, k * P:(k + 1) * P], self.ident[:, :])
            mm.then_inc(self.turn_done, 1)

    def scalar_hi(self, act, g, hi):
        for s in range(GT):
            act.wait_ge(self.turn_done, g * GT + s + 1)
            act.activation(hi(s), self.turned[s % 2][:, :, :], ACT.Copy).then_inc(self.hi_ready, 1)

    def vector_lo(self, dve, g, hi, lo):
        for s in range(GT):
            dve.wait_ge(self.hi_ready, g * GT + s + 1)
            dve.tensor_tensor(lo(s), self.turned[s % 2][:, :, :], f32(hi(s)), ALU.subtract).then_inc(self.lo_ready, 1)


def block_a(nc, sb, pb, sem, io, x, ident, cos_k, sin_k, key_last, weights, const_loaded):
    names = ("Wq", "Wk", "Wv", "Wo")
    wq = (sb("wq_hi", [P, KT, D], F32R), sb("wq_lo", [P, KT, D], F32R))
    split = {"Wq": wq, "Wk": weights[0], "Wv": weights[1], "Wo": weights[2]}
    w_raw = [sb(f"w_raw{i}", [P, KT, D]) for i in range(2)]
    norm = Norm("n1", sb, pb, sem, x, ident)
    xt_hi, xt_lo = sb("xt_hi", [P, KT, GROUP], F32R), sb("xt_lo", [P, KT, GROUP], F32R)
    last_raw = sb("last_raw", [P, KT, P])
    last_hi, last_lo = sb("last_hi", [P, KT, P], F32R), sb("last_lo", [P, KT, P], F32R)
    cos_part = sb("cos_part", [P, GROUP])
    sin_part = sb("sin_part", [P, GROUP])
    value_last = sb("value_last", [BATCH, D])
    queries = sb("queries", [P, KT, TOKENS])
    proj = [pb(f"proj_a{i}", [P, D]) for i in range(2)]

    x_loaded = sem("x_loaded")
    w_loaded = [sem(f"w_loaded_{n}") for n in names]
    w_hi = sem("w_hi")
    w_lo = sem("w_lo")
    last_zeroed = sem("last_zeroed")
    last_loaded = sem("last_loaded")
    last_hi_ready = sem("last_hi_ready")
    last_lo_ready = sem("last_lo_ready")
    q_done = sem("q_done")
    q_halves = sem("q_halves")
    q_sin = sem("q_sin")
    q_ready = sem("q_ready")
    Q_CREDIT = 1
    last_done = sem("last_done")
    last_read = sem("last_read")
    last_turned = sem("last_turned")
    v_last_ready = sem("v_last_ready")
    v_last_stored = sem("v_last_stored")
    q_stored = sem("q_stored")

    with nc.Block() as block:
        @block.sync
        def _(sp):
            x_v = io["x"].rearrange("(t p) d -> p t d", p=P)
            sp.dma_start(w_raw[0][:, :, :], io["Wq"].rearrange("(k p) n -> p k n", p=P)).then_inc(w_loaded[0], 16)
            for g in range(GROUPS):
                sp.dma_start(x[:, g * GT:(g + 1) * GT, :], x_v[:, g * GT:(g + 1) * GT, :]).then_inc(x_loaded, 16)
            sp.dma_start(w_raw[1][:, :, :], io["Wk"].rearrange("(k p) n -> p k n", p=P)).then_inc(w_loaded[1], 16)
            sp.wait_ge(last_zeroed, 1)
            sp.dma_start(last_raw[:, :, 0:BATCH], io["ctx_last"].rearrange("(k p) n -> p k n", p=P)).then_inc(last_loaded, 16)
            for n in (2, 3):
                sp.wait_ge(w_lo, n - 1)
                sp.dma_start(w_raw[n % 2][:, :, :], io[names[n]].rearrange("(k p) n -> p k n", p=P)).then_inc(w_loaded[n], 16)
            for g in range(GROUPS):
                sp.wait_ge(q_ready, KT * (g + 1) + Q_CREDIT)
                sp.dma_start(io["queries"][:, :, g * GROUP:(g + 1) * GROUP], queries[:, :, g * GROUP:(g + 1) * GROUP])\
                    .then_inc(q_stored, 16)
            sp.wait_ge(v_last_ready, 1)
            sp.dma_start(io["v_last"], value_last[:, :]).then_inc(v_last_stored, 16)
            sp.wait_ge(v_last_stored, 16)
            sp.wait_ge(q_stored, 16 * GROUPS)

        @block.gpsimd
        def _(gp):
            gp.memset(last_raw[:, :, BATCH:P], 0.0).then_inc(last_zeroed, 1)
            for n in range(4):
                gp.wait_ge(w_hi, n + 1)
                gp.tensor_tensor(split[names[n]][1][:, :, :], w_raw[n % 2][:, :, :], f32(split[names[n]][0][:, :, :]),
                                 ALU.subtract).then_inc(w_lo, 1)
                if n == 0:
                    gp.wait_ge(const_loaded, 16 * CONSTS)
                    sin_q = sin_k[:, 0:TQ].unsqueeze(1).broadcast_to([P, GROUP // TQ, TQ])
                    with gp.Fori(0, GROUPS) as g:
                        for t in range(KT):
                            gp.wait_ge(q_halves, g * KT + t + 1)
                            part = sin_part[:, :].rearrange("p (b q) -> p b q", q=TQ)
                            gp.tensor_tensor(part, part, sin_q, ALU.mult).then_inc(q_sin, 1)
                if n == 1:
                    gp.wait_ge(last_hi_ready, 1)
                    gp.tensor_tensor(last_lo[:, :, :], last_raw[:, :, :], f32(last_hi[:, :, :]), ALU.subtract)\
                        .then_inc(last_lo_ready, 1)

        @block.scalar
        def _(act):
            act.wait_ge(w_loaded[0], 16)
            act.activation(wq[0][:, :, :], w_raw[0][:, :, :], ACT.Copy).then_inc(w_hi, 1)
            act.wait_ge(norm.eps_set, 1)
            with act.Fori(0, GROUPS) as g:
                norm.scalar_sd(act, g)
                norm.scalar_hi(act, g, lambda s: xt_hi[:, :, s * P:(s + 1) * P])
            for n in range(1, 4):
                act.wait_ge(w_loaded[n], 16)
                act.activation(split[names[n]][0][:, :, :], w_raw[n % 2][:, :, :], ACT.Copy).then_inc(w_hi, 1)
                if n == 1:
                    act.wait_ge(last_loaded, 16)
                    act.activation(last_hi[:, :, :], last_raw[:, :, :], ACT.Copy).then_inc(last_hi_ready, 1)
            act.wait_ge(last_done, KT + 1)
            act.activation(value_last[:, :], proj[0][0:BATCH, :], ACT.Copy).then_inc(v_last_ready, 1)

        @block.tensor
        def _(pe):
            pe.wait_ge(const_loaded, 16 * CONSTS)
            pe.wait_ge(w_lo, 1)
            pe.wait_ge(w_hi, 1)
            with pe.Fori(0, GROUPS) as g:
                norm.tensor_turn(pe, g)
                pe.wait_ge(norm.lo_ready, g * GT + GT)
                for t in range(KT):
                    if t >= 2:
                        pe.wait_ge(q_halves, g * KT + t - 1)
                    cols = slice(t * P, (t + 1) * P)
                    three_pass(pe, proj[t % 2][:, :], [((wq[0][:, k, cols], wq[1][:, k, cols]),
                                                        (xt_hi[:, k, :], xt_lo[:, k, :])) for k in range(KT)])\
                        .then_inc(q_done, 1)
            pe.wait_ge(w_lo, 2)
            pe.wait_ge(last_lo_ready, 1)
            for t in range(KT):
                pe.wait_ge(q_ready, GROUPS * KT + Q_CREDIT) if t == 0 else None
                if t >= 2:
                    pe.wait_ge(last_read, t - 1)
                cols = slice(t * P, (t + 1) * P)
                three_pass(pe, proj[t % 2][:, 0:P], [((weights[0][0][:, k, cols], weights[0][1][:, k, cols]),
                                                      (last_hi[:, k, :], last_lo[:, k, :])) for k in range(KT)])\
                    .then_inc(last_done, 1)
            pe.wait_ge(w_lo, 3)
            pe.wait_ge(last_read, KT)
            three_pass(pe, proj[0][:, :], [((last_hi[:, k, :], last_lo[:, k, :]),
                                            (weights[1][0][:, k, :], weights[1][1][:, k, :])) for k in range(KT)])\
                .then_inc(last_done, 1)

        @block.vector
        def _(dve):
            dve.sem_inc(q_ready, Q_CREDIT)
            norm.start(dve)
            dve.wait_ge(x_loaded, 16 * GROUPS)
            dve.wait_ge(const_loaded, 16 * CONSTS)
            cos_q = cos_k[:, 0:TQ].unsqueeze(1).broadcast_to([P, GROUP // TQ, TQ])
            with dve.Fori(0, GROUPS) as g:
                norm.vector_stats(dve, g)
                norm.vector_lo(dve, g, lambda s: xt_hi[:, :, s * P:(s + 1) * P], lambda s: xt_lo[:, :, s * P:(s + 1) * P])
                for t in range(KT):
                    dve.wait_ge(q_done, g * KT + t + 1)
                    dve.wait_ge(q_ready, g * KT + t + Q_CREDIT)
                    dve.tensor_tensor(cos_part[:, :].rearrange("p (b q) -> p b q", q=TQ),
                                      proj[t % 2][:, :].rearrange("p (b q) -> p b q", q=TQ), cos_q, ALU.mult)
                    dve.stream_shuffle(sin_part[:, :], proj[t % 2][:, :], SHUFFLE_HALVES).then_inc(q_halves, 1)
                    dve.wait_ge(q_sin, g * KT + t + 1)
                    dve.tensor_tensor(queries[:, t, bass.ds(g * GROUP, GROUP)], cos_part[:, :], sin_part[:, :], ALU.add)\
                        .then_inc(q_ready, 1)
            for t in range(KT):
                if t == 0:
                    dve.wait_ge(q_ready, GROUPS * KT + Q_CREDIT)
                else:
                    dve.wait_ge(last_read, t)
                dve.wait_ge(last_done, t + 1)
                dve.stream_shuffle(sin_part[:, 0:BATCH], proj[t % 2][:, 0:BATCH], SHUFFLE_HALVES).then_inc(last_turned, 1)
                dve.wait_ge(last_turned, 2 * t + 1)
                dve.tensor_scalar(sin_part[:, 0:BATCH], sin_part[:, 0:BATCH], sin_k[:, TKM:TK], None, ALU.mult)\
                    .then_inc(last_turned, 1)
                dve.wait_ge(last_turned, 2 * t + 2)
                dve.scalar_tensor_tensor(key_last[:, t, :], proj[t % 2][:, 0:BATCH], cos_k[:, TKM:TK],
                                         sin_part[:, 0:BATCH], ALU.mult, ALU.add).then_inc(last_read, 1)


def block_b(nc, sb, pb, sem, io, x, ident, cos_k, sin_k, key_last, weights):
    wk, wv, wo = weights
    ctx_raw = [sb(f"ctx_raw{i}", [P, KT, 2 * TKM]) for i in range(2)]
    ctx_hi = [sb(f"ctx_hi{i}", [P, KT, 2 * TKM], F32R) for i in range(2)]
    ctx_lo = [sb(f"ctx_lo{i}", [P, KT, 2 * TKM], F32R) for i in range(2)]
    keys = [sb(f"keys{i}", [P, KT, 2, TK]) for i in range(2)]
    values = [sb(f"values{i}", [P, 4, D]) for i in range(2)]
    v_last = [sb(f"v_last{i}", [1, 2, D]) for i in range(2)]
    q_pair = [sb(f"q_pair{i}", [P, KT, 2 * TQ]) for i in range(2)]
    q_diag = [sb(f"q_diag{i}", [P, KT, 2, P]) for i in range(2)]
    cos_part = [sb(f"cos_b{i}", [P, 2 * TKM]) for i in range(2)]
    sin_part = [sb(f"sin_b{i}", [P, 2 * TKM]) for i in range(2)]
    row_max = sb("row_max", [P, 2])
    neg_max = sb("neg_max", [P, 2])
    row_sum = sb("row_sum", [P, 2])
    row_inv = sb("row_inv", [P, 2])
    probs = sb("probs", [P, 2, TK])
    probs_t = sb("probs_t", [P, 2, 3 * P])
    heads_t = sb("heads_t", [P, KT, P])
    heads_hi, heads_lo = sb("heads_hi", [P, KT, P], F32R), sb("heads_lo", [P, KT, P], F32R)
    proj = [pb(f"proj_b{i}", [P, D]) for i in range(2)]
    scores = pb("scores_b", [P, 2, 512])
    turned = pb("turned_b", [P, 2, 512])
    heads = [pb(f"heads_b{i}", [P, 2, 2, P]) for i in range(2)]

    zeroed = sem("b_zeroed")
    turned_zeroed = sem("b_turned_zeroed")
    ctx_loaded = [sem(f"ctx_loaded{i}") for i in range(2)]
    v_last_loaded = [sem(f"v_last_loaded{i}") for i in range(2)]
    q_loaded = [sem(f"q_loaded{i}") for i in range(2)]
    ctx_hi_ready = sem("ctx_hi_ready")
    ctx_lo_ready = sem("ctx_lo_ready")
    q_diag_ready = sem("q_diag_ready")
    proj_done = sem("proj_done")
    v_ready = sem("v_ready")
    k_read = sem("k_read")
    k_sin = sem("k_sin")
    k_ready = sem("k_ready")
    s_done = sem("s_done")
    max_ready = sem("max_ready")
    neg_max_ready = sem("neg_max_ready")
    exp_done = sem("exp_done")
    inv_ready = sem("inv_ready")
    p_ready = sem("p_ready")
    t_done = sem("t_done")
    pt_ready = sem("pt_ready")
    pv_done = sem("pv_done")
    heads_read = sem("heads_read")
    heads_hi_ready = sem("heads_hi_ready")
    heads_lo_ready = sem("heads_lo_ready")
    wo_done = sem("b_wo_done")
    x_added = sem("b_x_added")

    ctx_v = io["ctx_main"].rearrange("(k p) n -> p k n", p=P)
    v_last_v = io["v_last"].rearrange("(a b) d -> a b d", a=1)
    LOOPS = (PAIRS - 2) // 2

    def phases(eng, phase):
        with eng.Fori(0, LOOPS) as u:
            for j in range(2):
                phase(u * 2 + j, j, True, True, u)
        phase(PAIRS - 2, 0, True, False, LOOPS)
        phase(PAIRS - 1, 1, False, False, LOOPS)

    with nc.Block() as block:
        @block.sync
        def _(sp):
            def load_ctx(r, par):
                sp.dma_start(ctx_raw[par][:, :, :], ctx_v[:, :, bass.ds(r * 2 * TKM, 2 * TKM)]).then_inc(ctx_loaded[par], 16)

            def load_v_last(r, par):
                sp.dma_start(v_last[par][:, :, :], v_last_v[:, bass.ds(r * 2, 2), :]).then_inc(v_last_loaded[par], 16)

            def load_q(r, par):
                sp.dma_start(q_pair[par][:, :, :], io["queries"][:, :, bass.ds(r * 2 * TQ, 2 * TQ)]).then_inc(q_loaded[par], 16)

            for r in range(2):
                load_ctx(r, r)
                load_v_last(r, r)
                load_q(r, r)
            for r in range(2, 4):
                sp.wait_ge(ctx_lo_ready, 4 * (r - 1))
                load_ctx(r, r % 2)
            with sp.Fori(0, (PAIRS - 4) // 2) as u:
                for j in range(2):
                    p = u * 2 + j
                    sp.wait_ge(ctx_lo_ready, 4 * (p + 3))
                    load_ctx(p + 4, j)
                    sp.wait_ge(pv_done, 4 * (p + 1))
                    load_v_last(p + 2, j)
                    sp.wait_ge(q_diag_ready, p + 1)
                    load_q(p + 2, j)
            for p in range(PAIRS - 4, PAIRS - 2):
                sp.wait_ge(pv_done, 4 * (p + 1))
                load_v_last(p + 2, p % 2)
                sp.wait_ge(q_diag_ready, p + 1)
                load_q(p + 2, p % 2)

        @block.gpsimd
        def _(gp):
            def split_lo(r, par):
                for k in range(KT):
                    gp.wait_ge(ctx_hi_ready, 4 * r + k + 1)
                    gp.tensor_tensor(ctx_lo[par][:, k, :], ctx_raw[par][:, k, :], f32(ctx_hi[par][:, k, :]), ALU.subtract)\
                        .then_inc(ctx_lo_ready, 1)

            def sines(r):
                for t in range(KT):
                    gp.wait_ge(k_read, 4 * r + t + 1)
                    part = sin_part[t % 2][:, :].rearrange("p (b k) -> p b k", k=TKM)
                    gp.tensor_tensor(part, part, sin_k[:, 0:TKM].unsqueeze(1).broadcast_to([P, 2, TKM]), ALU.mult)\
                        .then_inc(k_sin, 1)

            for par in range(2):
                ins = gp.memset(q_diag[par][:, :, :, :], 0.0)
            ins.then_inc(zeroed, 1)
            split_lo(0, 0)
            split_lo(1, 1)
            sines(0)

            def phase(p, par, projects, splits, u):
                if splits:
                    split_lo(p + 2, par)
                if projects:
                    sines(p + 1)

            phases(gp, phase)

        @block.scalar
        def _(act):
            def value_out(r, m, par):
                act.wait_ge(proj_done, 8 * r + m + 1)
                act.activation(values[par][:, m, :], proj[m % 2][:, :], ACT.Copy).then_inc(v_ready, 1)

            def split_hi(r, k, par, count):
                if k == 0:
                    act.wait_ge(ctx_loaded[par], 16 * count)
                act.activation(ctx_hi[par][:, k, :], ctx_raw[par][:, k, :], ACT.Copy).then_inc(ctx_hi_ready, 1)

            def exps(p, n):
                act.wait_ge(neg_max_ready, 4 * p + n + 1)
                for b in range(2):
                    ins = act.activation(probs[:, b, :], scores[:, b, 0:TK], ACT.Exp, bias=neg_max[:, b:b + 1], scale=X_SCALE,
                                         accum_out=row_sum[:, b:b + 1])
                ins.then_inc(exp_done, 1)

            def probs_out(p, n):
                act.wait_ge(t_done, 4 * p + n + 1)
                act.activation(probs_t[:, :, :], turned[:, :, 0:3 * P], ACT.Copy).then_inc(pt_ready, 1)

            def heads_out(p, half, par):
                act.wait_ge(pv_done, 4 * p + 2 * half + 2)
                for a in range(4):
                    rows = slice(a * X_HEAD, (a + 1) * X_HEAD)
                    ins = act.activation(
                        heads_t[rows, 2 * half:2 * half + 2, par * 2 * TQ:(par + 1) * 2 * TQ].rearrange("p t (b q) -> p t b q", q=TQ),
                        heads[half][rows, :, :, rows], ACT.Copy)
                ins.then_inc(heads_read, 1)

            for r in range(2):
                for k in range(KT):
                    split_hi(r, k, r, 1)
            for m in range(4):
                value_out(0, m, 0)

            def phase(p, par, projects, splits, u):
                for n in range(4):
                    if n:
                        probs_out(p, n - 1)
                    exps(p, n)
                    if projects:
                        value_out(p + 1, n, 1 - par)
                    if splits:
                        split_hi(p + 2, n, par, u + 2)
                probs_out(p, 3)
                heads_out(p, 0, par)
                heads_out(p, 1, par)
                if par:
                    act.wait_ge(heads_read, 2 * p + 2)
                    act.activation(heads_hi[:, :, :], heads_t[:, :, :], ACT.Copy).then_inc(heads_hi_ready, 1)

            phases(act, phase)

        @block.tensor
        def _(pe):
            def project(r, m, par):
                if m == 0:
                    pe.wait_ge(ctx_lo_ready, 4 * r + 4)
                    pe.wait_ge(ctx_hi_ready, 4 * r + 4)
                if m < 2:
                    if not isinstance(r, int) or r > 0:
                        pe.wait_ge(k_read, 4 * r - 1 + m)
                elif m < 6:
                    pe.wait_ge(v_ready, 4 * r + m - 1)
                else:
                    pe.wait_ge(k_read, 4 * r + m - 5)
                hi, lo = ctx_hi[par], ctx_lo[par]
                if m < 4:
                    rows = slice(m * P, (m + 1) * P)
                    terms = [((hi[:, k, rows], lo[:, k, rows]), (wv[0][:, k, :], wv[1][:, k, :])) for k in range(KT)]
                else:
                    cols = slice((m - 4) * P, (m - 3) * P)
                    terms = [((wk[0][:, k, cols], wk[1][:, k, cols]), (hi[:, k, :], lo[:, k, :])) for k in range(KT)]
                three_pass(pe, proj[m % 2][:, :], terms).then_inc(proj_done, 1)

            def score(p, n, par):
                if n == 0:
                    pe.wait_ge(q_diag_ready, p + 1)
                pe.wait_ge(k_ready, 4 * p + n + 1)
                for b in range(2):
                    mm = pe.matmul(scores[:, b, 0:TK], q_diag[par][:, n, b, :], keys[par][:, n, b, :], start=True, stop=True)
                mm.then_inc(s_done, 1)

            def turn(p, n):
                pe.wait_ge(p_ready, 4 * p + n + 1)
                for b in range(2):
                    for c in range(2):
                        pe.transpose(turned[:, b, c * P:(c + 1) * P], probs[:, b, c * P:(c + 1) * P], ident[:, :])
                    mm = pe.transpose(turned[0:1, b, 2 * P:3 * P], probs[:, b, TKM:TK], ident[:, :])
                mm.then_inc(t_done, 1)

            def attend(p, n, par, count):
                if n == 0:
                    pe.wait_ge(v_ready, 4 * p + 4)
                    pe.wait_ge(v_last_loaded[par], 16 * count)
                pe.wait_ge(pt_ready, 4 * p + n + 1)
                cols = slice(n * P, (n + 1) * P)
                for b in range(2):
                    out = heads[n // 2][:, n % 2, b, :]
                    for c in range(2):
                        pe.matmul(out, values[par][:, 2 * b + c, cols], probs_t[:, b, c * P:(c + 1) * P],
                                  start=(c == 0), stop=False)
                    mm = pe.matmul(out, v_last[par][0:1, b, cols], probs_t[0:1, b, 2 * P:3 * P], start=False, stop=True)
                mm.then_inc(pv_done, 1)

            def output(v):
                pe.wait_ge(heads_hi_ready, v + 1)
                pe.wait_ge(heads_lo_ready, v + 1)
                three_pass(pe, heads[0][:, :, :, :].rearrange("p a b q -> p (a b q)"),
                           [((heads_hi[:, k, :], heads_lo[:, k, :]), (wo[0][:, k, :], wo[1][:, k, :])) for k in range(KT)])\
                    .then_inc(wo_done, 1)

            for m in range(8):
                project(0, m, 0)
            pe.wait_ge(turned_zeroed, 1)

            def phase(p, par, projects, splits, u):
                for slot in range(8):
                    if slot == 0:
                        score(p, 0, par)
                    if 2 <= slot <= 5:
                        attend(p, slot - 2, par, u + 1)
                    if 1 <= slot <= 4:
                        turn(p, slot - 1)
                    if 1 <= slot <= 3:
                        score(p, slot, par)
                    if projects:
                        project(p + 1, slot, 1 - par)
                if par:
                    output(u)

            phases(pe, phase)

        @block.vector
        def _(dve):
            def key_sum(r, t, par):
                dve.wait_ge(k_sin, 4 * r + t + 1)
                dve.tensor_tensor(keys[par][:, t, :, 0:TKM], cos_part[t % 2][:, :].rearrange("p (b k) -> p b k", k=TKM),
                                  sin_part[t % 2][:, :].rearrange("p (b k) -> p b k", k=TKM), ALU.add).then_inc(k_ready, 1)

            def key_tile(r, t, par):
                if not isinstance(r, int) or r > 0 or t >= 2:
                    dve.wait_ge(k_ready, 4 * r + t - 1)
                dve.wait_ge(proj_done, 8 * r + t + 5)
                dve.tensor_tensor(cos_part[t % 2][:, :].rearrange("p (b k) -> p b k", k=TKM),
                                  proj[t % 2][:, :].rearrange("p (b k) -> p b k", k=TKM),
                                  cos_k[:, 0:TKM].unsqueeze(1).broadcast_to([P, 2, TKM]), ALU.mult)
                dve.stream_shuffle(sin_part[t % 2][:, :], proj[t % 2][:, :], SHUFFLE_HALVES).then_inc(k_read, 1)
                if t == 0:
                    dve.tensor_copy(keys[par][:, :, :, TKM], key_last[:, :, bass.ds(r * 2, 2)])
                else:
                    key_sum(r, t - 1, par)

            def diagonal(par, count):
                dve.wait_ge(q_loaded[par], 16 * count)
                for a in range(4):
                    rows = slice(a * X_HEAD, (a + 1) * X_HEAD)
                    ins = dve.tensor_copy(q_diag[par][rows, :, :, rows],
                                          q_pair[par][rows, :, :].rearrange("p t (b q) -> p t b q", q=TQ))
                ins.then_inc(q_diag_ready, 1)

            dve.wait_ge(zeroed, 1)
            diagonal(0, 1)
            for b in range(2):
                ins = dve.memset(turned[:, b, :], 0.0)
            ins.then_inc(turned_zeroed, 1)
            for t in range(KT):
                key_tile(0, t, 0)
            key_sum(0, 3, 0)

            def phase(p, par, projects, splits, u):
                for n in range(4):
                    q = 4 * p + n
                    dve.wait_ge(s_done, q + 1)
                    dve.tensor_reduce(row_max[:, :], scores[:, :, 0:TK], AX.X, ALU.max).then_inc(max_ready, 1)
                    dve.wait_ge(max_ready, q + 1)
                    dve.tensor_scalar(neg_max[:, :], row_max[:, :], -X_SCALE, None, ALU.mult).then_inc(neg_max_ready, 1)
                    dve.wait_ge(exp_done, q + 1)
                    dve.reciprocal(row_inv[:, :], row_sum[:, :]).then_inc(inv_ready, 1)
                    dve.wait_ge(inv_ready, q + 1)
                    for b in range(2):
                        ins = dve.tensor_scalar(probs[:, b, :], probs[:, b, :], row_inv[:, b:b + 1], None, ALU.mult)
                    ins.then_inc(p_ready, 1)
                if projects:
                    diagonal(1 - par, u + 1 + par)
                    for t in range(KT):
                        key_tile(p + 1, t, 1 - par)
                    key_sum(p + 1, 3, 1 - par)
                if par:
                    dve.wait_ge(heads_hi_ready, u + 1)
                    dve.tensor_tensor(heads_lo[:, :, :], heads_t[:, :, :], f32(heads_hi[:, :, :]), ALU.subtract)\
                        .then_inc(heads_lo_ready, 1)
                    dve.wait_ge(wo_done, u + 1)
                    row = x[:, bass.ds(u, 1), :].rearrange("p a d -> p (a d)")
                    dve.tensor_tensor(row, heads[0][:, :, :, :].rearrange("p a b q -> p (a b q)"), row, ALU.add)\
                        .then_inc(x_added, 1)

            phases(dve, phase)


def block_c(nc, sb, pb, sem, io, x, ident, xt_hi, xt_lo):
    w_qk_raw, w_v_raw, w_o_raw = sb("w_qk_raw", [P, KT, 4 * DH]), sb("w_v_raw", [P, KT, 2 * DH]), sb("w_o_raw", [P, 2, D])
    w_qk = (sb("w_qk_hi", [P, KT, 4 * DH], F32R), sb("w_qk_lo", [P, KT, 4 * DH], F32R))
    w_v = (sb("w_v_hi", [P, KT, 2 * DH], F32R), sb("w_v_lo", [P, KT, 2 * DH], F32R))
    w_o = (sb("w_o_hi", [P, 2, D], F32R), sb("w_o_lo", [P, 2, D], F32R))
    rms_scale = sb("rms_scale", [P, 2])
    out_scale = sb("out_scale", [P, 2])
    mask_rows = sb("mask_rows", [4, P], BF16)
    mask_cols = sb("mask_cols", [4, D], BF16)
    neg_half = sb("neg_half", [P, GT])
    lam = sb("lam", [P, 2, HEADS])
    neg_lam = sb("neg_lam", [P, HEADS])
    neg_lam_now = sb("neg_lam_now", [P, 1])

    const_c = sem("const_c")
    lam_step = sem("lam_step")
    lam_exp = sem("lam_exp")

    with ExitStack() as part:
        def psb(name, shape, dt=F32):
            return part.enter_context(nc.sbuf_tensor(name, shape, dt))

        def ppb(name, shape, dt=F32):
            return part.enter_context(nc.psum_tensor(name, shape, dt))

        norm = Norm("n2", psb, ppb, sem, x, ident)
        lam_in = [psb(f"lam_in{i}", [P, HEADS, DH]) for i in range(2)]
        lam_prod = [psb(f"lam_prod{i}", [P, HEADS, DH]) for i in range(2)]
        lam_k = [psb(f"lam_k{i}", [P, HEADS, DH]) for i in range(2)]
        with nc.Block() as block:
            @block.sync
            def _(sp):
                for i, (a, b) in enumerate((("lq1", "lk1"), ("lq2", "lk2"))):
                    sp.dma_start(lam_in[i][:, :, :], io[a].partition_broadcast(P)).then_inc(const_c, 16)
                    sp.dma_start(lam_k[i][:, :, :], io[b].partition_broadcast(P)).then_inc(const_c, 16)
                sp.dma_start(rms_scale[:, :], io["rms"]).then_inc(const_c, 16)
                sp.dma_start(mask_rows[:, :], io["mask_rows"]).then_inc(const_c, 16)
                sp.dma_start(mask_cols[:, :], io["mask_cols"]).then_inc(const_c, 16)

            @block.scalar
            def _(act):
                act.wait_ge(norm.eps_set, 1)
                with act.Fori(0, GROUPS) as g:
                    norm.scalar_sd(act, g)
                    norm.scalar_hi(act, g, lambda s: xt_hi[:, :, bass.ds(g * GROUP + s * P, P)])
                act.wait_ge(lam_step, 2)
                act.activation(lam[:, :, :], lam[:, :, :], ACT.Exp).then_inc(lam_exp, 1)

            @block.tensor
            def _(pe):
                with pe.Fori(0, GROUPS) as g:
                    norm.tensor_turn(pe, g)

            @block.vector
            def _(dve):
                norm.start(dve)
                dve.memset(neg_half[:, :], -0.5)
                with dve.Fori(0, GROUPS) as g:
                    norm.vector_stats(dve, g)
                    norm.vector_lo(dve, g, lambda s: xt_hi[:, :, bass.ds(g * GROUP + s * P, P)],
                                   lambda s: xt_lo[:, :, bass.ds(g * GROUP + s * P, P)])
                dve.wait_ge(const_c, 16 * 7)
                for i in range(2):
                    ins = dve.tensor_tensor(lam_prod[i][:, :, :], lam_in[i][:, :, :], lam_k[i][:, :, :], ALU.mult)
                ins.then_inc(lam_step, 1)
                dve.wait_ge(lam_step, 1)
                dve.tensor_scalar(out_scale[:, :], rms_scale[:, :], 1.0 - LAMBDA_INIT, None, ALU.mult)
                for i in range(2):
                    ins = dve.tensor_reduce(lam[:, i, :], lam_prod[i][:, :, :], AX.X, ALU.add)
                ins.then_inc(lam_step, 1)
                dve.wait_ge(lam_exp, 1)
                dve.scalar_tensor_tensor(neg_lam[:, :], lam[:, 1, :], -LAMBDA_INIT, lam[:, 0, :], ALU.add, ALU.subtract)\
                    .then_inc(lam_step, 1)

    qk = sb("qk", [P, 4, GROUP])
    v = sb("v_c", [P, GT, 2 * DH])
    row_max = sb("c_row_max", [P, 2, GT])
    neg_max = sb("c_neg_max", [P, 2, GT])
    row_sum = sb("c_row_sum", [P, 2, GT])
    coef = sb("c_coef", [P, 2, GT])
    probs = sb("c_probs", [P, 2, GT, P])
    probs_t = sb("c_probs_t", [P, GT, P])
    sum_sq = sb("c_sum_sq", [P, GT])
    mean_sq = sb("c_mean_sq", [P, GT])
    rms_inv = sb("c_rms_inv", [P, GT])
    normed = sb("c_normed", [P, GT, 2 * DH])
    out_t = (sb("out_t_hi", [P, 2, GROUP], F32R), sb("out_t_lo", [P, 2, GROUP], F32R))
    proj = [pb(f"proj_c{i}", [P, D]) for i in range(2)]
    scores = pb("scores_c", [P, 2, GT, P])
    turned = [pb(f"turned_c{i}", [P, GT, P]) for i in range(2)]
    heads = pb("heads_c", [P, GT, 2 * DH])

    raw_loaded = {n: sem(f"c_{n}_loaded") for n in ("qk", "v", "o")}
    w_hi = {n: sem(f"c_{n}_hi") for n in ("qk", "v", "o")}
    w_lo = {n: sem(f"c_{n}_lo") for n in ("qk", "v", "o")}
    proj_done = sem("c_proj_done")
    proj_read = sem("c_proj_read")
    s_done = sem("c_s_done")
    max_ready = sem("c_max_ready")
    neg_max_ready = sem("c_neg_max_ready")
    exp_done = sem("c_exp_done")
    coef_step = sem("c_coef_step")
    p_ready = sem("c_p_ready")
    t_done = sem("c_t_done")
    pt_ready = sem("c_pt_ready")
    pv_done = sem("c_pv_done")
    sq_done = sem("c_sq_done")
    mean_sq_ready = sem("c_mean_sq_ready")
    rms_ready = sem("c_rms_ready")
    normed_ready = sem("c_normed_ready")
    turn_done = sem("c_turn_done")
    out_hi_ready = sem("c_out_hi")
    out_lo_ready = sem("c_out_lo")
    wo_done = sem("c_wo_done")
    x_added = sem("c_x_added")
    ADD_CREDIT = 8
    QK_TILE = [(0, 0), (1, 1), (2, 2), (3, 3)]

    def stages(eng, stage):
        stage(0, 0, first=True)
        with eng.Fori(0, HEADS - 1) as h:
            for g in range(1, GROUPS):
                stage(h, g)
            stage(h + 1, 0)
        for g in range(1, GROUPS):
            stage(HEADS - 1, g, final=True)

    with nc.Block() as block:
        @block.sync
        def _(sp):
            def load(name, raw, h):
                sp.dma_start(raw[:, :, :], io["w_" + name][bass.ds(h, 1), :, :, :].rearrange("h p k n -> (h p) k n"))\
                    .then_inc(raw_loaded[name], 16)

            load("qk", w_qk_raw, 0)
            load("v", w_v_raw, 0)
            load("o", w_o_raw, 0)
            with sp.Fori(0, HEADS - 1) as h:
                sp.wait_ge(w_lo["qk"], h + 1)
                sp.wait_ge(w_hi["qk"], h + 1)
                load("qk", w_qk_raw, h + 1)
                sp.wait_ge(w_lo["v"], h + 1)
                load("v", w_v_raw, h + 1)
                sp.wait_ge(w_lo["o"], h + 1)
                load("o", w_o_raw, h + 1)

        @block.gpsimd
        def _(gp):
            def split_lo(name, raw, w, h):
                gp.wait_ge(w_hi[name], h + 1)
                gp.tensor_tensor(w[1][:, :, :], raw[:, :, :], f32(w[0][:, :, :]), ALU.subtract).then_inc(w_lo[name], 1)

            def rms(n):
                gp.wait_ge(mean_sq_ready, n + 1)
                gp.tensor_tensor(rms_inv[:, :], mean_sq[:, :], neg_half[:, :], ALU.pow).then_inc(rms_ready, 1)

            def stage(h, g, first=False, final=False):
                n = h * GROUPS + g
                if not first:
                    rms(n - 1)
                if g == GROUPS - 1 and not final:
                    split_lo("qk", w_qk_raw, w_qk, h + 1)
                    split_lo("v", w_v_raw, w_v, h + 1)

            split_lo("qk", w_qk_raw, w_qk, 0)
            split_lo("v", w_v_raw, w_v, 0)
            stages(gp, stage)
            rms(HEADS * GROUPS - 1)

        @block.scalar
        def _(act):
            def split_hi(name, raw, w, h):
                act.wait_ge(raw_loaded[name], 16 * h + 16)
                act.activation(w[0][:, :, :], raw[:, :, :], ACT.Copy).then_inc(w_hi[name], 1)

            def split_o(h):
                act.wait_ge(raw_loaded["o"], 16 * h + 16)
                for f in range(2):
                    ins = act.activation(w_o[0][:, f, :], w_o_raw[:, f, :], ACT.Copy, scale=out_scale[:, f:f + 1])
                ins.then_inc(w_hi["o"], 1)

            def proj_out(n, m):
                act.wait_ge(proj_done, 6 * n + m + 1)
                if m < 4:
                    dst = qk[:, m, :]
                else:
                    dst = v[:, 2 * (m - 4):2 * (m - 4) + 2, :].rearrange("p a d -> p (a d)")
                act.activation(dst, proj[m % 2][:, :], ACT.Copy).then_inc(proj_read, 1)

            def probs_out(n):
                act.wait_ge(t_done, n + 1)
                act.activation(probs_t[:, :, :], turned[0][:, :, :], ACT.Copy).then_inc(pt_ready, 1)

            def squares(n):
                act.wait_ge(pv_done, n + 1)
                for s in range(GT):
                    ins = act.activation(normed[:, s, :], heads[:, s, :], ACT.Square, accum_out=sum_sq[:, s:s + 1])
                ins.then_inc(sq_done, 1)

            def out_hi(n):
                act.wait_ge(turn_done, n + 1)
                for f in range(2):
                    ins = act.activation(out_t[0][:, f, :], turned[f][:, :, :].rearrange("p a q -> p (a q)"), ACT.Copy)
                ins.then_inc(out_hi_ready, 1)

            def exps(n, half):
                if half == 0:
                    act.wait_ge(neg_max_ready, n + 1)
                for s in range(GT):
                    ins = act.activation(probs[:, half, s, :], scores[:, half, s, :], ACT.Exp, bias=neg_max[:, half, s:s + 1],
                                         scale=D_SCALE, accum_out=row_sum[:, half, s:s + 1])
                if half == 1:
                    ins.then_inc(exp_done, 1)

            def stage(h, g, first=False, final=False):
                n = h * GROUPS + g
                proj_out(n, 0)
                proj_out(n, 1)
                if g == 1:
                    split_o(h)
                if not first:
                    probs_out(n - 1)
                proj_out(n, 2)
                if not first:
                    squares(n - 1)
                proj_out(n, 3)
                if not first:
                    out_hi(n - 1)
                if g == GROUPS - 1 and not final:
                    split_hi("qk", w_qk_raw, w_qk, h + 1)
                proj_out(n, 4)
                exps(n, 0)
                proj_out(n, 5)
                exps(n, 1)
                if g == GROUPS - 1 and not final:
                    split_hi("v", w_v_raw, w_v, h + 1)

            split_hi("qk", w_qk_raw, w_qk, 0)
            split_hi("v", w_v_raw, w_v, 0)
            stages(act, stage)
            last = HEADS * GROUPS - 1
            probs_out(last)
            squares(last)
            out_hi(last)

        @block.tensor
        def _(pe):
            def project(n, h, g, m, first):
                if m < 2:
                    if not first:
                        pe.wait_ge(proj_read, 6 * n - 1 + m)
                        pe.wait_ge(x_added, 4 * n - 5 + m + ADD_CREDIT)
                else:
                    pe.wait_ge(proj_read, 6 * n + m - 1)
                rows = slice(g * GROUP, (g + 1) * GROUP)
                if m < 4:
                    if m == 0 and g == 0:
                        pe.wait_ge(w_lo["qk"], h + 1)
                    cols = slice(m * P, (m + 1) * P)
                    three_pass(pe, proj[m % 2][:, :], [((w_qk[0][:, k, cols], w_qk[1][:, k, cols]),
                                                        (xt_hi[:, k, rows], xt_lo[:, k, rows])) for k in range(KT)])\
                        .then_inc(proj_done, 1)
                else:
                    if m == 4 and g == 0:
                        pe.wait_ge(w_lo["v"], h + 1)
                    for s in (2 * (m - 4), 2 * (m - 4) + 1):
                        rows = slice((g * GT + s) * P, (g * GT + s + 1) * P)
                        mm = three_pass(pe, proj[m % 2][:, (s % 2) * 2 * DH:(s % 2 + 1) * 2 * DH],
                                        [((xt_hi[:, k, rows], xt_lo[:, k, rows]), (w_v[0][:, k, :], w_v[1][:, k, :]))
                                         for k in range(KT)])
                    mm.then_inc(proj_done, 1)

            def score(n):
                pe.wait_ge(proj_read, 6 * n + 4)
                for half in range(2):
                    pe.matmul(scores[:, half, :, :].rearrange("p a q -> p (a q)"), mask_rows[:, :], mask_cols[:, :],
                              start=True, stop=False, skip_group_check=True)
                    for s in range(GT):
                        cols = slice(s * P, (s + 1) * P)
                        mm = pe.matmul(scores[:, half, s, :], qk[:, half, cols], qk[:, 2 + half, cols],
                                       start=False, stop=(s == GT - 1), skip_group_check=True)
                mm.then_inc(s_done, 1)

            def turn(n):
                pe.wait_ge(p_ready, n + 1)
                for s in range(GT):
                    mm = pe.transpose(turned[0][:, s, :], probs[:, 0, s, :], ident[:, :])
                mm.then_inc(t_done, 1)

            def attend(n):
                pe.wait_ge(pt_ready, n + 1)
                pe.wait_ge(proj_read, 6 * n + 6)
                for s in range(GT):
                    mm = pe.matmul(heads[:, s, :], probs_t[:, s, :], v[:, s, :], start=True, stop=True)
                mm.then_inc(pv_done, 1)

            def turn_out(n):
                pe.wait_ge(normed_ready, n + 1)
                for f in range(2):
                    for s in range(GT):
                        mm = pe.transpose(turned[f][:, s, :], normed[:, s, f * P:(f + 1) * P], ident[:, :])
                mm.then_inc(turn_done, 1)

            def output(n, h, final_wait=True):
                pe.wait_ge(w_lo["o"], h + 1)
                pe.wait_ge(out_lo_ready, n + 1)
                for s in range(GT):
                    if s >= 2:
                        pe.wait_ge(x_added, 4 * n + s - 1 + ADD_CREDIT)
                    cols = slice(s * P, (s + 1) * P)
                    three_pass(pe, proj[s % 2][:, :], [((out_t[0][:, f, cols], out_t[1][:, f, cols]),
                                                        (w_o[0][:, f, :], w_o[1][:, f, :])) for f in range(2)])\
                        .then_inc(wo_done, 1)

            def stage(h, g, first=False, final=False):
                n = h * GROUPS + g
                prev = n - 1
                prev_head = h if g else h - 1
                project(n, h, g, 0, first)
                project(n, h, g, 1, first)
                if not first:
                    turn(prev)
                project(n, h, g, 2, first)
                if not first:
                    attend(prev)
                project(n, h, g, 3, first)
                score(n)
                if not first:
                    turn_out(prev)
                project(n, h, g, 4, first)
                project(n, h, g, 5, first)
                if not first:
                    pe.wait_ge(proj_read, 6 * n + 6)
                    output(prev, prev_head)

            stages(pe, stage)
            last = HEADS * GROUPS - 1
            turn(last)
            attend(last)
            turn_out(last)
            output(last, HEADS - 1)

        @block.vector
        def _(dve):
            dve.sem_inc(x_added, ADD_CREDIT)

            def split_o(h):
                dve.wait_ge(w_hi["o"], h + 1)
                for f in range(2):
                    ins = dve.scalar_tensor_tensor(w_o[1][:, f, :], w_o_raw[:, f, :], out_scale[:, f:f + 1],
                                                   f32(w_o[0][:, f, :]), ALU.mult, ALU.subtract)
                ins.then_inc(w_lo["o"], 1)

            def mean_squares(n):
                dve.wait_ge(sq_done, n + 1)
                dve.tensor_scalar(mean_sq[:, :], sum_sq[:, :], 1.0 / (2 * DH), EPS, ALU.mult, ALU.add).then_inc(mean_sq_ready, 1)

            def normalise(n):
                dve.wait_ge(rms_ready, n + 1)
                for s in range(GT):
                    ins = dve.tensor_scalar(normed[:, s, :], heads[:, s, :], rms_inv[:, s:s + 1], None, ALU.mult)
                ins.then_inc(normed_ready, 1)

            def maxima(n):
                dve.wait_ge(s_done, n + 1)
                dve.tensor_reduce(row_max[:, :, :], scores[:, :, :, :], AX.X, ALU.max).then_inc(max_ready, 1)
                dve.wait_ge(max_ready, n + 1)
                dve.tensor_scalar(neg_max[:, :, :], row_max[:, :, :], -D_SCALE, None, ALU.mult).then_inc(neg_max_ready, 1)

            def out_lo(n):
                dve.wait_ge(out_hi_ready, n + 1)
                for f in range(2):
                    ins = dve.tensor_tensor(out_t[1][:, f, :], turned[f][:, :, :].rearrange("p a q -> p (a q)"),
                                            f32(out_t[0][:, f, :]), ALU.subtract)
                ins.then_inc(out_lo_ready, 1)

            def combine(n):
                dve.wait_ge(exp_done, n + 1)
                dve.reciprocal(coef[:, :, :], row_sum[:, :, :]).then_inc(coef_step, 1)
                dve.wait_ge(coef_step, 3 * n + 1)
                dve.tensor_scalar(coef[:, 1, :], coef[:, 1, :], neg_lam_now[:, :], None, ALU.mult).then_inc(coef_step, 1)
                dve.wait_ge(coef_step, 3 * n + 2)
                for s in range(GT):
                    ins = dve.tensor_scalar(probs[:, 1, s, :], probs[:, 1, s, :], coef[:, 1, s:s + 1], None, ALU.mult)
                ins.then_inc(coef_step, 1)
                dve.wait_ge(coef_step, 3 * n + 3)
                for s in range(GT):
                    ins = dve.scalar_tensor_tensor(probs[:, 0, s, :], probs[:, 0, s, :], coef[:, 0, s:s + 1],
                                                   probs[:, 1, s, :], ALU.mult, ALU.add)
                ins.then_inc(p_ready, 1)

            def add(n, g):
                for s in range(GT):
                    dve.wait_ge(wo_done, 4 * n + s + 1)
                    dve.tensor_tensor(x[:, g * GT + s, :], proj[s % 2][:, :], x[:, g * GT + s, :], ALU.add).then_inc(x_added, 1)

            def stage(h, g, first=False, final=False):
                n = h * GROUPS + g
                if g == 1:
                    split_o(h)
                if not first:
                    mean_squares(n - 1)
                    normalise(n - 1)
                maxima(n)
                if not first:
                    out_lo(n - 1)
                if g == 0:
                    dve.tensor_copy(neg_lam_now[:, :], neg_lam[:, bass.ds(h, 1)])
                combine(n)
                if not first:
                    add(n - 1, (g - 1) % GROUPS)

            stages(dve, stage)
            last = HEADS * GROUPS - 1
            mean_squares(last)
            normalise(last)
            out_lo(last)
            add(last, GROUPS - 1)


def block_d(nc, sb, pb, sem, io, x, ident, xt_hi, xt_lo):
    masks = sb("masks", [P, EXPERTS, TOKENS], BF16)
    b1_all = sb("b1_all", [P, CHUNKS, HT])
    norm_loaded = sem("d_loaded")
    gate_wide = sem("gate_wide")
    gate_hi_ready = sem("gate_hi_ready")
    gate_lo_ready = sem("gate_lo_ready")
    gate_done = sem("gate_done")
    gate_read = sem("gate_read")
    gate_step = sem("gate_step")
    gate_shift = sem("gate_shift")
    gate_exp = sem("gate_exp")
    mask_ready = sem("mask_ready")
    bias_step = sem("bias_step")
    bias_sum_ready = sem("bias_sum_ready")
    xn_used = sem("xn_used")

    with ExitStack() as part:
        def psb(name, shape, dt=F32):
            return part.enter_context(nc.sbuf_tensor(name, shape, dt))

        def ppb(name, shape, dt=F32):
            return part.enter_context(nc.psum_tensor(name, shape, dt))

        norm = Norm("n3", psb, ppb, sem, x, ident)
        gate_raw = psb("gate_raw", [P, KT, 2])
        gate_w = psb("gate_w", [P, KT, 2, P])
        gate_hi, gate_lo = psb("gate_hi", [P, KT, 2, P], F32R), psb("gate_lo", [P, KT, 2, P], F32R)
        first_score = psb("first_score", [P, GROUP])
        top = psb("top", [P, GROUP])
        shifted = psb("shifted", [P, 2, GROUP])
        bias2 = psb("bias2", [P, EXPERTS, D])
        gate_ps = ppb("gate_ps", [P, 2, GROUP])
        with nc.Block() as block:
            @block.sync
            def _(sp):
                sp.dma_start(gate_raw[:, :, :], io["gate"]).then_inc(norm_loaded, 16)
                sp.dma_start(bias2[:, :, :], io["b2"].partition_broadcast(P)).then_inc(norm_loaded, 16)
                sp.dma_start(b1_all[:, :, :], io["b1"]).then_inc(norm_loaded, 16)

            @block.gpsimd
            def _(gp):
                gp.wait_ge(norm_loaded, 48)
                gp.tensor_copy(gate_w[:, :, :, :], gate_raw[:, :, :].unsqueeze(3).broadcast_to([P, KT, 2, P])).then_inc(gate_wide, 1)
                gp.wait_ge(gate_hi_ready, 1)
                gp.tensor_tensor(gate_lo[:, :, :, :], gate_w[:, :, :, :], f32(gate_hi[:, :, :, :]), ALU.subtract)\
                    .then_inc(gate_lo_ready, 1)
                gp.tensor_tensor(bias2[:, 0, :], bias2[:, 0, :], bias2[:, 1, :], ALU.add).then_inc(bias_step, 1)
                gp.wait_ge(bias_step, 1)
                gp.tensor_tensor(bias2[:, 0, :], bias2[:, 0, :], bias2[:, 2, :], ALU.add).then_inc(bias_step, 1)
                gp.wait_ge(bias_step, 2)
                with gp.Fori(0, GROUPS) as g:
                    gp.wait_ge(norm.xn_ready, g + 1)
                    rows = x[:, bass.ds(g * GT, GT), :]
                    gp.tensor_tensor(rows, rows, bias2[:, 0, :].unsqueeze(1).broadcast_to([P, GT, D]), ALU.add).then_inc(xn_used, 1)

            @block.scalar
            def _(act):
                act.wait_ge(gate_wide, 1)
                act.activation(gate_hi[:, :, :, :], gate_w[:, :, :, :], ACT.Copy).then_inc(gate_hi_ready, 1)
                act.wait_ge(norm.eps_set, 1)
                with act.Fori(0, GROUPS) as g:
                    norm.scalar_sd(act, g)
                    norm.scalar_hi(act, g, lambda s: xt_hi[:, :, bass.ds(g * GROUP + s * P, P)])
                    act.wait_ge(gate_done, g + 1)
                    act.activation(first_score[:, :], gate_ps[:, 0, :], ACT.Copy).then_inc(gate_read, 1)
                    act.wait_ge(gate_shift, g + 1)
                    act.activation(shifted[:, :, :], shifted[:, :, :], ACT.Exp).then_inc(gate_exp, 1)

            @block.tensor
            def _(pe):
                pe.wait_ge(gate_lo_ready, 1)
                with pe.Fori(0, GROUPS) as g:
                    norm.tensor_turn(pe, g)
                    pe.wait_ge(norm.lo_ready, g * GT + GT)
                    for e in range(2):
                        mm = three_pass(pe, gate_ps[:, e, :], [((gate_hi[:, k, e, :], gate_lo[:, k, e, :]),
                                                                (xt_hi[:, k, bass.ds(g * GROUP, GROUP)],
                                                                 xt_lo[:, k, bass.ds(g * GROUP, GROUP)])) for k in range(KT)])
                    mm.then_inc(gate_done, 1)

            @block.vector
            def _(dve):
                norm.start(dve)
                dve.memset(masks[:, 2, :], 1.0)
                with dve.Fori(0, GROUPS) as g:
                    norm.vector_stats(dve, g)
                    norm.vector_lo(dve, g, lambda s: xt_hi[:, :, bass.ds(g * GROUP + s * P, P)],
                                   lambda s: xt_lo[:, :, bass.ds(g * GROUP + s * P, P)])
                    dve.wait_ge(gate_read, g + 1)
                    dve.tensor_tensor(top[:, :], gate_ps[:, 1, :], first_score[:, :], ALU.max).then_inc(gate_step, 1)
                    dve.wait_ge(gate_step, g * 2 + 1)
                    dve.tensor_tensor(shifted[:, 0, :], first_score[:, :], top[:, :], ALU.subtract)
                    dve.tensor_tensor(shifted[:, 1, :], gate_ps[:, 1, :], top[:, :], ALU.subtract).then_inc(gate_shift, 1)
                    dve.wait_ge(gate_exp, g + 1)
                    cols = bass.ds(g * GROUP, GROUP)
                    dve.tensor_tensor(masks[:, 1, cols], shifted[:, 1, :], shifted[:, 0, :], ALU.is_gt).then_inc(gate_step, 1)
                    dve.wait_ge(gate_step, g * 2 + 2)
                    dve.tensor_scalar(masks[:, 0, cols], masks[:, 1, cols], -1.0, 1.0, ALU.mult, ALU.add).then_inc(mask_ready, 1)

    w1_raw, w2_raw = sb("w1_raw", [P, KT, HC]), sb("w2_raw", [P, HT, D])
    w1 = (sb("w1_hi", [P, KT, HC], F32R), sb("w1_lo", [P, KT, HC], F32R))
    w2 = (sb("w2_hi", [P, HT, D], F32R), sb("w2_lo", [P, HT, D], F32R))
    hidden = [(sb(f"hidden_hi{i}", [P, HT, GROUP], F32R), sb(f"hidden_lo{i}", [P, HT, GROUP], F32R)) for i in range(2)]
    masked = [sb(f"masked{i}", [P, GROUP]) for i in range(2)]
    relu = [sb(f"relu{i}", [P, GROUP]) for i in range(2)]
    mask_now = sb("mask_now", [P, TOKENS], BF16)
    b1_now = sb("b1_now", [P, HT])
    hid_ps = [pb(f"hid_ps{i}", [P, GROUP]) for i in range(2)]
    out_ps = [pb(f"out_ps{i}", [P, D]) for i in range(2)]

    w1_loaded = sem("w1_loaded")
    w2_loaded = sem("w2_loaded")
    w1_hi = sem("w1_hi_s")
    w1_lo = sem("w1_lo_s")
    w2_hi = sem("w2_hi_s")
    w2_lo = sem("w2_lo_s")
    now_ready = sem("now_ready")
    h_done = sem("h_done")
    h_read = sem("h_read")
    h_hi = sem("h_hi")
    h_relu = sem("h_relu")
    h_lo = sem("h_lo")
    o_done = sem("o_done")
    o_added = sem("o_added")
    O_CREDIT = 2
    stored = sem("stored")

    def stages(eng, stage):
        stage(0, 0, first=True)
        with eng.Fori(0, CHUNKS - 1) as c:
            for g in range(1, GROUPS):
                stage(c, g)
            stage(c + 1, 0)
        for g in range(1, GROUPS):
            stage(CHUNKS - 1, g, final=True)

    with nc.Block() as block:
        @block.sync
        def _(sp):
            def load(raw, src, c, loaded):
                sp.dma_start(raw[:, :, :], src[bass.ds(c, 1), :, :, :].rearrange("c p k n -> (c p) k n")).then_inc(loaded, 16)

            load(w1_raw, io["w1"], 0, w1_loaded)
            load(w2_raw, io["w2"], 0, w2_loaded)
            with sp.Fori(0, CHUNKS - 1) as c:
                sp.wait_ge(w1_lo, c + 1)
                load(w1_raw, io["w1"], c + 1, w1_loaded)
                sp.wait_ge(w2_lo, c + 1)
                load(w2_raw, io["w2"], c + 1, w2_loaded)
            out_v = io["out"].rearrange("(t p) d -> p t d", p=P)
            for g in range(GROUPS):
                sp.wait_ge(o_added, 4 * (GROUPS * (CHUNKS - 1) + g + 1) + O_CREDIT)
                sp.dma_start(out_v[:, g * GT:(g + 1) * GT, :], x[:, g * GT:(g + 1) * GT, :]).then_inc(stored, 16)
            sp.wait_ge(stored, 16 * GROUPS)

        @block.gpsimd
        def _(gp):
            def split(c, raw, w, hi_sem, lo_sem):
                gp.wait_ge(hi_sem, c + 1)
                gp.tensor_tensor(w[1][:, :, :], raw[:, :, :], f32(w[0][:, :, :]), ALU.subtract).then_inc(lo_sem, 1)

            def stage(c, g, first=False, final=False):
                n = c * GROUPS + g
                if g == 1:
                    split(c, w2_raw, w2, w2_hi, w2_lo)
                for m in range(HT):
                    gp.wait_ge(h_hi, HT * n + m + 1)
                    gp.wait_ge(h_relu, HT * n + m + 1)
                    gp.tensor_tensor(hidden[g % 2][1][:, m, :], relu[m % 2][:, :], f32(hidden[g % 2][0][:, m, :]),
                                     ALU.subtract).then_inc(h_lo, 1)
                if g == GROUPS - 1 and not final:
                    split(c + 1, w1_raw, w1, w1_hi, w1_lo)

            split(0, w1_raw, w1, w1_hi, w1_lo)
            stages(gp, stage)

        @block.scalar
        def _(act):
            def split(c, raw, w, loaded, hi_sem):
                act.wait_ge(loaded, 16 * c + 16)
                act.activation(w[0][:, :, :], raw[:, :, :], ACT.Copy).then_inc(hi_sem, 1)

            def stage(c, g, first=False, final=False):
                n = c * GROUPS + g
                if g == 1:
                    act.wait_ge(h_done, HT * n + 1)
                    split(c, w2_raw, w2, w2_loaded, w2_hi)
                for m in range(HT):
                    act.wait_ge(h_read, HT * n + m + 1)
                    act.activation(hidden[g % 2][0][:, m, :], masked[m % 2][:, :], ACT.Relu, bias=b1_now[:, m:m + 1])\
                        .then_inc(h_hi, 1)
                if g == GROUPS - 1 and not final:
                    split(c + 1, w1_raw, w1, w1_loaded, w1_hi)

            split(0, w1_raw, w1, w1_loaded, w1_hi)
            stages(act, stage)

        @block.tensor
        def _(pe):
            def hide(c, n, g, first):
                rows = slice(g * GROUP, (g + 1) * GROUP)
                if g == 0:
                    pe.wait_ge(w1_lo, c + 1)
                for m in range(HT):
                    if not first or m >= 2:
                        pe.wait_ge(h_read, HT * n + m - 1)
                    cols = slice(m * P, (m + 1) * P)
                    three_pass(pe, hid_ps[m % 2][:, :], [((w1[0][:, k, cols], w1[1][:, k, cols]),
                                                          (xt_hi[:, k, rows], xt_lo[:, k, rows])) for k in range(KT)])\
                        .then_inc(h_done, 1)

            def output(c, n, g):
                if g == 0:
                    pe.wait_ge(w2_lo, c + 1)
                pe.wait_ge(h_lo, HT * n + HT)
                hi, lo = hidden[g % 2]
                for s in range(GT):
                    pe.wait_ge(o_added, GT * n + s + 1)
                    cols = slice(s * P, (s + 1) * P)
                    three_pass(pe, out_ps[s % 2][:, :], [((hi[:, m, cols], lo[:, m, cols]), (w2[0][:, m, :], w2[1][:, m, :]))
                                                         for m in range(HT)]).then_inc(o_done, 1)

            def stage(c, g, first=False, final=False):
                n = c * GROUPS + g
                hide(c, n, g, first)
                if not first:
                    output(c if g else c - 1, n - 1, (g - 1) % GROUPS)

            stages(pe, stage)
            output(CHUNKS - 1, CHUNKS * GROUPS - 1, GROUPS - 1)

        @block.vector
        def _(dve):
            dve.sem_inc(o_added, O_CREDIT)

            def add(n, g):
                for s in range(GT):
                    dve.wait_ge(o_done, GT * n + s + 1)
                    dve.tensor_tensor(x[:, g * GT + s, :], out_ps[s % 2][:, :], x[:, g * GT + s, :], ALU.add).then_inc(o_added, 1)

            def stage(c, g, first=False, final=False):
                n = c * GROUPS + g
                if g == 0:
                    if not first:
                        dve.wait_ge(h_hi, HT * n)
                    dve.tensor_copy(b1_now[:, :], b1_all[:, bass.ds(c, 1), :].rearrange("p a n -> p (a n)"))
                    dve.tensor_copy(mask_now[:, :], masks[:, bass.ds(c // CHUNKS_PER_EXPERT, 1), :].rearrange("p a n -> p (a n)"))\
                        .then_inc(now_ready, 1)
                    dve.wait_ge(now_ready, c + 1)
                for m in range(HT):
                    if not first or m >= 2:
                        dve.wait_ge(h_hi, HT * n + m - 1)
                        dve.wait_ge(h_lo, HT * n + m - 1)
                    dve.wait_ge(h_done, HT * n + m + 1)
                    dve.tensor_tensor(masked[m % 2][:, :], hid_ps[m % 2][:, :], mask_now[:, g * GROUP:(g + 1) * GROUP],
                                      ALU.mult).then_inc(h_read, 1)
                    dve.wait_ge(h_read, HT * n + m + 1)
                    dve.tensor_scalar(relu[m % 2][:, :], masked[m % 2][:, :], b1_now[:, m:m + 1], 0.0, ALU.add, ALU.max)\
                        .then_inc(h_relu, 1)
                if not first:
                    add(n - 1, (g - 1) % GROUPS)

            stages(dve, stage)
            add(CHUNKS * GROUPS - 1, GROUPS - 1)


def build(nc, io):
    with ExitStack() as ctx:
        def sem(name):
            return ctx.enter_context(nc.semaphore(name))

        def scope():
            stack = ctx.enter_context(ExitStack())

            def sb(name, shape, dt=F32):
                return stack.enter_context(nc.sbuf_tensor(name, shape, dt))

            def pb(name, shape, dt=F32):
                return stack.enter_context(nc.psum_tensor(name, shape, dt))

            return stack, sb, pb

        _, sb, pb = scope()
        x = sb("x_res", [P, TILES, D])
        ident = sb("ident", [P, P])
        const_loaded = sem("const_loaded")

        cross, csb, cpb = scope()
        cos_k, sin_k = csb("cos_k", [P, TK]), csb("sin_k", [P, TK])
        key_last = csb("key_last", [P, KT, BATCH])
        weights = [(csb(n + "_hi", [P, KT, D], F32R), csb(n + "_lo", [P, KT, D], F32R)) for n in ("wk", "wv", "wo")]
        with nc.Block() as block:
            @block.sync
            def _(sp):
                sp.dma_start(ident[:, :], io["ident"]).then_inc(const_loaded, 16)
                sp.dma_start(cos_k[:, :], io["cos"]).then_inc(const_loaded, 16)
                sp.dma_start(sin_k[:, :], io["sin"]).then_inc(const_loaded, 16)
                sp.wait_ge(const_loaded, 48)
        stack, asb, apb = scope()
        block_a(nc, asb, apb, sem, io, x, ident, cos_k, sin_k, key_last, weights, const_loaded)
        stack.close()
        stack, bsb, bpb = scope()
        block_b(nc, bsb, bpb, sem, io, x, ident, cos_k, sin_k, key_last, weights)
        stack.close()
        cross.close()

        _, sb, pb = scope()
        xt_hi, xt_lo = sb("x_t_hi", [P, KT, TOKENS], F32R), sb("x_t_lo", [P, KT, TOKENS], F32R)
        stack, csb, cpb = scope()
        block_c(nc, csb, cpb, sem, io, x, ident, xt_hi, xt_lo)
        stack.close()
        stack, dsb, dpb = scope()
        block_d(nc, dsb, dpb, sem, io, x, ident, xt_hi, xt_lo)
        stack.close()


def kernel(**inputs):
    import ml_dtypes
    import numpy as np
    import concourse.bacc as bacc
    from concourse.bass_utils import run_bass_kernel_spmd

    a = {n: np.asarray(v) for n, v in inputs.items()}
    half = X_HEAD // 2
    inv_freq = (1.0 / np.float32(10000.0) ** (np.arange(0, X_HEAD, 2, dtype=np.float32) / np.float32(X_HEAD))).astype(np.float32)
    angle = np.outer(np.arange(TK, dtype=np.float32), inv_freq).astype(np.float32).T
    cos, sin = np.cos(angle), np.sin(angle)
    wq, wk, wv = (a[f"L0_attn_{n}"].reshape(HEADS, 2, DH, KT, P) for n in ("Wq", "Wk", "Wv"))
    w_qk = np.concatenate([wq, wk], 1).transpose(0, 4, 3, 1, 2).reshape(HEADS, P, KT, 4 * DH)
    w_v = wv.transpose(0, 4, 3, 1, 2).reshape(HEADS, P, KT, 2 * DH)
    w_o = a["L0_attn_Wo"].reshape(D, HEADS, 2, DH).transpose(1, 3, 2, 0)
    w1 = np.concatenate([a["L0_ffn_w1"], a["L0_ffn_sw1"][None]]).reshape(EXPERTS, KT, P, CHUNKS_PER_EXPERT, HC)
    w2 = np.concatenate([a["L0_ffn_w2"], a["L0_ffn_sw2"][None]]).reshape(CHUNKS, HT, P, D)
    b1 = np.concatenate([a["L0_ffn_b1"], a["L0_ffn_sb1"][None]]).reshape(CHUNKS, HT, P)
    b2 = np.concatenate([a["L0_ffn_b2"], a["L0_ffn_sb2"][None]])
    same = np.arange(4)[:, None] == np.arange(P)[None, :] // TQ
    arrays = {
        "x": a["x"].reshape(TOKENS, D),
        "ctx_main": a["ctx_1024"][:, :TKM].reshape(BATCH * TKM, D).T,
        "ctx_last": a["ctx_1024"][:, TKM].T,
        "Wq": a["L0_xattn_Wq"].T, "Wk": a["L0_xattn_Wk"].T, "Wv": a["L0_xattn_Wv"].T, "Wo": a["L0_xattn_Wo"].T,
        "ident": np.eye(P, dtype=np.float32),
        "cos": np.tile(cos, (P // half, 1)),
        "sin": np.tile(np.concatenate([-sin, sin]), (P // X_HEAD, 1)),
        "lq1": a["L0_attn_lambda_q1"], "lk1": a["L0_attn_lambda_k1"],
        "lq2": a["L0_attn_lambda_q2"], "lk2": a["L0_attn_lambda_k2"],
        "rms": a["L0_attn_rms_scale"].reshape(2, DH).T,
        "mask_rows": same.astype(ml_dtypes.bfloat16),
        "mask_cols": np.tile(np.where(same, 0.0, MASKED), (1, D // P)).astype(ml_dtypes.bfloat16),
        "w_qk": w_qk, "w_v": w_v, "w_o": w_o,
        "gate": a["L0_ffn_gate_w"].reshape(2, KT, P).transpose(2, 1, 0),
        "w1": w1.transpose(0, 3, 2, 1, 4).reshape(CHUNKS, P, KT, HC),
        "w2": w2.transpose(0, 2, 1, 3),
        "b1": b1.transpose(2, 0, 1),
        "b2": b2,
    }
    nc = bacc.Bacc("TRN2", target_bir_lowering=False, num_devices=1)
    feeds, io = {}, {}
    for name, v in arrays.items():
        v = np.ascontiguousarray(v)
        feeds[f"in_{name}_dram"] = v
        io[name] = nc.dram_tensor(f"in_{name}_dram", v.shape, mybir.dt.from_np(v.dtype), kind="ExternalInput").ap()
    io["v_last"] = nc.dram_tensor("v_last_dram", (BATCH, D), F32, kind="Internal").ap()
    io["queries"] = nc.dram_tensor("queries_dram", (P, KT, TOKENS), F32, kind="Internal").ap()
    io["out"] = nc.dram_tensor("out_0_dram", (TOKENS, D), F32, kind="ExternalOutput").ap()
    build(nc, io)
    r = run_bass_kernel_spmd(nc, [feeds], core_ids=[0])
    return np.asarray(r.results[0]["out_0_dram"]).reshape(BATCH, TQ, D)
```

```python
from contextlib import ExitStack
import math

import concourse.bass as bass
from concourse import mybir

ALU = mybir.AluOpType
ACT = mybir.ActivationFunctionType
AX = mybir.AxisListType
F32 = mybir.dt.float32
F32R = mybir.dt.float32r
BF16 = mybir.dt.bfloat16

P = 128
D = 512
KT = D // P
BATCH = 64
TQ = 32
TK = 257
TKM = TK - 1
TOKENS = BATCH * TQ
TILES = TOKENS // P
GROUP = 512
GROUPS = TOKENS // GROUP
GT = GROUP // P
PAIRS = BATCH // 2
X_HEAD = 32
X_SCALE = 1.0 / math.sqrt(X_HEAD)
HEADS = 8
DH = 128
D_SCALE = 1.0 / math.sqrt(DH)
LAMBDA_INIT = 0.8 - 0.6 * math.exp(-0.3 * 1)
EPS = 1e-5
HIDDEN = 2048
EXPERTS = 3
HC = 512
HT = HC // P
CHUNKS = EXPERTS * HIDDEN // HC
CHUNKS_PER_EXPERT = HIDDEN // HC
MASKED = -(2.0 ** 100)
SHUFFLE_HALVES = [(j + X_HEAD // 2) % X_HEAD for j in range(X_HEAD)]
CONSTS = 3
BN = 6


def f32(ap):
    return ap.bitcast(F32)


def three_pass(pe, out, terms, start=True, stop=True):
    passes = [(a, b) for (a_hi, a_lo), (b_hi, b_lo) in terms for a, b in ((a_hi, b_hi), (a_hi, b_lo), (a_lo, b_hi))]
    for n, (a, b) in enumerate(passes):
        mm = pe.matmul(out, a, b, start=start and n == 0, stop=stop and n == len(passes) - 1)
    return mm


class Norm:

    CHAIN = 4

    def __init__(self, name, sb, pb, sem, x, ident):
        self.x, self.ident = x, ident
        self.stats = sb(name + "_stats", [P, GT, BN])
        self.mean_sum = sb(name + "_mean_sum", [P, GT])
        self.mean_gap = sb(name + "_mean_gap", [P, GT])
        self.means = [sb(f"{name}_mean{i}", [P, GT]) for i in range(2)]
        self.gap_sq = sb(name + "_gap_sq", [P, GT])
        self.var_sum = sb(name + "_var_sum", [P, GT])
        self.sd = sb(name + "_sd", [P, GT])
        self.rstds = [sb(f"{name}_rstd{i}", [P, GT]) for i in range(2)]
        self.eps = sb(name + "_eps", [P, 1])
        self.xn = [sb(f"{name}_xn{i}", [P, GT, D]) for i in range(2)]
        self.turned = [pb(f"{name}_turned{i}", [P, KT, P]) for i in range(2)]
        self.chain = sem(name + "_chain")
        self.eps_set = sem(name + "_eps_set")
        self.var_ready = sem(name + "_var_ready")
        self.sd_ready = sem(name + "_sd_ready")
        self.xn_ready = sem(name + "_xn_ready")
        self.turn_done = sem(name + "_turn_done")
        self.hi_ready = sem(name + "_hi_ready")
        self.lo_ready = sem(name + "_lo_ready")

    def start(self, dve):
        dve.memset(self.eps[:, :], EPS).then_inc(self.eps_set, 1)

    def vector_stats(self, dve, g):
        mean, rstd = self.means[g % 2], self.rstds[g % 2]
        for s in range(GT):
            ins = dve.bn_stats(self.stats[:, s, :], self.x[:, g * GT + s, :])
        ins.then_inc(self.chain, 1)
        dve.wait_ge(self.chain, g * self.CHAIN + 1)
        dve.tensor_tensor(self.mean_sum[:, :], self.stats[:, :, 1], self.stats[:, :, 4], ALU.add)
        dve.tensor_tensor(self.mean_gap[:, :], self.stats[:, :, 1], self.stats[:, :, 4], ALU.subtract)
        dve.tensor_tensor(self.var_sum[:, :], self.stats[:, :, 2], self.stats[:, :, 5], ALU.add).then_inc(self.chain, 1)
        dve.wait_ge(self.chain, g * self.CHAIN + 2)
        dve.tensor_scalar(mean[:, :], self.mean_sum[:, :], 0.5, None, ALU.mult)
        dve.tensor_tensor(self.gap_sq[:, :], self.mean_gap[:, :], self.mean_gap[:, :], ALU.mult).then_inc(self.chain, 1)
        dve.wait_ge(self.chain, g * self.CHAIN + 3)
        dve.scalar_tensor_tensor(self.var_sum[:, :], self.gap_sq[:, :], D / 4.0, self.var_sum[:, :], ALU.mult, ALU.add)\
            .then_inc(self.var_ready, 1)
        dve.wait_ge(self.sd_ready, g + 1)
        dve.reciprocal(rstd[:, :], self.sd[:, :]).then_inc(self.chain, 1)
        dve.wait_ge(self.chain, g * self.CHAIN + 4)
        for s in range(GT):
            ins = dve.tensor_scalar(self.xn[g % 2][:, s, :], self.x[:, g * GT + s, :],
                                    mean[:, s:s + 1], rstd[:, s:s + 1], ALU.subtract, ALU.mult)
        ins.then_inc(self.xn_ready, 1)

    def scalar_sd(self, act, g):
        act.wait_ge(self.var_ready, g + 1)
        act.activation(self.sd[:, :], self.var_sum[:, :], ACT.Sqrt, bias=self.eps[:, :], scale=1.0 / D).then_inc(self.sd_ready, 1)

    def tensor_turn(self, pe, g):
        pe.wait_ge(self.xn_ready, g + 1)
        for s in range(GT):
            if g * GT + s >= 2:
                pe.wait_ge(self.lo_ready, g * GT + s - 1)
            for k in range(KT):
                mm = pe.transpose(self.turned[s % 2][:, k, :], self.xn[g % 2][:, s, k * P:(k + 1) * P], self.ident[:, :])
            mm.then_inc(self.turn_done, 1)

    def scalar_hi(self, act, g, hi):
        for s in range(GT):
            act.wait_ge(self.turn_done, g * GT + s + 1)
            act.activation(hi(s), self.turned[s % 2][:, :, :], ACT.Copy).then_inc(self.hi_ready, 1)

    def vector_lo(self, dve, g, hi, lo):
        for s in range(GT):
            dve.wait_ge(self.hi_ready, g * GT + s + 1)
            dve.tensor_tensor(lo(s), self.turned[s % 2][:, :, :], f32(hi(s)), ALU.subtract).then_inc(self.lo_ready, 1)


def block_a(nc, sb, pb, sem, io, x, ident, cos_k, sin_k, key_last, value_last, weights, const_loaded, ctx_raw, ctx_loaded):
    names = ("Wq", "Wk", "Wv", "Wo")
    wq = (sb("wq_hi", [P, KT, D], F32R), sb("wq_lo", [P, KT, D], F32R))
    split = {"Wq": wq, "Wk": weights[0], "Wv": weights[1], "Wo": weights[2]}
    w_raw = [sb(f"w_raw{i}", [P, KT, D]) for i in range(2)]
    norm = Norm("n1", sb, pb, sem, x, ident)
    xt = [(sb(f"xt_hi{i}", [P, KT, GROUP], F32R), sb(f"xt_lo{i}", [P, KT, GROUP], F32R)) for i in range(2)]
    last_raw = sb("last_raw", [P, KT, BATCH])
    last_hi, last_lo = sb("last_hi", [P, KT, BATCH], F32R), sb("last_lo", [P, KT, BATCH], F32R)
    last_sin = sb("last_sin", [P, KT, BATCH])
    cos_part = [sb(f"cos_part{i}", [P, GROUP]) for i in range(2)]
    sin_part = [sb(f"sin_part{i}", [P, GROUP]) for i in range(2)]
    queries = sb("queries", [P, KT, GROUP])
    proj = [pb(f"proj_a{i}", [P, D]) for i in range(2)]
    last_ps = pb("last_ps", [P, 2, KT, BATCH])

    x_loaded = [sem(f"x_loaded{g}") for g in range(GROUPS)]
    w_loaded = [sem(f"w_loaded_{n}") for n in names]
    w_hi = sem("w_hi")
    w_lo = sem("w_lo")
    last_loaded = sem("last_loaded")
    last_hi_ready = sem("last_hi_ready")
    last_lo_ready = sem("last_lo_ready")
    q_done = sem("q_done")
    q_halves = sem("q_halves")
    q_sin = sem("q_sin")
    q_ready = sem("q_ready")
    last_done = sem("last_done")
    last_step = sem("last_step")
    last_ready = sem("last_ready")
    q_stored = [sem(f"q_stored{t}") for t in range(KT)]

    with nc.Block() as block:
        @block.sync
        def _(sp):
            x_v = io["x"].rearrange("(t p) d -> p t d", p=P)
            ctx_v = io["ctx_main"].rearrange("(k p) n -> p k n", p=P)

            def load_w(n):
                sp.dma_start(w_raw[n % 2][:, :, :], io[names[n]].rearrange("(k p) n -> p k n", p=P)).then_inc(w_loaded[n], 16)

            for g in range(GROUPS):
                sp.dma_start(x[:, g * GT:(g + 1) * GT, :], x_v[:, g * GT:(g + 1) * GT, :]).then_inc(x_loaded[g], 16)
                if g == 0:
                    load_w(0)
            load_w(1)
            sp.dma_start(last_raw[:, :, :], io["ctx_last"].rearrange("(k p) n -> p k n", p=P)).then_inc(last_loaded, 16)
            for r in range(2):
                sp.dma_start(ctx_raw[r][:, :, :], ctx_v[:, :, r * 2 * TKM:(r + 1) * 2 * TKM]).then_inc(ctx_loaded[r], 16)
            for g in range(GROUPS):
                if g < 2:
                    sp.wait_ge(w_lo, g + 1)
                    load_w(g + 2)
                for t in range(KT):
                    sp.wait_ge(q_ready, g * KT + t + 1)
                    sp.dma_start(io["queries"][:, t, g * GROUP:(g + 1) * GROUP], queries[:, t, :]).then_inc(q_stored[t], 16)
            for t in range(KT):
                sp.wait_ge(q_stored[t], 16 * GROUPS)

        @block.gpsimd
        def _(gp):
            def split_lo(n):
                gp.wait_ge(w_hi, n + 1)
                gp.tensor_tensor(split[names[n]][1][:, :, :], w_raw[n % 2][:, :, :], f32(split[names[n]][0][:, :, :]),
                                 ALU.subtract).then_inc(w_lo, 1)

            sin_q = sin_k[:, 0:TQ].unsqueeze(1).broadcast_to([P, GROUP // TQ, TQ])
            split_lo(0)
            gp.wait_ge(const_loaded, 16 * CONSTS)
            for g in range(GROUPS):
                for t in range(KT):
                    gp.wait_ge(q_halves, g * KT + t + 1)
                    part = sin_part[t % 2][:, :].rearrange("p (b q) -> p b q", q=TQ)
                    gp.tensor_tensor(part, part, sin_q, ALU.mult).then_inc(q_sin, 1)
                    gp.wait_ge(q_sin, g * KT + t + 1)
                    if g:
                        gp.wait_ge(q_stored[t], 16 * g)
                    gp.tensor_tensor(queries[:, t, :], cos_part[t % 2][:, :], sin_part[t % 2][:, :],
                                     ALU.add).then_inc(q_ready, 1)
                if g < 3:
                    split_lo(g + 1)
                if g == 1:
                    gp.wait_ge(last_hi_ready, 1)
                    gp.tensor_tensor(last_lo[:, :, :], last_raw[:, :, :], f32(last_hi[:, :, :]), ALU.subtract)\
                        .then_inc(last_lo_ready, 1)

        @block.scalar
        def _(act):
            def split_hi(n):
                act.wait_ge(w_loaded[n], 16)
                act.activation(split[names[n]][0][:, :, :], w_raw[n % 2][:, :, :], ACT.Copy).then_inc(w_hi, 1)

            act.wait_ge(norm.eps_set, 1)
            norm.scalar_sd(act, 0)
            split_hi(0)
            for g in range(GROUPS):
                if g + 1 < GROUPS:
                    norm.scalar_sd(act, g + 1)
                norm.scalar_hi(act, g, lambda s: xt[g % 2][0][:, :, s * P:(s + 1) * P])
                if g >= 1:
                    split_hi(g)
                if g == 1:
                    act.wait_ge(last_loaded, 16)
                    act.activation(last_hi[:, :, :], last_raw[:, :, :], ACT.Copy).then_inc(last_hi_ready, 1)

        @block.tensor
        def _(pe):
            def query(g):
                pe.wait_ge(norm.lo_ready, (g + 1) * GT)
                for t in range(KT):
                    if g * KT + t >= 2:
                        pe.wait_ge(q_halves, g * KT + t - 1)
                    cols = slice(t * P, (t + 1) * P)
                    three_pass(pe, proj[t % 2][:, :], [((wq[0][:, k, cols], wq[1][:, k, cols]),
                                                        (xt[g % 2][0][:, k, :], xt[g % 2][1][:, k, :])) for k in range(KT)])\
                        .then_inc(q_done, 1)

            pe.wait_ge(const_loaded, 16 * CONSTS)
            norm.tensor_turn(pe, 0)
            for g in range(1, GROUPS):
                norm.tensor_turn(pe, g)
                if g == 1:
                    pe.wait_ge(w_lo, 1)
                query(g - 1)
            pe.wait_ge(w_lo, 3)
            pe.wait_ge(last_lo_ready, 1)
            for i in range(2):
                for t in range(KT):
                    cols = slice(t * P, (t + 1) * P)
                    mm = three_pass(pe, last_ps[:, i, t, :], [((weights[i][0][:, k, cols], weights[i][1][:, k, cols]),
                                                               (last_hi[:, k, :], last_lo[:, k, :])) for k in range(KT)])
            mm.then_inc(last_done, 1)
            query(GROUPS - 1)

        @block.vector
        def _(dve):
            cos_q = cos_k[:, 0:TQ].unsqueeze(1).broadcast_to([P, GROUP // TQ, TQ])

            def rope(g):
                for t in range(KT):
                    n = g * KT + t
                    if n >= 2:
                        dve.wait_ge(q_ready, n - 1)
                    dve.wait_ge(q_done, n + 1)
                    dve.tensor_tensor(cos_part[t % 2][:, :].rearrange("p (b q) -> p b q", q=TQ),
                                      proj[t % 2][:, :].rearrange("p (b q) -> p b q", q=TQ), cos_q, ALU.mult)
                    dve.stream_shuffle(sin_part[t % 2][:, :], proj[t % 2][:, :], SHUFFLE_HALVES).then_inc(q_halves, 1)

            norm.start(dve)
            dve.wait_ge(x_loaded[0], 16)
            norm.vector_stats(dve, 0)
            for g in range(GROUPS):
                if g + 1 < GROUPS:
                    dve.wait_ge(x_loaded[g + 1], 16)
                    norm.vector_stats(dve, g + 1)
                norm.vector_lo(dve, g, lambda s: xt[g % 2][0][:, :, s * P:(s + 1) * P],
                               lambda s: xt[g % 2][1][:, :, s * P:(s + 1) * P])
                if g == 0:
                    dve.wait_ge(const_loaded, 16 * CONSTS)
                else:
                    rope(g - 1)
            dve.wait_ge(last_done, 1)
            dve.stream_shuffle(last_sin[:, :, :], last_ps[:, 0, :, :], SHUFFLE_HALVES).then_inc(last_step, 1)
            dve.wait_ge(last_step, 1)
            dve.tensor_scalar(last_sin[:, :, :], last_sin[:, :, :], sin_k[:, TKM:TK], None, ALU.mult).then_inc(last_step, 1)
            dve.wait_ge(last_step, 2)
            dve.scalar_tensor_tensor(key_last[:, :, :], last_ps[:, 0, :, :], cos_k[:, TKM:TK], last_sin[:, :, :],
                                     ALU.mult, ALU.add)
            dve.tensor_copy(value_last[:, :, :], last_ps[:, 1, :, :])
            rope(GROUPS - 1)


def block_b(nc, sb, pb, sem, io, x, ident, cos_k, sin_k, key_last, value_last, weights, ctx_raw, ctx_loaded):
    wk, wv, wo = weights
    ctx_hi = [sb(f"ctx_hi{i}", [P, KT, 2 * TKM], F32R) for i in range(2)]
    ctx_lo = [sb(f"ctx_lo{i}", [P, KT, 2 * TKM], F32R) for i in range(2)]
    keys = [sb(f"keys{i}", [P, KT, 2, TK]) for i in range(2)]
    values = [sb(f"values{i}", [P, 4, D]) for i in range(2)]
    q_pair = [sb(f"q_pair{i}", [P, KT, 2 * TQ]) for i in range(2)]
    q_diag = [sb(f"q_diag{i}", [P, KT, 2, P]) for i in range(2)]
    cos_part = [sb(f"cos_b{i}", [P, 2 * TKM]) for i in range(2)]
    sin_part = [sb(f"sin_b{i}", [P, 2 * TKM]) for i in range(2)]
    row_max = sb("row_max", [P, 2])
    neg_max = sb("neg_max", [P, 2])
    row_sum = sb("row_sum", [P, 2])
    row_inv = sb("row_inv", [P, 2])
    probs = sb("probs", [P, 2, TK])
    probs_t = sb("probs_t", [P, 2, TKM])
    p_last = sb("p_last", [P, KT, 2])
    p_last_t = sb("p_last_t", [P, KT, 2, TQ])
    last_part = sb("last_part", [P, KT, 2, TQ])
    heads_t = sb("heads_t", [P, KT, P])
    heads_hi, heads_lo = sb("heads_hi", [P, KT, P], F32R), sb("heads_lo", [P, KT, P], F32R)
    proj = [pb(f"proj_b{i}", [P, D]) for i in range(2)]
    scores = pb("scores_b", [P, 2, 512])
    turned = pb("turned_b", [P, 2, 512])
    heads = [pb(f"heads_b{i}", [P, 2, 2, P]) for i in range(2)]

    zeroed = sem("b_zeroed")
    last_step = sem("b_last_step")
    heads_ready = sem("b_heads_ready")
    q_loaded = [sem(f"q_loaded{i}") for i in range(2)]
    ctx_hi_ready = sem("ctx_hi_ready")
    ctx_lo_ready = sem("ctx_lo_ready")
    q_diag_ready = sem("q_diag_ready")
    proj_done = sem("proj_done")
    v_ready = sem("v_ready")
    k_read = sem("k_read")
    k_sin = sem("k_sin")
    k_ready = sem("k_ready")
    s_done = sem("s_done")
    max_ready = sem("max_ready")
    neg_max_ready = sem("neg_max_ready")
    exp_done = sem("exp_done")
    inv_ready = sem("inv_ready")
    p_last_ready = sem("p_last_ready")
    p_ready = sem("p_ready")
    t_done = sem("t_done")
    pt_ready = sem("pt_ready")
    pv_done = sem("pv_done")
    heads_read = sem("heads_read")
    heads_hi_ready = sem("heads_hi_ready")
    heads_lo_ready = sem("heads_lo_ready")
    wo_done = sem("b_wo_done")
    x_added = sem("b_x_added")
    X_CREDIT = 1

    ctx_v = io["ctx_main"].rearrange("(k p) n -> p k n", p=P)
    LOOPS = (PAIRS - 2) // 2

    def phases(eng, phase):
        with eng.Fori(0, LOOPS) as u:
            for j in range(2):
                phase(u * 2 + j, j, True, True, u)
        phase(PAIRS - 2, 0, True, False, LOOPS)
        phase(PAIRS - 1, 1, False, False, LOOPS)

    with nc.Block() as block:
        @block.sync
        def _(sp):
            def load_ctx(r, par):
                sp.dma_start(ctx_raw[par][:, :, :], ctx_v[:, :, bass.ds(r * 2 * TKM, 2 * TKM)]).then_inc(ctx_loaded[par], 16)

            def load_q(r, par):
                sp.dma_start(q_pair[par][:, :, :], io["queries"][:, :, bass.ds(r * 2 * TQ, 2 * TQ)]).then_inc(q_loaded[par], 16)

            for r in range(2):
                load_q(r, r)
            for r in range(2, 4):
                sp.wait_ge(ctx_lo_ready, 4 * (r - 1))
                load_ctx(r, r % 2)
            with sp.Fori(0, (PAIRS - 4) // 2) as u:
                for j in range(2):
                    p = u * 2 + j
                    sp.wait_ge(ctx_lo_ready, 4 * (p + 3))
                    load_ctx(p + 4, j)
                    sp.wait_ge(q_diag_ready, p + 1)
                    load_q(p + 2, j)
            for p in range(PAIRS - 4, PAIRS - 2):
                sp.wait_ge(q_diag_ready, p + 1)
                load_q(p + 2, p % 2)

        @block.gpsimd
        def _(gp):
            def split_lo(r, par):
                for k in range(KT):
                    gp.wait_ge(ctx_hi_ready, 4 * r + k + 1)
                    gp.tensor_tensor(ctx_lo[par][:, k, :], ctx_raw[par][:, k, :], f32(ctx_hi[par][:, k, :]), ALU.subtract)\
                        .then_inc(ctx_lo_ready, 1)

            def sines(r):
                for t in range(KT):
                    gp.wait_ge(k_read, 4 * r + t + 1)
                    part = sin_part[t % 2][:, :].rearrange("p (b k) -> p b k", k=TKM)
                    gp.tensor_tensor(part, part, sin_k[:, 0:TKM].unsqueeze(1).broadcast_to([P, 2, TKM]), ALU.mult)\
                        .then_inc(k_sin, 1)

            for par in range(2):
                ins = gp.memset(q_diag[par][:, :, :, :], 0.0)
            ins.then_inc(zeroed, 1)
            split_lo(0, 0)
            split_lo(1, 1)
            sines(0)

            def phase(p, par, projects, splits, u):
                if splits:
                    split_lo(p + 2, par)
                if projects:
                    sines(p + 1)

            phases(gp, phase)

        @block.scalar
        def _(act):
            def value_out(r, m, par):
                act.wait_ge(proj_done, 8 * r + m + 1)
                act.activation(values[par][:, m, :], proj[m % 2][:, :], ACT.Copy).then_inc(v_ready, 1)

            def split_hi(r, k, par, count):
                if k == 0:
                    act.wait_ge(ctx_loaded[par], 16 * count)
                act.activation(ctx_hi[par][:, k, :], ctx_raw[par][:, k, :], ACT.Copy).then_inc(ctx_hi_ready, 1)

            def exps(p, n):
                act.wait_ge(neg_max_ready, 4 * p + n + 1)
                for b in range(2):
                    ins = act.activation(probs[:, b, :], scores[:, b, 0:TK], ACT.Exp, bias=neg_max[:, b:b + 1], scale=X_SCALE,
                                         accum_out=row_sum[:, b:b + 1])
                ins.then_inc(exp_done, 1)

            def probs_out(p, n):
                act.wait_ge(t_done, 4 * p + n + 1)
                act.activation(probs_t[:, :, :], turned[:, :, 0:TKM], ACT.Copy).then_inc(pt_ready, 1)

            def heads_out(p, half, par):
                act.wait_ge(pv_done, 4 * p + 2 * half + 2)
                for a in range(4):
                    rows = slice(a * X_HEAD, (a + 1) * X_HEAD)
                    ins = act.activation(
                        heads_t[rows, 2 * half:2 * half + 2, par * 2 * TQ:(par + 1) * 2 * TQ].rearrange("p t (b q) -> p t b q", q=TQ),
                        heads[half][rows, :, :, rows], ACT.Copy)
                ins.then_inc(heads_read, 1)

            for r in range(2):
                for k in range(KT):
                    split_hi(r, k, r, 1)
            for m in range(4):
                value_out(0, m, 0)
            exps(0, 0)

            def phase(p, par, projects, splits, u):
                for n in range(4):
                    probs_out(p, n)
                    if n < 3:
                        exps(p, n + 1)
                    if projects:
                        value_out(p + 1, n, 1 - par)
                    if splits:
                        split_hi(p + 2, n, par, u + 2)
                heads_out(p, 0, par)
                heads_out(p, 1, par)
                if par:
                    act.wait_ge(heads_ready, p + 1)
                    act.activation(heads_hi[:, :, :], heads_t[:, :, :], ACT.Copy).then_inc(heads_hi_ready, 1)
                if projects:
                    exps(p + 1, 0)

            phases(act, phase)

        @block.tensor
        def _(pe):
            def project(r, m, par):
                if m == 0:
                    pe.wait_ge(ctx_lo_ready, 4 * r + 4)
                    pe.wait_ge(ctx_hi_ready, 4 * r + 4)
                if m < 2:
                    if not isinstance(r, int) or r > 0:
                        pe.wait_ge(k_read, 4 * r - 1 + m)
                elif m < 6:
                    pe.wait_ge(v_ready, 4 * r + m - 1)
                else:
                    pe.wait_ge(k_read, 4 * r + m - 5)
                hi, lo = ctx_hi[par], ctx_lo[par]
                if m < 4:
                    rows = slice(m * P, (m + 1) * P)
                    terms = [((hi[:, k, rows], lo[:, k, rows]), (wv[0][:, k, :], wv[1][:, k, :])) for k in range(KT)]
                else:
                    cols = slice((m - 4) * P, (m - 3) * P)
                    terms = [((wk[0][:, k, cols], wk[1][:, k, cols]), (hi[:, k, :], lo[:, k, :])) for k in range(KT)]
                three_pass(pe, proj[m % 2][:, :], terms).then_inc(proj_done, 1)

            def score(p, n, par):
                if n == 0:
                    pe.wait_ge(q_diag_ready, p + 1)
                pe.wait_ge(k_ready, 4 * p + n + 1)
                for b in range(2):
                    mm = pe.matmul(scores[:, b, 0:TK], q_diag[par][:, n, b, :], keys[par][:, n, b, :], start=True, stop=True)
                mm.then_inc(s_done, 1)

            def turn(p, n):
                pe.wait_ge(p_ready, 4 * p + n + 1)
                for b in range(2):
                    for c in range(2):
                        mm = pe.transpose(turned[:, b, c * P:(c + 1) * P], probs[:, b, c * P:(c + 1) * P], ident[:, :])
                mm.then_inc(t_done, 1)

            def attend(p, n, par, count):
                if n == 0 and par == 0:
                    pe.wait_ge(x_added, count - 1 + X_CREDIT)
                if n == 0:
                    pe.wait_ge(v_ready, 4 * p + 4)
                pe.wait_ge(pt_ready, 4 * p + n + 1)
                cols = slice(n * P, (n + 1) * P)
                for b in range(2):
                    out = heads[n // 2][:, n % 2, b, :]
                    for c in range(2):
                        mm = pe.matmul(out, values[par][:, 2 * b + c, cols], probs_t[:, b, c * P:(c + 1) * P],
                                       start=(c == 0), stop=(c == 1))
                mm.then_inc(pv_done, 1)

            def output(v):
                pe.wait_ge(heads_hi_ready, v + 1)
                pe.wait_ge(heads_lo_ready, v + 1)
                three_pass(pe, heads[0][:, :, :, :].rearrange("p a b q -> p (a b q)"),
                           [((heads_hi[:, k, :], heads_lo[:, k, :]), (wo[0][:, k, :], wo[1][:, k, :])) for k in range(KT)])\
                    .then_inc(wo_done, 1)

            for m in range(8):
                if m == 7:
                    score(0, 0, 0)
                project(0, m, 0)

            def phase(p, par, projects, splits, u):
                for slot in range(8):
                    if 1 <= slot <= 4:
                        attend(p, slot - 1, par, u + 1)
                    if slot <= 3:
                        turn(p, slot)
                    if slot <= 2:
                        score(p, slot + 1, par)
                    if slot == 7 and projects:
                        score(p + 1, 0, 1 - par)
                    if projects:
                        project(p + 1, slot, 1 - par)
                if par:
                    output(u)

            phases(pe, phase)

        @block.vector
        def _(dve):
            def key_sum(r, t, par):
                dve.wait_ge(k_sin, 4 * r + t + 1)
                dve.tensor_tensor(keys[par][:, t, :, 0:TKM], cos_part[t % 2][:, :].rearrange("p (b k) -> p b k", k=TKM),
                                  sin_part[t % 2][:, :].rearrange("p (b k) -> p b k", k=TKM), ALU.add).then_inc(k_ready, 1)

            def key_tile(r, t, par):
                if not isinstance(r, int) or r > 0 or t >= 2:
                    dve.wait_ge(k_ready, 4 * r + t - 1)
                dve.wait_ge(proj_done, 8 * r + t + 5)
                dve.tensor_tensor(cos_part[t % 2][:, :].rearrange("p (b k) -> p b k", k=TKM),
                                  proj[t % 2][:, :].rearrange("p (b k) -> p b k", k=TKM),
                                  cos_k[:, 0:TKM].unsqueeze(1).broadcast_to([P, 2, TKM]), ALU.mult)
                dve.stream_shuffle(sin_part[t % 2][:, :], proj[t % 2][:, :], SHUFFLE_HALVES).then_inc(k_read, 1)
                if t == 0:
                    dve.tensor_copy(keys[par][:, :, :, TKM], key_last[:, :, bass.ds(r * 2, 2)])
                else:
                    key_sum(r, t - 1, par)

            def diagonal(par, count):
                dve.wait_ge(q_loaded[par], 16 * count)
                for a in range(4):
                    rows = slice(a * X_HEAD, (a + 1) * X_HEAD)
                    ins = dve.tensor_copy(q_diag[par][rows, :, :, rows],
                                          q_pair[par][rows, :, :].rearrange("p t (b q) -> p t b q", q=TQ))
                ins.then_inc(q_diag_ready, 1)

            def softmax(p, n):
                q = 4 * p + n
                dve.wait_ge(s_done, q + 1)
                dve.tensor_reduce(row_max[:, :], scores[:, :, 0:TK], AX.X, ALU.max).then_inc(max_ready, 1)
                dve.wait_ge(max_ready, q + 1)
                dve.tensor_scalar(neg_max[:, :], row_max[:, :], -X_SCALE, None, ALU.mult).then_inc(neg_max_ready, 1)
                dve.wait_ge(exp_done, q + 1)
                dve.reciprocal(row_inv[:, :], row_sum[:, :]).then_inc(inv_ready, 1)
                dve.wait_ge(inv_ready, q + 1)
                for b in range(2):
                    ins = dve.tensor_scalar(probs[:, b, 0:TKM], probs[:, b, 0:TKM], row_inv[:, b:b + 1], None, ALU.mult)
                ins.then_inc(p_ready, 1)
                dve.tensor_tensor(p_last[:, n, :], probs[:, :, TKM], row_inv[:, :], ALU.mult).then_inc(p_last_ready, 1)

            def last_rows(p):
                dve.wait_ge(p_last_ready, 4 * p + 4)
                dve.transpose(p_last_t[:, :, :, :].rearrange("p t b q -> p (t b) q"),
                              p_last[:, :, :].rearrange("p t b -> p (t b)").unsqueeze(2).broadcast_to([P, 2 * KT, TQ]))\
                    .then_inc(last_step, 1)
                dve.wait_ge(last_step, 2 * p + 1)
                dve.tensor_tensor(last_part[:, :, :, :], p_last_t[:, :, :, :],
                                  value_last[:, :, bass.ds(p * 2, 2)].unsqueeze(3).broadcast_to([P, KT, 2, TQ]), ALU.mult)\
                    .then_inc(last_step, 1)

            def add_last(p, par):
                dve.wait_ge(heads_read, 2 * p + 2)
                dve.wait_ge(last_step, 2 * p + 2)
                own = heads_t[:, :, par * 2 * TQ:(par + 1) * 2 * TQ]
                dve.tensor_tensor(own, own, last_part[:, :, :, :].rearrange("p t b q -> p t (b q)"), ALU.add)\
                    .then_inc(heads_ready, 1)

            dve.wait_ge(zeroed, 1)
            diagonal(0, 1)
            dve.sem_inc(x_added, X_CREDIT)
            for t in range(3):
                key_tile(0, t, 0)
            softmax(0, 0)
            key_tile(0, 3, 0)
            key_sum(0, 3, 0)

            def phase(p, par, projects, splits, u):
                for n in range(1, 4):
                    softmax(p, n)
                last_rows(p)
                if projects:
                    diagonal(1 - par, u + 1 + par)
                    for t in range(3):
                        key_tile(p + 1, t, 1 - par)
                        if t == 1:
                            add_last(p, par)
                else:
                    add_last(p, par)
                if par:
                    dve.wait_ge(heads_hi_ready, u + 1)
                    dve.tensor_tensor(heads_lo[:, :, :], heads_t[:, :, :], f32(heads_hi[:, :, :]), ALU.subtract)\
                        .then_inc(heads_lo_ready, 1)
                if projects:
                    softmax(p + 1, 0)
                    key_tile(p + 1, 3, 1 - par)
                    key_sum(p + 1, 3, 1 - par)
                if par:
                    dve.wait_ge(wo_done, u + 1)
                    row = x[:, bass.ds(u, 1), :].rearrange("p a d -> p (a d)")
                    dve.tensor_tensor(row, heads[0][:, :, :, :].rearrange("p a b q -> p (a b q)"), row, ALU.add)\
                        .then_inc(x_added, 1)

            phases(dve, phase)


def block_c(nc, sb, pb, sem, io, x, ident, xt_hi, xt_lo):
    w_qk_raw, w_v_raw, w_o_raw = sb("w_qk_raw", [P, KT, 4 * DH]), sb("w_v_raw", [P, KT, 2 * DH]), sb("w_o_raw", [P, 2, D])
    w_qk = (sb("w_qk_hi", [P, KT, 4 * DH], F32R), sb("w_qk_lo", [P, KT, 4 * DH], F32R))
    w_v = (sb("w_v_hi", [P, KT, 2 * DH], F32R), sb("w_v_lo", [P, KT, 2 * DH], F32R))
    w_o = (sb("w_o_hi", [P, 2, D], F32R), sb("w_o_lo", [P, 2, D], F32R))
    rms_scale = sb("rms_scale", [P, 2])
    out_scale = sb("out_scale", [P, 2])
    mask_rows = sb("mask_rows", [4, P], BF16)
    mask_cols = sb("mask_cols", [4, D], BF16)
    neg_half = sb("neg_half", [P, GT])
    lam = sb("lam", [P, 2, HEADS])
    neg_lam = sb("neg_lam", [P, HEADS])
    neg_lam_now = sb("neg_lam_now", [P, 1])

    const_c = sem("const_c")
    lam_step = sem("lam_step")
    lam_exp = sem("lam_exp")

    raw_loaded = {n: sem(f"c_{n}_loaded") for n in ("qk", "v", "o")}
    w_hi = {n: sem(f"c_{n}_hi") for n in ("qk", "v", "o")}
    w_lo = {n: sem(f"c_{n}_lo") for n in ("qk", "v", "o")}

    def load(sp, name, raw, h):
        sp.dma_start(raw[:, :, :], io["w_" + name][bass.ds(h, 1), :, :, :].rearrange("h p k n -> (h p) k n"))\
            .then_inc(raw_loaded[name], 16)

    def split_hi(act, name, raw, w, h):
        act.wait_ge(raw_loaded[name], 16 * h + 16)
        act.activation(w[0][:, :, :], raw[:, :, :], ACT.Copy).then_inc(w_hi[name], 1)

    def split_lo(gp, name, raw, w, h):
        gp.wait_ge(w_hi[name], h + 1)
        gp.tensor_tensor(w[1][:, :, :], raw[:, :, :], f32(w[0][:, :, :]), ALU.subtract).then_inc(w_lo[name], 1)

    with ExitStack() as part:
        def psb(name, shape, dt=F32):
            return part.enter_context(nc.sbuf_tensor(name, shape, dt))

        def ppb(name, shape, dt=F32):
            return part.enter_context(nc.psum_tensor(name, shape, dt))

        norm = Norm("n2", psb, ppb, sem, x, ident)
        lam_in = [psb(f"lam_in{i}", [P, HEADS, DH]) for i in range(2)]
        lam_prod = [psb(f"lam_prod{i}", [P, HEADS, DH]) for i in range(2)]
        lam_k = [psb(f"lam_k{i}", [P, HEADS, DH]) for i in range(2)]
        with nc.Block() as block:
            @block.sync
            def _(sp):
                load(sp, "qk", w_qk_raw, 0)
                load(sp, "v", w_v_raw, 0)
                load(sp, "o", w_o_raw, 0)
                for i, (a, b) in enumerate((("lq1", "lk1"), ("lq2", "lk2"))):
                    sp.dma_start(lam_in[i][:, :, :], io[a].partition_broadcast(P)).then_inc(const_c, 16)
                    sp.dma_start(lam_k[i][:, :, :], io[b].partition_broadcast(P)).then_inc(const_c, 16)
                sp.dma_start(rms_scale[:, :], io["rms"]).then_inc(const_c, 16)
                sp.dma_start(mask_rows[:, :], io["mask_rows"]).then_inc(const_c, 16)
                sp.dma_start(mask_cols[:, :], io["mask_cols"]).then_inc(const_c, 16)

            @block.scalar
            def _(act):
                act.wait_ge(norm.eps_set, 1)
                norm.scalar_sd(act, 0)
                for g in range(GROUPS):
                    if g + 1 < GROUPS:
                        norm.scalar_sd(act, g + 1)
                    norm.scalar_hi(act, g, lambda s: xt_hi[:, :, g * GROUP + s * P:g * GROUP + (s + 1) * P])
                    if g == 0:
                        split_hi(act, "qk", w_qk_raw, w_qk, 0)
                    if g == 1:
                        split_hi(act, "v", w_v_raw, w_v, 0)
                act.wait_ge(lam_step, 2)
                act.activation(lam[:, :, :], lam[:, :, :], ACT.Exp).then_inc(lam_exp, 1)

            @block.gpsimd
            def _(gp):
                split_lo(gp, "qk", w_qk_raw, w_qk, 0)
                split_lo(gp, "v", w_v_raw, w_v, 0)

            @block.tensor
            def _(pe):
                for g in range(GROUPS):
                    norm.tensor_turn(pe, g)

            @block.vector
            def _(dve):
                norm.start(dve)
                dve.memset(neg_half[:, :], -0.5)
                norm.vector_stats(dve, 0)
                for g in range(GROUPS):
                    if g + 1 < GROUPS:
                        norm.vector_stats(dve, g + 1)
                    norm.vector_lo(dve, g, lambda s: xt_hi[:, :, g * GROUP + s * P:g * GROUP + (s + 1) * P],
                                   lambda s: xt_lo[:, :, g * GROUP + s * P:g * GROUP + (s + 1) * P])
                dve.wait_ge(const_c, 16 * 7)
                for i in range(2):
                    ins = dve.tensor_tensor(lam_prod[i][:, :, :], lam_in[i][:, :, :], lam_k[i][:, :, :], ALU.mult)
                ins.then_inc(lam_step, 1)
                dve.wait_ge(lam_step, 1)
                dve.tensor_scalar(out_scale[:, :], rms_scale[:, :], 1.0 - LAMBDA_INIT, None, ALU.mult)
                for i in range(2):
                    ins = dve.tensor_reduce(lam[:, i, :], lam_prod[i][:, :, :], AX.X, ALU.add)
                ins.then_inc(lam_step, 1)
                dve.wait_ge(lam_exp, 1)
                dve.scalar_tensor_tensor(neg_lam[:, :], lam[:, 1, :], -LAMBDA_INIT, lam[:, 0, :], ALU.add, ALU.subtract)\
                    .then_inc(lam_step, 1)

    qk = sb("qk", [P, 4, GROUP])
    v = sb("v_c", [P, GT, 2 * DH])
    row_max = sb("c_row_max", [P, 2, GT])
    neg_max = sb("c_neg_max", [P, 2, GT])
    row_sum = sb("c_row_sum", [P, 2, GT])
    coef = sb("c_coef", [P, 2, GT])
    probs = sb("c_probs", [P, 2, GT, P])
    probs_t = sb("c_probs_t", [P, GT, P])
    sum_sq = sb("c_sum_sq", [P, GT])
    mean_sq = sb("c_mean_sq", [P, GT])
    rms_inv = sb("c_rms_inv", [P, GT])
    normed = sb("c_normed", [P, GT, 2 * DH])
    out_t = (sb("out_t_hi", [P, 2, GROUP], F32R), sb("out_t_lo", [P, 2, GROUP], F32R))
    proj = [pb(f"proj_c{i}", [P, D]) for i in range(2)]
    scores = pb("scores_c", [P, 2, GT, P])
    turned = [pb(f"turned_c{i}", [P, GT, P]) for i in range(2)]
    heads = pb("heads_c", [P, GT, 2 * DH])

    proj_done = sem("c_proj_done")
    proj_read = sem("c_proj_read")
    s_done = sem("c_s_done")
    max_ready = sem("c_max_ready")
    neg_max_ready = sem("c_neg_max_ready")
    exp_done = sem("c_exp_done")
    coef_step = sem("c_coef_step")
    p_ready = sem("c_p_ready")
    t_done = sem("c_t_done")
    pt_ready = sem("c_pt_ready")
    pv_done = sem("c_pv_done")
    sq_done = sem("c_sq_done")
    mean_sq_ready = sem("c_mean_sq_ready")
    rms_ready = sem("c_rms_ready")
    normed_ready = sem("c_normed_ready")
    turn_done = sem("c_turn_done")
    out_hi_ready = sem("c_out_hi")
    out_lo_ready = sem("c_out_lo")
    wo_done = sem("c_wo_done")
    x_added = sem("c_x_added")
    ADD_CREDIT = 8
    QK_TILE = [(0, 0), (1, 1), (2, 2), (3, 3)]

    def stages(eng, stage):
        stage(0, 0, first=True)
        with eng.Fori(0, HEADS - 1) as h:
            for g in range(1, GROUPS):
                stage(h, g)
            stage(h + 1, 0)
        for g in range(1, GROUPS):
            stage(HEADS - 1, g, final=True)

    with nc.Block() as block:
        @block.sync
        def _(sp):
            with sp.Fori(0, HEADS - 1) as h:
                sp.wait_ge(w_lo["qk"], h + 1)
                sp.wait_ge(w_hi["qk"], h + 1)
                load(sp, "qk", w_qk_raw, h + 1)
                sp.wait_ge(w_lo["v"], h + 1)
                load(sp, "v", w_v_raw, h + 1)
                sp.wait_ge(w_lo["o"], h + 1)
                load(sp, "o", w_o_raw, h + 1)

        @block.gpsimd
        def _(gp):
            def rms(n):
                gp.wait_ge(mean_sq_ready, n + 1)
                gp.tensor_tensor(rms_inv[:, :], mean_sq[:, :], neg_half[:, :], ALU.pow).then_inc(rms_ready, 1)

            def stage(h, g, first=False, final=False):
                n = h * GROUPS + g
                if not first:
                    rms(n - 1)
                if g == GROUPS - 1 and not final:
                    split_lo(gp, "qk", w_qk_raw, w_qk, h + 1)
                    split_lo(gp, "v", w_v_raw, w_v, h + 1)

            stages(gp, stage)
            rms(HEADS * GROUPS - 1)

        @block.scalar
        def _(act):
            def split_o(h):
                act.wait_ge(raw_loaded["o"], 16 * h + 16)
                for f in range(2):
                    ins = act.activation(w_o[0][:, f, :], w_o_raw[:, f, :], ACT.Copy, scale=out_scale[:, f:f + 1])
                ins.then_inc(w_hi["o"], 1)

            def proj_out(n, m):
                act.wait_ge(proj_done, 6 * n + m + 1)
                if m < 4:
                    dst = qk[:, m, :]
                else:
                    dst = v[:, 2 * (m - 4):2 * (m - 4) + 2, :].rearrange("p a d -> p (a d)")
                act.activation(dst, proj[m % 2][:, :], ACT.Copy).then_inc(proj_read, 1)

            def probs_out(n):
                act.wait_ge(t_done, n + 1)
                act.activation(probs_t[:, :, :], turned[0][:, :, :], ACT.Copy).then_inc(pt_ready, 1)

            def squares(n):
                act.wait_ge(pv_done, n + 1)
                for s in range(GT):
                    ins = act.activation(normed[:, s, :], heads[:, s, :], ACT.Square, accum_out=sum_sq[:, s:s + 1])
                ins.then_inc(sq_done, 1)

            def out_hi(n):
                act.wait_ge(turn_done, n + 1)
                for f in range(2):
                    ins = act.activation(out_t[0][:, f, :], turned[f][:, :, :].rearrange("p a q -> p (a q)"), ACT.Copy)
                ins.then_inc(out_hi_ready, 1)

            def exps(n, half):
                if half == 0:
                    act.wait_ge(neg_max_ready, n + 1)
                for s in range(GT):
                    ins = act.activation(probs[:, half, s, :], scores[:, half, s, :], ACT.Exp, bias=neg_max[:, half, s:s + 1],
                                         scale=D_SCALE, accum_out=row_sum[:, half, s:s + 1])
                if half == 1:
                    ins.then_inc(exp_done, 1)

            def stage(h, g, first=False, final=False):
                n = h * GROUPS + g
                proj_out(n, 0)
                proj_out(n, 1)
                if g == 1:
                    split_o(h)
                if not first:
                    probs_out(n - 1)
                proj_out(n, 2)
                if not first:
                    squares(n - 1)
                proj_out(n, 3)
                if g == GROUPS - 1 and not final:
                    split_hi(act, "qk", w_qk_raw, w_qk, h + 1)
                proj_out(n, 4)
                if not first:
                    out_hi(n - 1)
                exps(n, 0)
                proj_out(n, 5)
                exps(n, 1)
                if g == GROUPS - 1 and not final:
                    split_hi(act, "v", w_v_raw, w_v, h + 1)

            stages(act, stage)
            last = HEADS * GROUPS - 1
            probs_out(last)
            squares(last)
            out_hi(last)

        @block.tensor
        def _(pe):
            def project(n, h, g, m, first):
                if m < 2:
                    if not first:
                        pe.wait_ge(proj_read, 6 * n - 1 + m)
                        pe.wait_ge(x_added, 4 * n - 5 + m + ADD_CREDIT)
                else:
                    pe.wait_ge(proj_read, 6 * n + m - 1)
                rows = slice(g * GROUP, (g + 1) * GROUP)
                if m < 4:
                    if m == 0 and g == 0:
                        pe.wait_ge(w_lo["qk"], h + 1)
                    cols = slice(m * P, (m + 1) * P)
                    three_pass(pe, proj[m % 2][:, :], [((w_qk[0][:, k, cols], w_qk[1][:, k, cols]),
                                                        (xt_hi[:, k, rows], xt_lo[:, k, rows])) for k in range(KT)])\
                        .then_inc(proj_done, 1)
                else:
                    if m == 4 and g == 0:
                        pe.wait_ge(w_lo["v"], h + 1)
                    for s in (2 * (m - 4), 2 * (m - 4) + 1):
                        rows = slice((g * GT + s) * P, (g * GT + s + 1) * P)
                        mm = three_pass(pe, proj[m % 2][:, (s % 2) * 2 * DH:(s % 2 + 1) * 2 * DH],
                                        [((xt_hi[:, k, rows], xt_lo[:, k, rows]), (w_v[0][:, k, :], w_v[1][:, k, :]))
                                         for k in range(KT)])
                    mm.then_inc(proj_done, 1)

            def score(n):
                pe.wait_ge(proj_read, 6 * n + 4)
                for half in range(2):
                    pe.matmul(scores[:, half, :, :].rearrange("p a q -> p (a q)"), mask_rows[:, :], mask_cols[:, :],
                              start=True, stop=False, skip_group_check=True)
                    for s in range(GT):
                        cols = slice(s * P, (s + 1) * P)
                        mm = pe.matmul(scores[:, half, s, :], qk[:, half, cols], qk[:, 2 + half, cols],
                                       start=False, stop=(s == GT - 1), skip_group_check=True)
                mm.then_inc(s_done, 1)

            def turn(n):
                pe.wait_ge(p_ready, n + 1)
                for s in range(GT):
                    mm = pe.transpose(turned[0][:, s, :], probs[:, 0, s, :], ident[:, :])
                mm.then_inc(t_done, 1)

            def attend(n):
                pe.wait_ge(pt_ready, n + 1)
                pe.wait_ge(proj_read, 6 * n + 6)
                for s in range(GT):
                    mm = pe.matmul(heads[:, s, :], probs_t[:, s, :], v[:, s, :], start=True, stop=True)
                mm.then_inc(pv_done, 1)

            def turn_out(n):
                pe.wait_ge(normed_ready, n + 1)
                for f in range(2):
                    for s in range(GT):
                        mm = pe.transpose(turned[f][:, s, :], normed[:, s, f * P:(f + 1) * P], ident[:, :])
                mm.then_inc(turn_done, 1)

            def output(n, h, now):
                pe.wait_ge(w_lo["o"], h + 1)
                pe.wait_ge(out_lo_ready, n + 1)
                for s in range(GT):
                    if s < 2:
                        pe.wait_ge(proj_read, 6 * now + 5 + s)
                    else:
                        pe.wait_ge(x_added, 4 * n + s - 1 + ADD_CREDIT)
                    cols = slice(s * P, (s + 1) * P)
                    three_pass(pe, proj[s % 2][:, :], [((out_t[0][:, f, cols], out_t[1][:, f, cols]),
                                                        (w_o[0][:, f, :], w_o[1][:, f, :])) for f in range(2)])\
                        .then_inc(wo_done, 1)

            def stage(h, g, first=False, final=False):
                n = h * GROUPS + g
                prev = n - 1
                prev_head = h if g else h - 1
                project(n, h, g, 0, first)
                project(n, h, g, 1, first)
                if not first:
                    turn(prev)
                project(n, h, g, 2, first)
                if not first:
                    attend(prev)
                project(n, h, g, 3, first)
                project(n, h, g, 4, first)
                score(n)
                if not first:
                    turn_out(prev)
                project(n, h, g, 5, first)
                if not first:
                    output(prev, prev_head, n)

            stages(pe, stage)
            last = HEADS * GROUPS - 1
            turn(last)
            attend(last)
            turn_out(last)
            output(last, HEADS - 1, last)

        @block.vector
        def _(dve):
            dve.sem_inc(x_added, ADD_CREDIT)

            def split_o(h):
                dve.wait_ge(w_hi["o"], h + 1)
                for f in range(2):
                    ins = dve.scalar_tensor_tensor(w_o[1][:, f, :], w_o_raw[:, f, :], out_scale[:, f:f + 1],
                                                   f32(w_o[0][:, f, :]), ALU.mult, ALU.subtract)
                ins.then_inc(w_lo["o"], 1)

            def mean_squares(n):
                dve.wait_ge(sq_done, n + 1)
                dve.tensor_scalar(mean_sq[:, :], sum_sq[:, :], 1.0 / (2 * DH), EPS, ALU.mult, ALU.add).then_inc(mean_sq_ready, 1)

            def normalise(n):
                dve.wait_ge(rms_ready, n + 1)
                for s in range(GT):
                    ins = dve.tensor_scalar(normed[:, s, :], heads[:, s, :], rms_inv[:, s:s + 1], None, ALU.mult)
                ins.then_inc(normed_ready, 1)

            def maxima(n):
                dve.wait_ge(s_done, n + 1)
                dve.tensor_reduce(row_max[:, :, :], scores[:, :, :, :], AX.X, ALU.max).then_inc(max_ready, 1)
                dve.wait_ge(max_ready, n + 1)
                dve.tensor_scalar(neg_max[:, :, :], row_max[:, :, :], -D_SCALE, None, ALU.mult).then_inc(neg_max_ready, 1)

            def out_lo(n):
                dve.wait_ge(out_hi_ready, n + 1)
                for f in range(2):
                    ins = dve.tensor_tensor(out_t[1][:, f, :], turned[f][:, :, :].rearrange("p a q -> p (a q)"),
                                            f32(out_t[0][:, f, :]), ALU.subtract)
                ins.then_inc(out_lo_ready, 1)

            def combine(n):
                dve.wait_ge(exp_done, n + 1)
                dve.reciprocal(coef[:, :, :], row_sum[:, :, :]).then_inc(coef_step, 1)
                dve.wait_ge(coef_step, 3 * n + 1)
                dve.tensor_scalar(coef[:, 1, :], coef[:, 1, :], neg_lam_now[:, :], None, ALU.mult).then_inc(coef_step, 1)
                dve.wait_ge(coef_step, 3 * n + 2)
                for s in range(GT):
                    ins = dve.tensor_scalar(probs[:, 1, s, :], probs[:, 1, s, :], coef[:, 1, s:s + 1], None, ALU.mult)
                ins.then_inc(coef_step, 1)
                dve.wait_ge(coef_step, 3 * n + 3)
                for s in range(GT):
                    ins = dve.scalar_tensor_tensor(probs[:, 0, s, :], probs[:, 0, s, :], coef[:, 0, s:s + 1],
                                                   probs[:, 1, s, :], ALU.mult, ALU.add)
                ins.then_inc(p_ready, 1)

            def add(n, g):
                for s in range(GT):
                    dve.wait_ge(wo_done, 4 * n + s + 1)
                    dve.tensor_tensor(x[:, g * GT + s, :], proj[s % 2][:, :], x[:, g * GT + s, :], ALU.add).then_inc(x_added, 1)

            def stage(h, g, first=False, final=False):
                n = h * GROUPS + g
                if g == 1:
                    split_o(h)
                if not first:
                    mean_squares(n - 1)
                    normalise(n - 1)
                maxima(n)
                if not first:
                    out_lo(n - 1)
                if g == 0:
                    dve.tensor_copy(neg_lam_now[:, :], neg_lam[:, bass.ds(h, 1)])
                if not first:
                    add(n - 1, (g - 1) % GROUPS)
                combine(n)

            stages(dve, stage)
            last = HEADS * GROUPS - 1
            mean_squares(last)
            normalise(last)
            out_lo(last)
            add(last, GROUPS - 1)


def block_d(nc, sb, pb, sem, io, x, ident, xt_hi, xt_lo):
    w1_raw, w2_raw = sb("w1_raw", [P, KT, HC]), sb("w2_raw", [P, HT, D])
    w1 = (sb("w1_hi", [P, KT, HC], F32R), sb("w1_lo", [P, KT, HC], F32R))
    w2 = (sb("w2_hi", [P, HT, D], F32R), sb("w2_lo", [P, HT, D], F32R))
    w1_loaded = sem("w1_loaded")
    w2_loaded = sem("w2_loaded")
    w1_hi = sem("w1_hi_s")
    w1_lo = sem("w1_lo_s")
    w2_hi = sem("w2_hi_s")
    w2_lo = sem("w2_lo_s")

    def load(sp, raw, src, c, loaded):
        sp.dma_start(raw[:, :, :], src[bass.ds(c, 1), :, :, :].rearrange("c p k n -> (c p) k n")).then_inc(loaded, 16)

    def split_lo(gp, c, raw, w, hi_sem, lo_sem):
        gp.wait_ge(hi_sem, c + 1)
        gp.tensor_tensor(w[1][:, :, :], raw[:, :, :], f32(w[0][:, :, :]), ALU.subtract).then_inc(lo_sem, 1)

    def split_hi(act, c, raw, w, loaded, hi_sem):
        act.wait_ge(loaded, 16 * c + 16)
        act.activation(w[0][:, :, :], raw[:, :, :], ACT.Copy).then_inc(hi_sem, 1)

    masks = sb("masks", [P, EXPERTS, TOKENS], BF16)
    b1_all = sb("b1_all", [P, CHUNKS, HT])
    norm_loaded = sem("d_loaded")
    gate_wide = sem("gate_wide")
    gate_hi_ready = sem("gate_hi_ready")
    gate_lo_ready = sem("gate_lo_ready")
    gate_done = sem("gate_done")
    gate_read = sem("gate_read")
    gate_step = sem("gate_step")
    gate_shift = sem("gate_shift")
    gate_exp = sem("gate_exp")
    mask_ready = sem("mask_ready")
    bias_step = sem("bias_step")
    bias_sum_ready = sem("bias_sum_ready")
    xn_used = sem("xn_used")

    with ExitStack() as part:
        def psb(name, shape, dt=F32):
            return part.enter_context(nc.sbuf_tensor(name, shape, dt))

        def ppb(name, shape, dt=F32):
            return part.enter_context(nc.psum_tensor(name, shape, dt))

        norm = Norm("n3", psb, ppb, sem, x, ident)
        gate_raw = psb("gate_raw", [P, KT, 2])
        gate_w = psb("gate_w", [P, KT, 2, P])
        gate_hi, gate_lo = psb("gate_hi", [P, KT, 2, P], F32R), psb("gate_lo", [P, KT, 2, P], F32R)
        first_score = psb("first_score", [P, GROUP])
        top = psb("top", [P, GROUP])
        shifted = psb("shifted", [P, 2, GROUP])
        bias2 = psb("bias2", [P, EXPERTS, D])
        gate_ps = [ppb(f"gate_ps{i}", [P, 2, GROUP]) for i in range(2)]
        with nc.Block() as block:
            @block.sync
            def _(sp):
                sp.dma_start(gate_raw[:, :, :], io["gate"]).then_inc(norm_loaded, 16)
                sp.dma_start(bias2[:, :, :], io["b2"].partition_broadcast(P)).then_inc(norm_loaded, 16)
                sp.dma_start(b1_all[:, :, :], io["b1"]).then_inc(norm_loaded, 16)
                load(sp, w1_raw, io["w1"], 0, w1_loaded)
                load(sp, w2_raw, io["w2"], 0, w2_loaded)

            @block.gpsimd
            def _(gp):
                gp.wait_ge(norm_loaded, 48)
                gp.tensor_copy(gate_w[:, :, :, :], gate_raw[:, :, :].unsqueeze(3).broadcast_to([P, KT, 2, P])).then_inc(gate_wide, 1)
                gp.wait_ge(gate_hi_ready, 1)
                gp.tensor_tensor(gate_lo[:, :, :, :], gate_w[:, :, :, :], f32(gate_hi[:, :, :, :]), ALU.subtract)\
                    .then_inc(gate_lo_ready, 1)
                gp.tensor_tensor(bias2[:, 0, :], bias2[:, 0, :], bias2[:, 1, :], ALU.add).then_inc(bias_step, 1)
                gp.wait_ge(bias_step, 1)
                gp.tensor_tensor(bias2[:, 0, :], bias2[:, 0, :], bias2[:, 2, :], ALU.add).then_inc(bias_step, 1)
                gp.wait_ge(bias_step, 2)
                split_lo(gp, 0, w1_raw, w1, w1_hi, w1_lo)
                for g in range(GROUPS):
                    gp.wait_ge(norm.xn_ready, g + 1)
                    rows = x[:, g * GT:(g + 1) * GT, :]
                    gp.tensor_tensor(rows, rows, bias2[:, 0, :].unsqueeze(1).broadcast_to([P, GT, D]), ALU.add).then_inc(xn_used, 1)

            @block.scalar
            def _(act):
                act.wait_ge(gate_wide, 1)
                act.activation(gate_hi[:, :, :, :], gate_w[:, :, :, :], ACT.Copy).then_inc(gate_hi_ready, 1)
                act.wait_ge(norm.eps_set, 1)
                def first_scores(g):
                    act.wait_ge(gate_done, g + 1)
                    if g:
                        act.wait_ge(gate_shift, g)
                    act.activation(first_score[:, :], gate_ps[g % 2][:, 0, :], ACT.Copy).then_inc(gate_read, 1)

                def exps(g):
                    act.wait_ge(gate_shift, g + 1)
                    act.activation(shifted[:, :, :], shifted[:, :, :], ACT.Exp).then_inc(gate_exp, 1)

                norm.scalar_sd(act, 0)
                split_hi(act, 0, w1_raw, w1, w1_loaded, w1_hi)
                for g in range(GROUPS):
                    if g + 1 < GROUPS:
                        norm.scalar_sd(act, g + 1)
                    if g >= 2:
                        first_scores(g - 2)
                    norm.scalar_hi(act, g, lambda s: xt_hi[:, :, g * GROUP + s * P:g * GROUP + (s + 1) * P])
                    if g >= 2:
                        exps(g - 2)
                for g in range(GROUPS - 2, GROUPS):
                    first_scores(g)
                    exps(g)

            @block.tensor
            def _(pe):
                pe.wait_ge(gate_lo_ready, 1)
                def gate(g):
                    pe.wait_ge(norm.lo_ready, g * GT + GT)
                    if g >= 2:
                        pe.wait_ge(gate_shift, g - 1)
                    cols = slice(g * GROUP, (g + 1) * GROUP)
                    for e in range(2):
                        mm = three_pass(pe, gate_ps[g % 2][:, e, :],
                                        [((gate_hi[:, k, e, :], gate_lo[:, k, e, :]), (xt_hi[:, k, cols], xt_lo[:, k, cols]))
                                         for k in range(KT)])
                    mm.then_inc(gate_done, 1)

                for g in range(GROUPS):
                    norm.tensor_turn(pe, g)
                    if g:
                        gate(g - 1)
                gate(GROUPS - 1)

            @block.vector
            def _(dve):
                norm.start(dve)
                dve.memset(masks[:, 2, :], 1.0)
                def shift(g):
                    dve.wait_ge(gate_read, g + 1)
                    dve.tensor_tensor(top[:, :], gate_ps[g % 2][:, 1, :], first_score[:, :], ALU.max).then_inc(gate_step, 1)
                    dve.wait_ge(gate_step, g * 2 + 1)
                    dve.tensor_tensor(shifted[:, 0, :], first_score[:, :], top[:, :], ALU.subtract)
                    dve.tensor_tensor(shifted[:, 1, :], gate_ps[g % 2][:, 1, :], top[:, :], ALU.subtract).then_inc(gate_shift, 1)

                def mask(g):
                    dve.wait_ge(gate_exp, g + 1)
                    cols = slice(g * GROUP, (g + 1) * GROUP)
                    dve.tensor_tensor(masks[:, 1, cols], shifted[:, 1, :], shifted[:, 0, :], ALU.is_gt).then_inc(gate_step, 1)
                    dve.wait_ge(gate_step, g * 2 + 2)
                    dve.tensor_scalar(masks[:, 0, cols], masks[:, 1, cols], -1.0, 1.0, ALU.mult, ALU.add).then_inc(mask_ready, 1)

                norm.vector_stats(dve, 0)
                for g in range(GROUPS):
                    if g + 1 < GROUPS:
                        norm.vector_stats(dve, g + 1)
                    if g >= 2:
                        shift(g - 2)
                    norm.vector_lo(dve, g, lambda s: xt_hi[:, :, g * GROUP + s * P:g * GROUP + (s + 1) * P],
                                   lambda s: xt_lo[:, :, g * GROUP + s * P:g * GROUP + (s + 1) * P])
                    if g >= 2:
                        mask(g - 2)
                for g in range(GROUPS - 2, GROUPS):
                    shift(g)
                    mask(g)

    hidden = [(sb(f"hidden_hi{i}", [P, HT, GROUP], F32R), sb(f"hidden_lo{i}", [P, HT, GROUP], F32R)) for i in range(2)]
    masked = [sb(f"masked{i}", [P, GROUP]) for i in range(2)]
    relu = [sb(f"relu{i}", [P, GROUP]) for i in range(2)]
    mask_now = sb("mask_now", [P, TOKENS], BF16)
    b1_now = sb("b1_now", [P, HT])
    hid_ps = [pb(f"hid_ps{i}", [P, GROUP]) for i in range(2)]
    out_ps = [pb(f"out_ps{i}", [P, D]) for i in range(2)]

    now_ready = sem("now_ready")
    h_done = sem("h_done")
    h_read = sem("h_read")
    h_hi = sem("h_hi")
    h_relu = sem("h_relu")
    h_lo = sem("h_lo")
    o_done = sem("o_done")
    o_added = sem("o_added")
    O_CREDIT = 2
    stored = sem("stored")

    def stages(eng, stage):
        stage(0, 0, first=True)
        with eng.Fori(0, CHUNKS - 1) as c:
            for g in range(1, GROUPS):
                stage(c, g)
            stage(c + 1, 0)
        for g in range(1, GROUPS):
            stage(CHUNKS - 1, g, final=True)

    with nc.Block() as block:
        @block.sync
        def _(sp):
            with sp.Fori(0, CHUNKS - 1) as c:
                sp.wait_ge(w1_lo, c + 1)
                load(sp, w1_raw, io["w1"], c + 1, w1_loaded)
                sp.wait_ge(w2_lo, c + 1)
                load(sp, w2_raw, io["w2"], c + 1, w2_loaded)
            out_v = io["out"].rearrange("(t p) d -> p t d", p=P)
            for g in range(GROUPS):
                sp.wait_ge(o_added, 4 * (GROUPS * (CHUNKS - 1) + g + 1) + O_CREDIT)
                sp.dma_start(out_v[:, g * GT:(g + 1) * GT, :], x[:, g * GT:(g + 1) * GT, :]).then_inc(stored, 16)
            sp.wait_ge(stored, 16 * GROUPS)

        @block.gpsimd
        def _(gp):
            def stage(c, g, first=False, final=False):
                n = c * GROUPS + g
                if g == 1:
                    split_lo(gp, c, w2_raw, w2, w2_hi, w2_lo)
                for m in range(HT):
                    gp.wait_ge(h_hi, HT * n + m + 1)
                    gp.wait_ge(h_relu, HT * n + m + 1)
                    gp.tensor_tensor(hidden[g % 2][1][:, m, :], relu[m % 2][:, :], f32(hidden[g % 2][0][:, m, :]),
                                     ALU.subtract).then_inc(h_lo, 1)
                if g == GROUPS - 1 and not final:
                    split_lo(gp, c + 1, w1_raw, w1, w1_hi, w1_lo)

            stages(gp, stage)

        @block.scalar
        def _(act):
            def stage(c, g, first=False, final=False):
                n = c * GROUPS + g
                if g == 1:
                    act.wait_ge(h_done, HT * n + 1)
                    split_hi(act, c, w2_raw, w2, w2_loaded, w2_hi)
                for m in range(HT):
                    act.wait_ge(h_read, HT * n + m + 1)
                    act.activation(hidden[g % 2][0][:, m, :], masked[m % 2][:, :], ACT.Relu, bias=b1_now[:, m:m + 1])\
                        .then_inc(h_hi, 1)
                if g == GROUPS - 1 and not final:
                    split_hi(act, c + 1, w1_raw, w1, w1_loaded, w1_hi)

            stages(act, stage)

        @block.tensor
        def _(pe):
            def hide(c, n, g, first):
                rows = slice(g * GROUP, (g + 1) * GROUP)
                if g == 0:
                    pe.wait_ge(w1_lo, c + 1)
                for m in range(HT):
                    if not first or m >= 2:
                        pe.wait_ge(h_read, HT * n + m - 1)
                    cols = slice(m * P, (m + 1) * P)
                    three_pass(pe, hid_ps[m % 2][:, :], [((w1[0][:, k, cols], w1[1][:, k, cols]),
                                                          (xt_hi[:, k, rows], xt_lo[:, k, rows])) for k in range(KT)])\
                        .then_inc(h_done, 1)

            def output(c, n, g):
                if g == 0:
                    pe.wait_ge(w2_lo, c + 1)
                pe.wait_ge(h_lo, HT * n + HT)
                hi, lo = hidden[g % 2]
                for s in range(GT):
                    pe.wait_ge(o_added, GT * n + s + 1)
                    cols = slice(s * P, (s + 1) * P)
                    three_pass(pe, out_ps[s % 2][:, :], [((hi[:, m, cols], lo[:, m, cols]), (w2[0][:, m, :], w2[1][:, m, :]))
                                                         for m in range(HT)]).then_inc(o_done, 1)

            def stage(c, g, first=False, final=False):
                n = c * GROUPS + g
                hide(c, n, g, first)
                if not first:
                    output(c if g else c - 1, n - 1, (g - 1) % GROUPS)

            stages(pe, stage)
            output(CHUNKS - 1, CHUNKS * GROUPS - 1, GROUPS - 1)

        @block.vector
        def _(dve):
            dve.sem_inc(o_added, O_CREDIT)

            def add(n, g):
                for s in range(GT):
                    dve.wait_ge(o_done, GT * n + s + 1)
                    dve.tensor_tensor(x[:, g * GT + s, :], out_ps[s % 2][:, :], x[:, g * GT + s, :], ALU.add).then_inc(o_added, 1)

            def stage(c, g, first=False, final=False):
                n = c * GROUPS + g
                if g == 0:
                    if not first:
                        dve.wait_ge(h_hi, HT * n)
                    dve.tensor_copy(b1_now[:, :], b1_all[:, bass.ds(c, 1), :].rearrange("p a n -> p (a n)"))
                    dve.tensor_copy(mask_now[:, :], masks[:, bass.ds(c // CHUNKS_PER_EXPERT, 1), :].rearrange("p a n -> p (a n)"))\
                        .then_inc(now_ready, 1)
                    dve.wait_ge(now_ready, c + 1)
                for m in range(HT):
                    if not first or m >= 2:
                        dve.wait_ge(h_hi, HT * n + m - 1)
                        dve.wait_ge(h_lo, HT * n + m - 1)
                    dve.wait_ge(h_done, HT * n + m + 1)
                    dve.tensor_tensor(masked[m % 2][:, :], hid_ps[m % 2][:, :], mask_now[:, g * GROUP:(g + 1) * GROUP],
                                      ALU.mult).then_inc(h_read, 1)
                    dve.wait_ge(h_read, HT * n + m + 1)
                    dve.tensor_scalar(relu[m % 2][:, :], masked[m % 2][:, :], b1_now[:, m:m + 1], 0.0, ALU.add, ALU.max)\
                        .then_inc(h_relu, 1)
                if not first:
                    add(n - 1, (g - 1) % GROUPS)

            stages(dve, stage)
            add(CHUNKS * GROUPS - 1, GROUPS - 1)


def build(nc, io):
    with ExitStack() as ctx:
        def sem(name):
            return ctx.enter_context(nc.semaphore(name))

        def scope():
            stack = ctx.enter_context(ExitStack())

            def sb(name, shape, dt=F32):
                return stack.enter_context(nc.sbuf_tensor(name, shape, dt))

            def pb(name, shape, dt=F32):
                return stack.enter_context(nc.psum_tensor(name, shape, dt))

            return stack, sb, pb

        _, sb, pb = scope()
        x = sb("x_res", [P, TILES, D])
        ident = sb("ident", [P, P])
        const_loaded = sem("const_loaded")

        cross, csb, cpb = scope()
        cos_k, sin_k = csb("cos_k", [P, TK]), csb("sin_k", [P, TK])
        key_last, value_last = csb("key_last", [P, KT, BATCH]), csb("value_last", [P, KT, BATCH])
        ctx_raw = [csb(f"ctx_raw{i}", [P, KT, 2 * TKM]) for i in range(2)]
        ctx_loaded = [sem(f"ctx_loaded{i}") for i in range(2)]
        weights = [(csb(n + "_hi", [P, KT, D], F32R), csb(n + "_lo", [P, KT, D], F32R)) for n in ("wk", "wv", "wo")]
        with nc.Block() as block:
            @block.sync
            def _(sp):
                sp.dma_start(ident[:, :], io["ident"]).then_inc(const_loaded, 16)
                sp.dma_start(cos_k[:, :], io["cos"]).then_inc(const_loaded, 16)
                sp.dma_start(sin_k[:, :], io["sin"]).then_inc(const_loaded, 16)
        stack, asb, apb = scope()
        block_a(nc, asb, apb, sem, io, x, ident, cos_k, sin_k, key_last, value_last, weights, const_loaded,
                ctx_raw, ctx_loaded)
        stack.close()
        stack, bsb, bpb = scope()
        block_b(nc, bsb, bpb, sem, io, x, ident, cos_k, sin_k, key_last, value_last, weights, ctx_raw, ctx_loaded)
        stack.close()
        cross.close()

        _, sb, pb = scope()
        xt_hi, xt_lo = sb("x_t_hi", [P, KT, TOKENS], F32R), sb("x_t_lo", [P, KT, TOKENS], F32R)
        stack, csb, cpb = scope()
        block_c(nc, csb, cpb, sem, io, x, ident, xt_hi, xt_lo)
        stack.close()
        stack, dsb, dpb = scope()
        block_d(nc, dsb, dpb, sem, io, x, ident, xt_hi, xt_lo)
        stack.close()


def kernel(**inputs):
    import ml_dtypes
    import numpy as np
    import concourse.bacc as bacc
    from concourse.bass_utils import run_bass_kernel_spmd

    a = {n: np.asarray(v) for n, v in inputs.items()}
    half = X_HEAD // 2
    inv_freq = (1.0 / np.float32(10000.0) ** (np.arange(0, X_HEAD, 2, dtype=np.float32) / np.float32(X_HEAD))).astype(np.float32)
    angle = np.outer(np.arange(TK, dtype=np.float32), inv_freq).astype(np.float32).T
    cos, sin = np.cos(angle), np.sin(angle)
    wq, wk, wv = (a[f"L0_attn_{n}"].reshape(HEADS, 2, DH, KT, P) for n in ("Wq", "Wk", "Wv"))
    w_qk = np.concatenate([wq, wk], 1).transpose(0, 4, 3, 1, 2).reshape(HEADS, P, KT, 4 * DH)
    w_v = wv.transpose(0, 4, 3, 1, 2).reshape(HEADS, P, KT, 2 * DH)
    w_o = a["L0_attn_Wo"].reshape(D, HEADS, 2, DH).transpose(1, 3, 2, 0)
    w1 = np.concatenate([a["L0_ffn_w1"], a["L0_ffn_sw1"][None]]).reshape(EXPERTS, KT, P, CHUNKS_PER_EXPERT, HC)
    w2 = np.concatenate([a["L0_ffn_w2"], a["L0_ffn_sw2"][None]]).reshape(CHUNKS, HT, P, D)
    b1 = np.concatenate([a["L0_ffn_b1"], a["L0_ffn_sb1"][None]]).reshape(CHUNKS, HT, P)
    b2 = np.concatenate([a["L0_ffn_b2"], a["L0_ffn_sb2"][None]])
    same = np.arange(4)[:, None] == np.arange(P)[None, :] // TQ
    arrays = {
        "x": a["x"].reshape(TOKENS, D),
        "ctx_main": a["ctx_1024"][:, :TKM].reshape(BATCH * TKM, D).T,
        "ctx_last": a["ctx_1024"][:, TKM].T,
        "Wq": a["L0_xattn_Wq"].T, "Wk": a["L0_xattn_Wk"].T, "Wv": a["L0_xattn_Wv"].T, "Wo": a["L0_xattn_Wo"].T,
        "ident": np.eye(P, dtype=np.float32),
        "cos": np.tile(cos, (P // half, 1)),
        "sin": np.tile(np.concatenate([-sin, sin]), (P // X_HEAD, 1)),
        "lq1": a["L0_attn_lambda_q1"], "lk1": a["L0_attn_lambda_k1"],
        "lq2": a["L0_attn_lambda_q2"], "lk2": a["L0_attn_lambda_k2"],
        "rms": a["L0_attn_rms_scale"].reshape(2, DH).T,
        "mask_rows": same.astype(ml_dtypes.bfloat16),
        "mask_cols": np.tile(np.where(same, 0.0, MASKED), (1, D // P)).astype(ml_dtypes.bfloat16),
        "w_qk": w_qk, "w_v": w_v, "w_o": w_o,
        "gate": a["L0_ffn_gate_w"].reshape(2, KT, P).transpose(2, 1, 0),
        "w1": w1.transpose(0, 3, 2, 1, 4).reshape(CHUNKS, P, KT, HC),
        "w2": w2.transpose(0, 2, 1, 3),
        "b1": b1.transpose(2, 0, 1),
        "b2": b2,
    }
    nc = bacc.Bacc("TRN2", target_bir_lowering=False, num_devices=1)
    feeds, io = {}, {}
    for name, v in arrays.items():
        v = np.ascontiguousarray(v)
        feeds[f"in_{name}_dram"] = v
        io[name] = nc.dram_tensor(f"in_{name}_dram", v.shape, mybir.dt.from_np(v.dtype), kind="ExternalInput").ap()
    io["queries"] = nc.dram_tensor("queries_dram", (P, KT, TOKENS), F32, kind="Internal").ap()
    io["out"] = nc.dram_tensor("out_0_dram", (TOKENS, D), F32, kind="ExternalOutput").ap()
    build(nc, io)
    r = run_bass_kernel_spmd(nc, [feeds], core_ids=[0])
    return np.asarray(r.results[0]["out_0_dram"]).reshape(BATCH, TQ, D)
```

```python
from contextlib import ExitStack
import math

import concourse.bass as bass
from concourse import mybir

ALU = mybir.AluOpType
ACT = mybir.ActivationFunctionType
AX = mybir.AxisListType
F32 = mybir.dt.float32
F32R = mybir.dt.float32r
BF16 = mybir.dt.bfloat16
U32 = mybir.dt.uint32

P = 128
D = 512
KT = D // P
BATCH = 64
TQ = 32
TK = 257
TKM = TK - 1
TOKENS = BATCH * TQ
TILES = TOKENS // P
GROUP = 512
GROUPS = TOKENS // GROUP
GT = GROUP // P
PAIRS = BATCH // 2
X_HEAD = 32
X_SCALE = 1.0 / math.sqrt(X_HEAD)
HEADS = 8
DH = 128
D_SCALE = 1.0 / math.sqrt(DH)
LAMBDA_INIT = 0.8 - 0.6 * math.exp(-0.3 * 1)
EPS = 1e-5
HIDDEN = 2048
EXPERTS = 3
HC = 512
HT = HC // P
CHUNKS = EXPERTS * HIDDEN // HC
CHUNKS_PER_EXPERT = HIDDEN // HC
SLOT_GROUPS = GROUPS + 1
SLOTS = SLOT_GROUPS * GROUP
SHARED0 = 2 * CHUNKS_PER_EXPERT
SLOT_CONST_COLS = [(0, TILES), (TILES, 2 * TILES), (2 * TILES, 2 * TILES + SLOT_GROUPS),
                   (2 * TILES + SLOT_GROUPS, 2 * TILES + SLOT_GROUPS + CHUNKS_PER_EXPERT)]
SLOT_CONSTS = SLOT_CONST_COLS[-1][1]
MASKED = -(2.0 ** 100)
SHUFFLE_HALVES = [(j + X_HEAD // 2) % X_HEAD for j in range(X_HEAD)]
CONSTS = 3
BN = 6


def f32(ap):
    return ap.bitcast(F32)


def three_pass(pe, out, terms, start=True, stop=True):
    passes = [(a, b) for (a_hi, a_lo), (b_hi, b_lo) in terms for a, b in ((a_hi, b_hi), (a_hi, b_lo), (a_lo, b_hi))]
    for n, (a, b) in enumerate(passes):
        mm = pe.matmul(out, a, b, start=start and n == 0, stop=stop and n == len(passes) - 1)
    return mm


class Norm:

    CHAIN = 4

    def __init__(self, name, sb, pb, sem, x, ident):
        self.x, self.ident = x, ident
        self.stats = sb(name + "_stats", [P, GT, BN])
        self.mean_sum = sb(name + "_mean_sum", [P, GT])
        self.mean_gap = sb(name + "_mean_gap", [P, GT])
        self.means = [sb(f"{name}_mean{i}", [P, GT]) for i in range(2)]
        self.gap_sq = sb(name + "_gap_sq", [P, GT])
        self.var_sum = sb(name + "_var_sum", [P, GT])
        self.sd = sb(name + "_sd", [P, GT])
        self.rstds = [sb(f"{name}_rstd{i}", [P, GT]) for i in range(2)]
        self.eps = sb(name + "_eps", [P, 1])
        self.xn = [sb(f"{name}_xn{i}", [P, GT, D]) for i in range(2)]
        self.turned = [pb(f"{name}_turned{i}", [P, KT, P]) for i in range(2)]
        self.chain = sem(name + "_chain")
        self.eps_set = sem(name + "_eps_set")
        self.var_ready = sem(name + "_var_ready")
        self.sd_ready = sem(name + "_sd_ready")
        self.xn_ready = sem(name + "_xn_ready")
        self.turn_done = sem(name + "_turn_done")
        self.hi_ready = sem(name + "_hi_ready")
        self.lo_ready = sem(name + "_lo_ready")

    def start(self, dve):
        dve.memset(self.eps[:, :], EPS).then_inc(self.eps_set, 1)

    def vector_stats(self, dve, g):
        mean, rstd = self.means[g % 2], self.rstds[g % 2]
        for s in range(GT):
            ins = dve.bn_stats(self.stats[:, s, :], self.x[:, g * GT + s, :])
        ins.then_inc(self.chain, 1)
        dve.wait_ge(self.chain, g * self.CHAIN + 1)
        dve.tensor_tensor(self.mean_sum[:, :], self.stats[:, :, 1], self.stats[:, :, 4], ALU.add)
        dve.tensor_tensor(self.mean_gap[:, :], self.stats[:, :, 1], self.stats[:, :, 4], ALU.subtract)
        dve.tensor_tensor(self.var_sum[:, :], self.stats[:, :, 2], self.stats[:, :, 5], ALU.add).then_inc(self.chain, 1)
        dve.wait_ge(self.chain, g * self.CHAIN + 2)
        dve.tensor_scalar(mean[:, :], self.mean_sum[:, :], 0.5, None, ALU.mult)
        dve.tensor_tensor(self.gap_sq[:, :], self.mean_gap[:, :], self.mean_gap[:, :], ALU.mult).then_inc(self.chain, 1)
        dve.wait_ge(self.chain, g * self.CHAIN + 3)
        dve.scalar_tensor_tensor(self.var_sum[:, :], self.gap_sq[:, :], D / 4.0, self.var_sum[:, :], ALU.mult, ALU.add)\
            .then_inc(self.var_ready, 1)
        dve.wait_ge(self.sd_ready, g + 1)
        dve.reciprocal(rstd[:, :], self.sd[:, :]).then_inc(self.chain, 1)
        dve.wait_ge(self.chain, g * self.CHAIN + 4)
        for s in range(GT):
            ins = dve.tensor_scalar(self.xn[g % 2][:, s, :], self.x[:, g * GT + s, :],
                                    mean[:, s:s + 1], rstd[:, s:s + 1], ALU.subtract, ALU.mult)
        ins.then_inc(self.xn_ready, 1)

    def scalar_sd(self, act, g):
        act.wait_ge(self.var_ready, g + 1)
        act.activation(self.sd[:, :], self.var_sum[:, :], ACT.Sqrt, bias=self.eps[:, :], scale=1.0 / D).then_inc(self.sd_ready, 1)

    def tensor_turn(self, pe, g):
        pe.wait_ge(self.xn_ready, g + 1)
        for s in range(GT):
            if g * GT + s >= 2:
                pe.wait_ge(self.lo_ready, g * GT + s - 1)
            for k in range(KT):
                mm = pe.transpose(self.turned[s % 2][:, k, :], self.xn[g % 2][:, s, k * P:(k + 1) * P], self.ident[:, :])
            mm.then_inc(self.turn_done, 1)

    def scalar_hi(self, act, g, hi):
        for s in range(GT):
            act.wait_ge(self.turn_done, g * GT + s + 1)
            act.activation(hi(s), self.turned[s % 2][:, :, :], ACT.Copy).then_inc(self.hi_ready, 1)

    def vector_lo(self, dve, g, hi, lo):
        for s in range(GT):
            dve.wait_ge(self.hi_ready, g * GT + s + 1)
            dve.tensor_tensor(lo(s), self.turned[s % 2][:, :, :], f32(hi(s)), ALU.subtract).then_inc(self.lo_ready, 1)


def block_a(nc, sb, pb, sem, io, x, ident, cos_k, sin_k, key_last, value_last, weights, const_loaded, ctx_raw, ctx_loaded):
    names = ("Wq", "Wk", "Wv", "Wo")
    wq = (sb("wq_hi", [P, KT, D], F32R), sb("wq_lo", [P, KT, D], F32R))
    split = {"Wq": wq, "Wk": weights[0], "Wv": weights[1], "Wo": weights[2]}
    w_raw = [sb(f"w_raw{i}", [P, KT, D]) for i in range(2)]
    norm = Norm("n1", sb, pb, sem, x, ident)
    xt = [(sb(f"xt_hi{i}", [P, KT, GROUP], F32R), sb(f"xt_lo{i}", [P, KT, GROUP], F32R)) for i in range(2)]
    last_raw = sb("last_raw", [P, KT, BATCH])
    last_hi, last_lo = sb("last_hi", [P, KT, BATCH], F32R), sb("last_lo", [P, KT, BATCH], F32R)
    last_sin = sb("last_sin", [P, KT, BATCH])
    cos_part = [sb(f"cos_part{i}", [P, GROUP]) for i in range(2)]
    sin_part = [sb(f"sin_part{i}", [P, GROUP]) for i in range(2)]
    queries = sb("queries", [P, KT, GROUP])
    proj = [pb(f"proj_a{i}", [P, D]) for i in range(2)]
    last_ps = pb("last_ps", [P, 2, KT, BATCH])

    x_loaded = [sem(f"x_loaded{g}") for g in range(GROUPS)]
    w_loaded = [sem(f"w_loaded_{n}") for n in names]
    w_hi = sem("w_hi")
    w_lo = sem("w_lo")
    last_loaded = sem("last_loaded")
    last_hi_ready = sem("last_hi_ready")
    last_lo_ready = sem("last_lo_ready")
    q_done = sem("q_done")
    q_halves = sem("q_halves")
    q_sin = sem("q_sin")
    q_ready = sem("q_ready")
    last_done = sem("last_done")
    last_step = sem("last_step")
    last_ready = sem("last_ready")
    q_stored = [sem(f"q_stored{t}") for t in range(KT)]

    with nc.Block() as block:
        @block.sync
        def _(sp):
            x_v = io["x"].rearrange("(t p) d -> p t d", p=P)
            ctx_v = io["ctx_main"].rearrange("(k p) n -> p k n", p=P)

            def load_w(n):
                sp.dma_start(w_raw[n % 2][:, :, :], io[names[n]].rearrange("(k p) n -> p k n", p=P)).then_inc(w_loaded[n], 16)

            for g in range(GROUPS):
                sp.dma_start(x[:, g * GT:(g + 1) * GT, :], x_v[:, g * GT:(g + 1) * GT, :]).then_inc(x_loaded[g], 16)
                if g == 0:
                    load_w(0)
            load_w(1)
            sp.dma_start(last_raw[:, :, :], io["ctx_last"].rearrange("(k p) n -> p k n", p=P)).then_inc(last_loaded, 16)
            for r in range(2):
                sp.dma_start(ctx_raw[r][:, :, :], ctx_v[:, :, r * 2 * TKM:(r + 1) * 2 * TKM]).then_inc(ctx_loaded[r], 16)
            for g in range(GROUPS):
                if g < 2:
                    sp.wait_ge(w_lo, g + 1)
                    load_w(g + 2)
                for t in range(KT):
                    sp.wait_ge(q_ready, g * KT + t + 1)
                    sp.dma_start(io["queries"][:, t, g * GROUP:(g + 1) * GROUP], queries[:, t, :]).then_inc(q_stored[t], 16)
            for t in range(KT):
                sp.wait_ge(q_stored[t], 16 * GROUPS)

        @block.gpsimd
        def _(gp):
            def split_lo(n):
                gp.wait_ge(w_hi, n + 1)
                gp.tensor_tensor(split[names[n]][1][:, :, :], w_raw[n % 2][:, :, :], f32(split[names[n]][0][:, :, :]),
                                 ALU.subtract).then_inc(w_lo, 1)

            sin_q = sin_k[:, 0:TQ].unsqueeze(1).broadcast_to([P, GROUP // TQ, TQ])
            split_lo(0)
            gp.wait_ge(const_loaded, 16 * CONSTS)
            for g in range(GROUPS):
                for t in range(KT):
                    gp.wait_ge(q_halves, g * KT + t + 1)
                    part = sin_part[t % 2][:, :].rearrange("p (b q) -> p b q", q=TQ)
                    gp.tensor_tensor(part, part, sin_q, ALU.mult).then_inc(q_sin, 1)
                    gp.wait_ge(q_sin, g * KT + t + 1)
                    if g:
                        gp.wait_ge(q_stored[t], 16 * g)
                    gp.tensor_tensor(queries[:, t, :], cos_part[t % 2][:, :], sin_part[t % 2][:, :],
                                     ALU.add).then_inc(q_ready, 1)
                if g < 3:
                    split_lo(g + 1)
                if g == 1:
                    gp.wait_ge(last_hi_ready, 1)
                    gp.tensor_tensor(last_lo[:, :, :], last_raw[:, :, :], f32(last_hi[:, :, :]), ALU.subtract)\
                        .then_inc(last_lo_ready, 1)

        @block.scalar
        def _(act):
            def split_hi(n):
                act.wait_ge(w_loaded[n], 16)
                act.activation(split[names[n]][0][:, :, :], w_raw[n % 2][:, :, :], ACT.Copy).then_inc(w_hi, 1)

            act.wait_ge(norm.eps_set, 1)
            norm.scalar_sd(act, 0)
            split_hi(0)
            for g in range(GROUPS):
                if g + 1 < GROUPS:
                    norm.scalar_sd(act, g + 1)
                norm.scalar_hi(act, g, lambda s: xt[g % 2][0][:, :, s * P:(s + 1) * P])
                if g >= 1:
                    split_hi(g)
                if g == 1:
                    act.wait_ge(last_loaded, 16)
                    act.activation(last_hi[:, :, :], last_raw[:, :, :], ACT.Copy).then_inc(last_hi_ready, 1)

        @block.tensor
        def _(pe):
            def query(g):
                pe.wait_ge(norm.lo_ready, (g + 1) * GT)
                for t in range(KT):
                    if g * KT + t >= 2:
                        pe.wait_ge(q_halves, g * KT + t - 1)
                    cols = slice(t * P, (t + 1) * P)
                    three_pass(pe, proj[t % 2][:, :], [((wq[0][:, k, cols], wq[1][:, k, cols]),
                                                        (xt[g % 2][0][:, k, :], xt[g % 2][1][:, k, :])) for k in range(KT)])\
                        .then_inc(q_done, 1)

            pe.wait_ge(const_loaded, 16 * CONSTS)
            norm.tensor_turn(pe, 0)
            for g in range(1, GROUPS):
                norm.tensor_turn(pe, g)
                if g == 1:
                    pe.wait_ge(w_lo, 1)
                query(g - 1)
            pe.wait_ge(w_lo, 3)
            pe.wait_ge(last_lo_ready, 1)
            for i in range(2):
                for t in range(KT):
                    cols = slice(t * P, (t + 1) * P)
                    mm = three_pass(pe, last_ps[:, i, t, :], [((weights[i][0][:, k, cols], weights[i][1][:, k, cols]),
                                                               (last_hi[:, k, :], last_lo[:, k, :])) for k in range(KT)])
            mm.then_inc(last_done, 1)
            query(GROUPS - 1)

        @block.vector
        def _(dve):
            cos_q = cos_k[:, 0:TQ].unsqueeze(1).broadcast_to([P, GROUP // TQ, TQ])

            def rope(g):
                for t in range(KT):
                    n = g * KT + t
                    if n >= 2:
                        dve.wait_ge(q_ready, n - 1)
                    dve.wait_ge(q_done, n + 1)
                    dve.tensor_tensor(cos_part[t % 2][:, :].rearrange("p (b q) -> p b q", q=TQ),
                                      proj[t % 2][:, :].rearrange("p (b q) -> p b q", q=TQ), cos_q, ALU.mult)
                    dve.stream_shuffle(sin_part[t % 2][:, :], proj[t % 2][:, :], SHUFFLE_HALVES).then_inc(q_halves, 1)

            norm.start(dve)
            dve.wait_ge(x_loaded[0], 16)
            norm.vector_stats(dve, 0)
            for g in range(GROUPS):
                if g + 1 < GROUPS:
                    dve.wait_ge(x_loaded[g + 1], 16)
                    norm.vector_stats(dve, g + 1)
                norm.vector_lo(dve, g, lambda s: xt[g % 2][0][:, :, s * P:(s + 1) * P],
                               lambda s: xt[g % 2][1][:, :, s * P:(s + 1) * P])
                if g == 0:
                    dve.wait_ge(const_loaded, 16 * CONSTS)
                else:
                    rope(g - 1)
            dve.wait_ge(last_done, 1)
            dve.stream_shuffle(last_sin[:, :, :], last_ps[:, 0, :, :], SHUFFLE_HALVES).then_inc(last_step, 1)
            dve.wait_ge(last_step, 1)
            dve.tensor_scalar(last_sin[:, :, :], last_sin[:, :, :], sin_k[:, TKM:TK], None, ALU.mult).then_inc(last_step, 1)
            dve.wait_ge(last_step, 2)
            dve.scalar_tensor_tensor(key_last[:, :, :], last_ps[:, 0, :, :], cos_k[:, TKM:TK], last_sin[:, :, :],
                                     ALU.mult, ALU.add)
            dve.tensor_copy(value_last[:, :, :], last_ps[:, 1, :, :])
            rope(GROUPS - 1)


def block_b(nc, sb, pb, sem, io, x, ident, cos_k, sin_k, key_last, value_last, weights, ctx_raw, ctx_loaded):
    wk, wv, wo = weights
    ctx_hi = [sb(f"ctx_hi{i}", [P, KT, 2 * TKM], F32R) for i in range(2)]
    ctx_lo = [sb(f"ctx_lo{i}", [P, KT, 2 * TKM], F32R) for i in range(2)]
    keys = [sb(f"keys{i}", [P, KT, 2, TK]) for i in range(2)]
    values = [sb(f"values{i}", [P, 4, D]) for i in range(2)]
    q_pair = [sb(f"q_pair{i}", [P, KT, 2 * TQ]) for i in range(2)]
    q_diag = [sb(f"q_diag{i}", [P, KT, 2, P]) for i in range(2)]
    cos_part = [sb(f"cos_b{i}", [P, 2 * TKM]) for i in range(2)]
    sin_part = [sb(f"sin_b{i}", [P, 2 * TKM]) for i in range(2)]
    row_max = sb("row_max", [P, 2])
    neg_max = sb("neg_max", [P, 2])
    row_sum = sb("row_sum", [P, 2])
    row_inv = sb("row_inv", [P, 2])
    probs = sb("probs", [P, 2, TK])
    probs_t = sb("probs_t", [P, 2, TKM])
    p_last = sb("p_last", [P, KT, 2])
    p_last_t = sb("p_last_t", [P, KT, 2, TQ])
    last_part = sb("last_part", [P, KT, 2, TQ])
    heads_t = sb("heads_t", [P, KT, P])
    heads_hi, heads_lo = sb("heads_hi", [P, KT, P], F32R), sb("heads_lo", [P, KT, P], F32R)
    proj = [pb(f"proj_b{i}", [P, D]) for i in range(2)]
    scores = pb("scores_b", [P, 2, 512])
    turned = pb("turned_b", [P, 2, 512])
    heads = [pb(f"heads_b{i}", [P, 2, 2, P]) for i in range(2)]

    zeroed = sem("b_zeroed")
    last_step = sem("b_last_step")
    heads_ready = sem("b_heads_ready")
    q_loaded = [sem(f"q_loaded{i}") for i in range(2)]
    ctx_hi_ready = sem("ctx_hi_ready")
    ctx_lo_ready = sem("ctx_lo_ready")
    q_diag_ready = sem("q_diag_ready")
    proj_done = sem("proj_done")
    v_ready = sem("v_ready")
    k_read = sem("k_read")
    k_sin = sem("k_sin")
    k_ready = sem("k_ready")
    s_done = sem("s_done")
    max_ready = sem("max_ready")
    neg_max_ready = sem("neg_max_ready")
    exp_done = sem("exp_done")
    inv_ready = sem("inv_ready")
    p_last_ready = sem("p_last_ready")
    p_ready = sem("p_ready")
    t_done = sem("t_done")
    pt_ready = sem("pt_ready")
    pv_done = sem("pv_done")
    heads_read = sem("heads_read")
    heads_hi_ready = sem("heads_hi_ready")
    heads_lo_ready = sem("heads_lo_ready")
    wo_done = sem("b_wo_done")
    x_added = sem("b_x_added")
    X_CREDIT = 1

    ctx_v = io["ctx_main"].rearrange("(k p) n -> p k n", p=P)
    LOOPS = (PAIRS - 2) // 2

    def phases(eng, phase):
        with eng.Fori(0, LOOPS) as u:
            for j in range(2):
                phase(u * 2 + j, j, True, True, u)
        phase(PAIRS - 2, 0, True, False, LOOPS)
        phase(PAIRS - 1, 1, False, False, LOOPS)

    with nc.Block() as block:
        @block.sync
        def _(sp):
            def load_ctx(r, par):
                sp.dma_start(ctx_raw[par][:, :, :], ctx_v[:, :, bass.ds(r * 2 * TKM, 2 * TKM)]).then_inc(ctx_loaded[par], 16)

            def load_q(r, par):
                sp.dma_start(q_pair[par][:, :, :], io["queries"][:, :, bass.ds(r * 2 * TQ, 2 * TQ)]).then_inc(q_loaded[par], 16)

            for r in range(2):
                load_q(r, r)
            for r in range(2, 4):
                sp.wait_ge(ctx_lo_ready, 4 * (r - 1))
                load_ctx(r, r % 2)
            with sp.Fori(0, (PAIRS - 4) // 2) as u:
                for j in range(2):
                    p = u * 2 + j
                    sp.wait_ge(ctx_lo_ready, 4 * (p + 3))
                    load_ctx(p + 4, j)
                    sp.wait_ge(q_diag_ready, p + 1)
                    load_q(p + 2, j)
            for p in range(PAIRS - 4, PAIRS - 2):
                sp.wait_ge(q_diag_ready, p + 1)
                load_q(p + 2, p % 2)

        @block.gpsimd
        def _(gp):
            def split_lo(r, par):
                for k in range(KT):
                    gp.wait_ge(ctx_hi_ready, 4 * r + k + 1)
                    gp.tensor_tensor(ctx_lo[par][:, k, :], ctx_raw[par][:, k, :], f32(ctx_hi[par][:, k, :]), ALU.subtract)\
                        .then_inc(ctx_lo_ready, 1)

            def sines(r):
                for t in range(KT):
                    gp.wait_ge(k_read, 4 * r + t + 1)
                    part = sin_part[t % 2][:, :].rearrange("p (b k) -> p b k", k=TKM)
                    gp.tensor_tensor(part, part, sin_k[:, 0:TKM].unsqueeze(1).broadcast_to([P, 2, TKM]), ALU.mult)\
                        .then_inc(k_sin, 1)

            for par in range(2):
                ins = gp.memset(q_diag[par][:, :, :, :], 0.0)
            ins.then_inc(zeroed, 1)
            gp.wait_ge(ctx_lo_ready, KT)
            split_lo(1, 1)
            sines(0)

            def phase(p, par, projects, splits, u):
                if splits:
                    split_lo(p + 2, par)
                if projects:
                    sines(p + 1)

            phases(gp, phase)

        @block.scalar
        def _(act):
            def value_out(r, m, par):
                act.wait_ge(proj_done, 8 * r + m + 1)
                act.activation(values[par][:, m, :], proj[m % 2][:, :], ACT.Copy).then_inc(v_ready, 1)

            def split_hi(r, k, par, count):
                if k == 0:
                    act.wait_ge(ctx_loaded[par], 16 * count)
                act.activation(ctx_hi[par][:, k, :], ctx_raw[par][:, k, :], ACT.Copy).then_inc(ctx_hi_ready, 1)

            def exps(p, n):
                act.wait_ge(neg_max_ready, 4 * p + n + 1)
                for b in range(2):
                    ins = act.activation(probs[:, b, :], scores[:, b, 0:TK], ACT.Exp, bias=neg_max[:, b:b + 1], scale=X_SCALE,
                                         accum_out=row_sum[:, b:b + 1])
                ins.then_inc(exp_done, 1)

            def probs_out(p, n):
                act.wait_ge(t_done, 4 * p + n + 1)
                act.activation(probs_t[:, :, :], turned[:, :, 0:TKM], ACT.Copy).then_inc(pt_ready, 1)

            def heads_out(p, half, par):
                act.wait_ge(pv_done, 4 * p + 2 * half + 2)
                for a in range(4):
                    rows = slice(a * X_HEAD, (a + 1) * X_HEAD)
                    ins = act.activation(
                        heads_t[rows, 2 * half:2 * half + 2, par * 2 * TQ:(par + 1) * 2 * TQ].rearrange("p t (b q) -> p t b q", q=TQ),
                        heads[half][rows, :, :, rows], ACT.Copy)
                ins.then_inc(heads_read, 1)

            for r in range(2):
                for k in range(KT):
                    split_hi(r, k, r, 1)
            for m in range(4):
                value_out(0, m, 0)
            exps(0, 0)

            def phase(p, par, projects, splits, u):
                for n in range(4):
                    probs_out(p, n)
                    if n < 3:
                        exps(p, n + 1)
                    if projects:
                        value_out(p + 1, n, 1 - par)
                    if splits:
                        split_hi(p + 2, n, par, u + 2)
                heads_out(p, 0, par)
                heads_out(p, 1, par)
                if par:
                    act.wait_ge(heads_ready, p + 1)
                    act.activation(heads_hi[:, :, :], heads_t[:, :, :], ACT.Copy).then_inc(heads_hi_ready, 1)
                if projects:
                    exps(p + 1, 0)

            phases(act, phase)

        @block.tensor
        def _(pe):
            def project(r, m, par):
                if m == 0:
                    pe.wait_ge(ctx_lo_ready, 4 * r + 4)
                    pe.wait_ge(ctx_hi_ready, 4 * r + 4)
                if m < 2:
                    if not isinstance(r, int) or r > 0:
                        pe.wait_ge(k_read, 4 * r - 1 + m)
                elif m < 6:
                    pe.wait_ge(v_ready, 4 * r + m - 1)
                else:
                    pe.wait_ge(k_read, 4 * r + m - 5)
                hi, lo = ctx_hi[par], ctx_lo[par]
                if m < 4:
                    rows = slice(m * P, (m + 1) * P)
                    terms = [((hi[:, k, rows], lo[:, k, rows]), (wv[0][:, k, :], wv[1][:, k, :])) for k in range(KT)]
                else:
                    cols = slice((m - 4) * P, (m - 3) * P)
                    terms = [((wk[0][:, k, cols], wk[1][:, k, cols]), (hi[:, k, :], lo[:, k, :])) for k in range(KT)]
                three_pass(pe, proj[m % 2][:, :], terms).then_inc(proj_done, 1)

            def score(p, n, par):
                if n == 0:
                    pe.wait_ge(q_diag_ready, p + 1)
                pe.wait_ge(k_ready, 4 * p + n + 1)
                for b in range(2):
                    mm = pe.matmul(scores[:, b, 0:TK], q_diag[par][:, n, b, :], keys[par][:, n, b, :], start=True, stop=True)
                mm.then_inc(s_done, 1)

            def turn(p, n):
                pe.wait_ge(p_ready, 4 * p + n + 1)
                for b in range(2):
                    for c in range(2):
                        mm = pe.transpose(turned[:, b, c * P:(c + 1) * P], probs[:, b, c * P:(c + 1) * P], ident[:, :])
                mm.then_inc(t_done, 1)

            def attend(p, n, par, count):
                if n == 0 and par == 0:
                    pe.wait_ge(x_added, count - 1 + X_CREDIT)
                if n == 0:
                    pe.wait_ge(v_ready, 4 * p + 4)
                pe.wait_ge(pt_ready, 4 * p + n + 1)
                cols = slice(n * P, (n + 1) * P)
                for b in range(2):
                    out = heads[n // 2][:, n % 2, b, :]
                    for c in range(2):
                        mm = pe.matmul(out, values[par][:, 2 * b + c, cols], probs_t[:, b, c * P:(c + 1) * P],
                                       start=(c == 0), stop=(c == 1))
                mm.then_inc(pv_done, 1)

            def output(v):
                pe.wait_ge(heads_hi_ready, v + 1)
                pe.wait_ge(heads_lo_ready, v + 1)
                three_pass(pe, heads[0][:, :, :, :].rearrange("p a b q -> p (a b q)"),
                           [((heads_hi[:, k, :], heads_lo[:, k, :]), (wo[0][:, k, :], wo[1][:, k, :])) for k in range(KT)])\
                    .then_inc(wo_done, 1)

            for m in range(8):
                if m == 7:
                    score(0, 0, 0)
                project(0, m, 0)

            def phase(p, par, projects, splits, u):
                for slot in range(8):
                    if 1 <= slot <= 4:
                        attend(p, slot - 1, par, u + 1)
                    if slot <= 3:
                        turn(p, slot)
                    if slot <= 2:
                        score(p, slot + 1, par)
                    if slot == 7 and projects:
                        score(p + 1, 0, 1 - par)
                    if projects:
                        project(p + 1, slot, 1 - par)
                if par:
                    output(u)

            phases(pe, phase)

        @block.vector
        def _(dve):
            for k in range(KT):
                dve.wait_ge(ctx_hi_ready, k + 1)
                dve.tensor_tensor(ctx_lo[0][:, k, :], ctx_raw[0][:, k, :], f32(ctx_hi[0][:, k, :]), ALU.subtract)\
                    .then_inc(ctx_lo_ready, 1)

            def key_sum(r, t, par):
                dve.wait_ge(k_sin, 4 * r + t + 1)
                dve.tensor_tensor(keys[par][:, t, :, 0:TKM], cos_part[t % 2][:, :].rearrange("p (b k) -> p b k", k=TKM),
                                  sin_part[t % 2][:, :].rearrange("p (b k) -> p b k", k=TKM), ALU.add).then_inc(k_ready, 1)

            def key_tile(r, t, par):
                if not isinstance(r, int) or r > 0 or t >= 2:
                    dve.wait_ge(k_ready, 4 * r + t - 1)
                dve.wait_ge(proj_done, 8 * r + t + 5)
                dve.tensor_tensor(cos_part[t % 2][:, :].rearrange("p (b k) -> p b k", k=TKM),
                                  proj[t % 2][:, :].rearrange("p (b k) -> p b k", k=TKM),
                                  cos_k[:, 0:TKM].unsqueeze(1).broadcast_to([P, 2, TKM]), ALU.mult)
                dve.stream_shuffle(sin_part[t % 2][:, :], proj[t % 2][:, :], SHUFFLE_HALVES).then_inc(k_read, 1)
                if t == 0:
                    dve.tensor_copy(keys[par][:, :, :, TKM], key_last[:, :, bass.ds(r * 2, 2)])
                else:
                    key_sum(r, t - 1, par)

            def diagonal(par, count):
                dve.wait_ge(q_loaded[par], 16 * count)
                for a in range(4):
                    rows = slice(a * X_HEAD, (a + 1) * X_HEAD)
                    ins = dve.tensor_copy(q_diag[par][rows, :, :, rows],
                                          q_pair[par][rows, :, :].rearrange("p t (b q) -> p t b q", q=TQ))
                ins.then_inc(q_diag_ready, 1)

            def softmax(p, n):
                q = 4 * p + n
                dve.wait_ge(s_done, q + 1)
                dve.tensor_reduce(row_max[:, :], scores[:, :, 0:TK], AX.X, ALU.max).then_inc(max_ready, 1)
                dve.wait_ge(max_ready, q + 1)
                dve.tensor_scalar(neg_max[:, :], row_max[:, :], -X_SCALE, None, ALU.mult).then_inc(neg_max_ready, 1)
                dve.wait_ge(exp_done, q + 1)
                dve.reciprocal(row_inv[:, :], row_sum[:, :]).then_inc(inv_ready, 1)
                dve.wait_ge(inv_ready, q + 1)
                for b in range(2):
                    ins = dve.tensor_scalar(probs[:, b, 0:TKM], probs[:, b, 0:TKM], row_inv[:, b:b + 1], None, ALU.mult)
                ins.then_inc(p_ready, 1)
                dve.tensor_tensor(p_last[:, n, :], probs[:, :, TKM], row_inv[:, :], ALU.mult).then_inc(p_last_ready, 1)

            def last_rows(p):
                dve.wait_ge(p_last_ready, 4 * p + 4)
                dve.transpose(p_last_t[:, :, :, :].rearrange("p t b q -> p (t b) q"),
                              p_last[:, :, :].rearrange("p t b -> p (t b)").unsqueeze(2).broadcast_to([P, 2 * KT, TQ]))\
                    .then_inc(last_step, 1)
                dve.wait_ge(last_step, 2 * p + 1)
                dve.tensor_tensor(last_part[:, :, :, :], p_last_t[:, :, :, :],
                                  value_last[:, :, bass.ds(p * 2, 2)].unsqueeze(3).broadcast_to([P, KT, 2, TQ]), ALU.mult)\
                    .then_inc(last_step, 1)

            def add_last(p, par):
                dve.wait_ge(heads_read, 2 * p + 2)
                dve.wait_ge(last_step, 2 * p + 2)
                own = heads_t[:, :, par * 2 * TQ:(par + 1) * 2 * TQ]
                dve.tensor_tensor(own, own, last_part[:, :, :, :].rearrange("p t b q -> p t (b q)"), ALU.add)\
                    .then_inc(heads_ready, 1)

            dve.wait_ge(zeroed, 1)
            diagonal(0, 1)
            dve.sem_inc(x_added, X_CREDIT)
            for t in range(3):
                key_tile(0, t, 0)
            softmax(0, 0)
            key_tile(0, 3, 0)
            key_sum(0, 3, 0)

            def phase(p, par, projects, splits, u):
                for n in range(1, 4):
                    softmax(p, n)
                last_rows(p)
                if projects:
                    diagonal(1 - par, u + 1 + par)
                    for t in range(3):
                        key_tile(p + 1, t, 1 - par)
                        if t == 1:
                            add_last(p, par)
                else:
                    add_last(p, par)
                if par:
                    dve.wait_ge(heads_hi_ready, u + 1)
                    dve.tensor_tensor(heads_lo[:, :, :], heads_t[:, :, :], f32(heads_hi[:, :, :]), ALU.subtract)\
                        .then_inc(heads_lo_ready, 1)
                if projects:
                    softmax(p + 1, 0)
                    key_tile(p + 1, 3, 1 - par)
                    key_sum(p + 1, 3, 1 - par)
                if par:
                    dve.wait_ge(wo_done, u + 1)
                    row = x[:, bass.ds(u, 1), :].rearrange("p a d -> p (a d)")
                    dve.tensor_tensor(row, heads[0][:, :, :, :].rearrange("p a b q -> p (a b q)"), row, ALU.add)\
                        .then_inc(x_added, 1)

            phases(dve, phase)


def block_c(nc, sb, pb, sem, io, x, ident, xt_hi, xt_lo):
    w_qk_raw, w_v_raw, w_o_raw = sb("w_qk_raw", [P, KT, 4 * DH]), sb("w_v_raw", [P, KT, 2 * DH]), sb("w_o_raw", [P, 2, D])
    w_qk = (sb("w_qk_hi", [P, KT, 4 * DH], F32R), sb("w_qk_lo", [P, KT, 4 * DH], F32R))
    w_v = (sb("w_v_hi", [P, KT, 2 * DH], F32R), sb("w_v_lo", [P, KT, 2 * DH], F32R))
    w_o = (sb("w_o_hi", [P, 2, D], F32R), sb("w_o_lo", [P, 2, D], F32R))
    rms_scale = sb("rms_scale", [P, 2])
    out_scale = sb("out_scale", [P, 2])
    mask_rows = sb("mask_rows", [4, P], BF16)
    mask_cols = sb("mask_cols", [4, D], BF16)
    neg_half = sb("neg_half", [P, GT])
    lam = sb("lam", [P, 2, HEADS])
    neg_lam = sb("neg_lam", [P, HEADS])
    neg_lam_now = sb("neg_lam_now", [P, 1])

    const_c = sem("const_c")
    lam_step = sem("lam_step")
    lam_exp = sem("lam_exp")

    raw_loaded = {n: sem(f"c_{n}_loaded") for n in ("qk", "v", "o")}
    w_hi = {n: sem(f"c_{n}_hi") for n in ("qk", "v", "o")}
    w_lo = {n: sem(f"c_{n}_lo") for n in ("qk", "v", "o")}

    def load(sp, name, raw, h):
        sp.dma_start(raw[:, :, :], io["w_" + name][bass.ds(h, 1), :, :, :].rearrange("h p k n -> (h p) k n"))\
            .then_inc(raw_loaded[name], 16)

    def split_hi(act, name, raw, w, h):
        act.wait_ge(raw_loaded[name], 16 * h + 16)
        act.activation(w[0][:, :, :], raw[:, :, :], ACT.Copy).then_inc(w_hi[name], 1)

    def split_lo(gp, name, raw, w, h):
        gp.wait_ge(w_hi[name], h + 1)
        gp.tensor_tensor(w[1][:, :, :], raw[:, :, :], f32(w[0][:, :, :]), ALU.subtract).then_inc(w_lo[name], 1)

    with ExitStack() as part:
        def psb(name, shape, dt=F32):
            return part.enter_context(nc.sbuf_tensor(name, shape, dt))

        def ppb(name, shape, dt=F32):
            return part.enter_context(nc.psum_tensor(name, shape, dt))

        norm = Norm("n2", psb, ppb, sem, x, ident)
        lam_in = [psb(f"lam_in{i}", [P, HEADS, DH]) for i in range(2)]
        lam_prod = [psb(f"lam_prod{i}", [P, HEADS, DH]) for i in range(2)]
        lam_k = [psb(f"lam_k{i}", [P, HEADS, DH]) for i in range(2)]
        with nc.Block() as block:
            @block.sync
            def _(sp):
                load(sp, "qk", w_qk_raw, 0)
                load(sp, "v", w_v_raw, 0)
                load(sp, "o", w_o_raw, 0)
                for i, (a, b) in enumerate((("lq1", "lk1"), ("lq2", "lk2"))):
                    sp.dma_start(lam_in[i][:, :, :], io[a].partition_broadcast(P)).then_inc(const_c, 16)
                    sp.dma_start(lam_k[i][:, :, :], io[b].partition_broadcast(P)).then_inc(const_c, 16)
                sp.dma_start(rms_scale[:, :], io["rms"]).then_inc(const_c, 16)
                sp.dma_start(mask_rows[:, :], io["mask_rows"]).then_inc(const_c, 16)
                sp.dma_start(mask_cols[:, :], io["mask_cols"]).then_inc(const_c, 16)

            @block.scalar
            def _(act):
                act.wait_ge(norm.eps_set, 1)
                norm.scalar_sd(act, 0)
                for g in range(GROUPS):
                    if g + 1 < GROUPS:
                        norm.scalar_sd(act, g + 1)
                    norm.scalar_hi(act, g, lambda s: xt_hi[:, :, g * GROUP + s * P:g * GROUP + (s + 1) * P])
                    if g == 0:
                        split_hi(act, "qk", w_qk_raw, w_qk, 0)
                    if g == 1:
                        split_hi(act, "v", w_v_raw, w_v, 0)
                act.wait_ge(lam_step, 2)
                act.activation(lam[:, :, :], lam[:, :, :], ACT.Exp).then_inc(lam_exp, 1)

            @block.gpsimd
            def _(gp):
                split_lo(gp, "qk", w_qk_raw, w_qk, 0)
                split_lo(gp, "v", w_v_raw, w_v, 0)

            @block.tensor
            def _(pe):
                for g in range(GROUPS):
                    norm.tensor_turn(pe, g)

            @block.vector
            def _(dve):
                norm.start(dve)
                dve.memset(neg_half[:, :], -0.5)
                norm.vector_stats(dve, 0)
                for g in range(GROUPS):
                    if g + 1 < GROUPS:
                        norm.vector_stats(dve, g + 1)
                    norm.vector_lo(dve, g, lambda s: xt_hi[:, :, g * GROUP + s * P:g * GROUP + (s + 1) * P],
                                   lambda s: xt_lo[:, :, g * GROUP + s * P:g * GROUP + (s + 1) * P])
                dve.wait_ge(const_c, 16 * 7)
                for i in range(2):
                    ins = dve.tensor_tensor(lam_prod[i][:, :, :], lam_in[i][:, :, :], lam_k[i][:, :, :], ALU.mult)
                ins.then_inc(lam_step, 1)
                dve.wait_ge(lam_step, 1)
                dve.tensor_scalar(out_scale[:, :], rms_scale[:, :], 1.0 - LAMBDA_INIT, None, ALU.mult)
                for i in range(2):
                    ins = dve.tensor_reduce(lam[:, i, :], lam_prod[i][:, :, :], AX.X, ALU.add)
                ins.then_inc(lam_step, 1)
                dve.wait_ge(lam_exp, 1)
                dve.scalar_tensor_tensor(neg_lam[:, :], lam[:, 1, :], -LAMBDA_INIT, lam[:, 0, :], ALU.add, ALU.subtract)\
                    .then_inc(lam_step, 1)

    qk = sb("qk", [P, 4, GROUP])
    v = sb("v_c", [P, GT, 2 * DH])
    row_max = sb("c_row_max", [P, 2, GT])
    neg_max = sb("c_neg_max", [P, 2, GT])
    row_sum = sb("c_row_sum", [P, 2, GT])
    coef = sb("c_coef", [P, 2, GT])
    probs = sb("c_probs", [P, 2, GT, P])
    probs_t = sb("c_probs_t", [P, GT, P])
    sum_sq = sb("c_sum_sq", [P, GT])
    mean_sq = sb("c_mean_sq", [P, GT])
    rms_inv = sb("c_rms_inv", [P, GT])
    normed = sb("c_normed", [P, GT, 2 * DH])
    out_t = (sb("out_t_hi", [P, 2, GROUP], F32R), sb("out_t_lo", [P, 2, GROUP], F32R))
    proj = [pb(f"proj_c{i}", [P, D]) for i in range(2)]
    scores = pb("scores_c", [P, 2, GT, P])
    turned = [pb(f"turned_c{i}", [P, GT, P]) for i in range(2)]
    heads = pb("heads_c", [P, GT, 2 * DH])

    proj_done = sem("c_proj_done")
    proj_read = sem("c_proj_read")
    s_done = sem("c_s_done")
    max_ready = sem("c_max_ready")
    neg_max_ready = sem("c_neg_max_ready")
    exp_done = sem("c_exp_done")
    coef_step = sem("c_coef_step")
    p_ready = sem("c_p_ready")
    t_done = sem("c_t_done")
    pt_ready = sem("c_pt_ready")
    pv_done = sem("c_pv_done")
    sq_done = sem("c_sq_done")
    mean_sq_ready = sem("c_mean_sq_ready")
    rms_ready = sem("c_rms_ready")
    normed_ready = sem("c_normed_ready")
    turn_done = sem("c_turn_done")
    out_hi_ready = sem("c_out_hi")
    out_lo_ready = sem("c_out_lo")
    wo_done = sem("c_wo_done")
    x_added = sem("c_x_added")
    ADD_CREDIT = 8
    QK_TILE = [(0, 0), (1, 1), (2, 2), (3, 3)]

    def stages(eng, stage):
        stage(0, 0, first=True)
        with eng.Fori(0, HEADS - 1) as h:
            for g in range(1, GROUPS):
                stage(h, g)
            stage(h + 1, 0)
        for g in range(1, GROUPS):
            stage(HEADS - 1, g, final=True)

    with nc.Block() as block:
        @block.sync
        def _(sp):
            with sp.Fori(0, HEADS - 1) as h:
                sp.wait_ge(w_lo["qk"], h + 1)
                sp.wait_ge(w_hi["qk"], h + 1)
                load(sp, "qk", w_qk_raw, h + 1)
                sp.wait_ge(w_lo["v"], h + 1)
                load(sp, "v", w_v_raw, h + 1)
                sp.wait_ge(w_lo["o"], h + 1)
                load(sp, "o", w_o_raw, h + 1)

        @block.gpsimd
        def _(gp):
            def rms(n):
                gp.wait_ge(mean_sq_ready, n + 1)
                gp.tensor_tensor(rms_inv[:, :], mean_sq[:, :], neg_half[:, :], ALU.pow).then_inc(rms_ready, 1)

            def stage(h, g, first=False, final=False):
                n = h * GROUPS + g
                if not first:
                    rms(n - 1)
                if g == GROUPS - 1 and not final:
                    split_lo(gp, "qk", w_qk_raw, w_qk, h + 1)
                    split_lo(gp, "v", w_v_raw, w_v, h + 1)

            stages(gp, stage)
            rms(HEADS * GROUPS - 1)

        @block.scalar
        def _(act):
            def split_o(h):
                act.wait_ge(raw_loaded["o"], 16 * h + 16)
                for f in range(2):
                    ins = act.activation(w_o[0][:, f, :], w_o_raw[:, f, :], ACT.Copy, scale=out_scale[:, f:f + 1])
                ins.then_inc(w_hi["o"], 1)

            def proj_out(n, m):
                act.wait_ge(proj_done, 6 * n + m + 1)
                if m < 4:
                    dst = qk[:, m, :]
                else:
                    dst = v[:, 2 * (m - 4):2 * (m - 4) + 2, :].rearrange("p a d -> p (a d)")
                act.activation(dst, proj[m % 2][:, :], ACT.Copy).then_inc(proj_read, 1)

            def probs_out(n):
                act.wait_ge(t_done, n + 1)
                act.activation(probs_t[:, :, :], turned[0][:, :, :], ACT.Copy).then_inc(pt_ready, 1)

            def squares(n):
                act.wait_ge(pv_done, n + 1)
                for s in range(GT):
                    ins = act.activation(normed[:, s, :], heads[:, s, :], ACT.Square, accum_out=sum_sq[:, s:s + 1])
                ins.then_inc(sq_done, 1)

            def out_hi(n):
                act.wait_ge(turn_done, n + 1)
                for f in range(2):
                    ins = act.activation(out_t[0][:, f, :], turned[f][:, :, :].rearrange("p a q -> p (a q)"), ACT.Copy)
                ins.then_inc(out_hi_ready, 1)

            def exps(n, half):
                if half == 0:
                    act.wait_ge(neg_max_ready, n + 1)
                for s in range(GT):
                    ins = act.activation(probs[:, half, s, :], scores[:, half, s, :], ACT.Exp, bias=neg_max[:, half, s:s + 1],
                                         scale=D_SCALE, accum_out=row_sum[:, half, s:s + 1])
                if half == 1:
                    ins.then_inc(exp_done, 1)

            def stage(h, g, first=False, final=False):
                n = h * GROUPS + g
                proj_out(n, 0)
                proj_out(n, 1)
                if g == 1:
                    split_o(h)
                if not first:
                    probs_out(n - 1)
                proj_out(n, 2)
                if not first:
                    squares(n - 1)
                proj_out(n, 3)
                if g == GROUPS - 1 and not final:
                    split_hi(act, "qk", w_qk_raw, w_qk, h + 1)
                proj_out(n, 4)
                if not first:
                    out_hi(n - 1)
                exps(n, 0)
                proj_out(n, 5)
                exps(n, 1)
                if g == GROUPS - 1 and not final:
                    split_hi(act, "v", w_v_raw, w_v, h + 1)

            stages(act, stage)
            last = HEADS * GROUPS - 1
            probs_out(last)
            squares(last)
            out_hi(last)

        @block.tensor
        def _(pe):
            def project(n, h, g, m, first):
                if m < 2:
                    if not first:
                        pe.wait_ge(proj_read, 6 * n - 1 + m)
                        pe.wait_ge(x_added, 4 * n - 5 + m + ADD_CREDIT)
                else:
                    pe.wait_ge(proj_read, 6 * n + m - 1)
                rows = slice(g * GROUP, (g + 1) * GROUP)
                if m < 4:
                    if m == 0 and g == 0:
                        pe.wait_ge(w_lo["qk"], h + 1)
                    cols = slice(m * P, (m + 1) * P)
                    three_pass(pe, proj[m % 2][:, :], [((w_qk[0][:, k, cols], w_qk[1][:, k, cols]),
                                                        (xt_hi[:, k, rows], xt_lo[:, k, rows])) for k in range(KT)])\
                        .then_inc(proj_done, 1)
                else:
                    if m == 4 and g == 0:
                        pe.wait_ge(w_lo["v"], h + 1)
                    for s in (2 * (m - 4), 2 * (m - 4) + 1):
                        rows = slice((g * GT + s) * P, (g * GT + s + 1) * P)
                        mm = three_pass(pe, proj[m % 2][:, (s % 2) * 2 * DH:(s % 2 + 1) * 2 * DH],
                                        [((xt_hi[:, k, rows], xt_lo[:, k, rows]), (w_v[0][:, k, :], w_v[1][:, k, :]))
                                         for k in range(KT)])
                    mm.then_inc(proj_done, 1)

            def score(n):
                pe.wait_ge(proj_read, 6 * n + 4)
                for half in range(2):
                    pe.matmul(scores[:, half, :, :].rearrange("p a q -> p (a q)"), mask_rows[:, :], mask_cols[:, :],
                              start=True, stop=False, skip_group_check=True)
                    for s in range(GT):
                        cols = slice(s * P, (s + 1) * P)
                        mm = pe.matmul(scores[:, half, s, :], qk[:, half, cols], qk[:, 2 + half, cols],
                                       start=False, stop=(s == GT - 1), skip_group_check=True)
                mm.then_inc(s_done, 1)

            def turn(n):
                pe.wait_ge(p_ready, n + 1)
                for s in range(GT):
                    mm = pe.transpose(turned[0][:, s, :], probs[:, 0, s, :], ident[:, :])
                mm.then_inc(t_done, 1)

            def attend(n):
                pe.wait_ge(pt_ready, n + 1)
                pe.wait_ge(proj_read, 6 * n + 6)
                for s in range(GT):
                    mm = pe.matmul(heads[:, s, :], probs_t[:, s, :], v[:, s, :], start=True, stop=True)
                mm.then_inc(pv_done, 1)

            def turn_out(n):
                pe.wait_ge(normed_ready, n + 1)
                for f in range(2):
                    for s in range(GT):
                        mm = pe.transpose(turned[f][:, s, :], normed[:, s, f * P:(f + 1) * P], ident[:, :])
                mm.then_inc(turn_done, 1)

            def output(n, h, now):
                pe.wait_ge(w_lo["o"], h + 1)
                pe.wait_ge(out_lo_ready, n + 1)
                for s in range(GT):
                    if s < 2:
                        pe.wait_ge(proj_read, 6 * now + 5 + s)
                    else:
                        pe.wait_ge(x_added, 4 * n + s - 1 + ADD_CREDIT)
                    cols = slice(s * P, (s + 1) * P)
                    three_pass(pe, proj[s % 2][:, :], [((out_t[0][:, f, cols], out_t[1][:, f, cols]),
                                                        (w_o[0][:, f, :], w_o[1][:, f, :])) for f in range(2)])\
                        .then_inc(wo_done, 1)

            def stage(h, g, first=False, final=False):
                n = h * GROUPS + g
                prev = n - 1
                prev_head = h if g else h - 1
                project(n, h, g, 0, first)
                project(n, h, g, 1, first)
                if not first:
                    turn(prev)
                project(n, h, g, 2, first)
                if not first:
                    attend(prev)
                project(n, h, g, 3, first)
                project(n, h, g, 4, first)
                score(n)
                if not first:
                    turn_out(prev)
                project(n, h, g, 5, first)
                if not first:
                    output(prev, prev_head, n)

            stages(pe, stage)
            last = HEADS * GROUPS - 1
            turn(last)
            attend(last)
            turn_out(last)
            output(last, HEADS - 1, last)

        @block.vector
        def _(dve):
            dve.sem_inc(x_added, ADD_CREDIT)

            def split_o(h):
                dve.wait_ge(w_hi["o"], h + 1)
                for f in range(2):
                    ins = dve.scalar_tensor_tensor(w_o[1][:, f, :], w_o_raw[:, f, :], out_scale[:, f:f + 1],
                                                   f32(w_o[0][:, f, :]), ALU.mult, ALU.subtract)
                ins.then_inc(w_lo["o"], 1)

            def mean_squares(n):
                dve.wait_ge(sq_done, n + 1)
                dve.tensor_scalar(mean_sq[:, :], sum_sq[:, :], 1.0 / (2 * DH), EPS, ALU.mult, ALU.add).then_inc(mean_sq_ready, 1)

            def normalise(n):
                dve.wait_ge(rms_ready, n + 1)
                for s in range(GT):
                    ins = dve.tensor_scalar(normed[:, s, :], heads[:, s, :], rms_inv[:, s:s + 1], None, ALU.mult)
                ins.then_inc(normed_ready, 1)

            def maxima(n):
                dve.wait_ge(s_done, n + 1)
                dve.tensor_reduce(row_max[:, :, :], scores[:, :, :, :], AX.X, ALU.max).then_inc(max_ready, 1)
                dve.wait_ge(max_ready, n + 1)
                dve.tensor_scalar(neg_max[:, :, :], row_max[:, :, :], -D_SCALE, None, ALU.mult).then_inc(neg_max_ready, 1)

            def out_lo(n):
                dve.wait_ge(out_hi_ready, n + 1)
                for f in range(2):
                    ins = dve.tensor_tensor(out_t[1][:, f, :], turned[f][:, :, :].rearrange("p a q -> p (a q)"),
                                            f32(out_t[0][:, f, :]), ALU.subtract)
                ins.then_inc(out_lo_ready, 1)

            def combine(n):
                dve.wait_ge(exp_done, n + 1)
                dve.reciprocal(coef[:, :, :], row_sum[:, :, :]).then_inc(coef_step, 1)
                dve.wait_ge(coef_step, 3 * n + 1)
                dve.tensor_scalar(coef[:, 1, :], coef[:, 1, :], neg_lam_now[:, :], None, ALU.mult).then_inc(coef_step, 1)
                dve.wait_ge(coef_step, 3 * n + 2)
                for s in range(GT):
                    ins = dve.tensor_scalar(probs[:, 1, s, :], probs[:, 1, s, :], coef[:, 1, s:s + 1], None, ALU.mult)
                ins.then_inc(coef_step, 1)
                dve.wait_ge(coef_step, 3 * n + 3)
                for s in range(GT):
                    ins = dve.scalar_tensor_tensor(probs[:, 0, s, :], probs[:, 0, s, :], coef[:, 0, s:s + 1],
                                                   probs[:, 1, s, :], ALU.mult, ALU.add)
                ins.then_inc(p_ready, 1)

            def add(n, g):
                for s in range(GT):
                    dve.wait_ge(wo_done, 4 * n + s + 1)
                    dve.tensor_tensor(x[:, g * GT + s, :], proj[s % 2][:, :], x[:, g * GT + s, :], ALU.add).then_inc(x_added, 1)

            def stage(h, g, first=False, final=False):
                n = h * GROUPS + g
                if g == 1:
                    split_o(h)
                if not first:
                    mean_squares(n - 1)
                    normalise(n - 1)
                maxima(n)
                if not first:
                    out_lo(n - 1)
                if g == 0:
                    dve.tensor_copy(neg_lam_now[:, :], neg_lam[:, bass.ds(h, 1)])
                if not first:
                    add(n - 1, (g - 1) % GROUPS)
                combine(n)

            stages(dve, stage)
            last = HEADS * GROUPS - 1
            mean_squares(last)
            normalise(last)
            out_lo(last)
            add(last, GROUPS - 1)


class Weights:

    def __init__(self, sb, sem, name):
        self.raw = sb(name + "_raw", [P, HT, D])
        self.hi, self.lo = sb(name + "_hi", [P, HT, D], F32R), sb(name + "_lo", [P, HT, D], F32R)
        self.loaded = sem(name + "_loaded")
        self.gathered = sem(name + "_gathered")
        self.hi_ready = sem(name + "_hi_ready")
        self.lo_ready = sem(name + "_lo_ready")

    def load(self, sp, src, chunk):
        sp.dma_start(self.raw[:, :, :], src[bass.ds(chunk, 1), :, :, :].rearrange("c p k n -> (c p) k n")).then_inc(self.loaded, 16)

    def gather(self, gp, src, index):
        gp.indirect_dma_start(self.raw[:, :, :].rearrange("p k n -> p (k n)"), None, src.rearrange("c p k n -> (c p) (k n)"),
                              bass.IndirectOffsetOnAxis(index, 0)).then_inc(self.gathered, 16)

    def split_hi(self, act, k, shared=True):
        if not shared:
            act.wait_ge(self.gathered, 16 * k)
        elif isinstance(k, int) and k == 0:
            act.wait_ge(self.loaded, 16)
        else:
            act.wait_ge(self.loaded, 16 * (k - SLOT_GROUPS * CHUNKS_PER_EXPERT + 1))
        act.activation(self.hi[:, :, :], self.raw[:, :, :], ACT.Copy).then_inc(self.hi_ready, 1)

    def split_lo(self, eng, k):
        eng.wait_ge(self.hi_ready, k + 1)
        eng.tensor_tensor(self.lo[:, :, :], self.raw[:, :, :], f32(self.hi[:, :, :]), ALU.subtract).then_inc(self.lo_ready, 1)


class Hidden:

    def __init__(self, name, sb, pb, sem):
        self.split = [(sb(f"{name}_hidden_hi{i}", [P, HT, GROUP], F32R), sb(f"{name}_hidden_lo{i}", [P, HT, GROUP], F32R))
                      for i in range(2)]
        self.relu = [sb(f"{name}_relu{i}", [P, GROUP]) for i in range(2)]
        self.ps = [pb(f"{name}_hid_ps{i}", [P, GROUP]) for i in range(2)]
        self.done = sem(name + "_h_done")
        self.relu_ready = sem(name + "_h_relu")
        self.hi_ready = sem(name + "_h_hi")
        self.lo_ready = sem(name + "_h_lo")

    def product(self, pe, n, m, w1, xt, first):
        if not first or m >= 2:
            pe.wait_ge(self.relu_ready, HT * n + m - 1)
        cols = slice(m * P, (m + 1) * P)
        three_pass(pe, self.ps[m % 2][:, :], [((w1.hi[:, k, cols], w1.lo[:, k, cols]), xt(k)) for k in range(KT)])\
            .then_inc(self.done, 1)

    def vector_relu(self, dve, n, m, bias, first):
        if not first or m >= 2:
            dve.wait_ge(self.lo_ready, HT * n + m - 1)
        dve.wait_ge(self.done, HT * n + m + 1)
        dve.tensor_scalar(self.relu[m % 2][:, :], self.ps[m % 2][:, :], bias[:, m:m + 1], 0.0, ALU.add, ALU.max)\
            .then_inc(self.relu_ready, 1)

    def scalar_hi(self, act, n, m, i):
        act.wait_ge(self.relu_ready, HT * n + m + 1)
        act.activation(self.split[i][0][:, m, :], self.relu[m % 2][:, :], ACT.Copy).then_inc(self.hi_ready, 1)

    def pool_lo(self, gp, n, m, i):
        gp.wait_ge(self.hi_ready, HT * n + m + 1)
        gp.tensor_tensor(self.split[i][1][:, m, :], self.relu[m % 2][:, :], f32(self.split[i][0][:, m, :]), ALU.subtract)\
            .then_inc(self.lo_ready, 1)

    def terms(self, i, s, w2):
        cols = slice(s * P, (s + 1) * P)
        hi, lo = self.split[i]
        return [((hi[:, m, cols], lo[:, m, cols]), (w2.hi[:, m, :], w2.lo[:, m, :])) for m in range(HT)]


def rotated(eng, outer, inner, stage):
    stage(0, 0, first=True)
    if outer > 1:
        with eng.Fori(0, outer - 1) as a:
            for b in range(1, inner):
                stage(a, b)
            stage(a + 1, 0)
    for b in range(1, inner):
        stage(outer - 1, b, final=True)


def shared_ffn(nc, sb, pb, sem, name, x, xt_hi, xt_lo, b1_all, weights, io, k0, chunk0, chunks, extra):
    w1, w2 = weights
    hid = Hidden(name, sb, pb, sem)
    b1_now = sb(name + "_b1_now", [P, HT])
    out_ps = [pb(f"{name}_out_ps{i}", [P, D]) for i in range(2)]
    now_ready = sem(name + "_now_ready")
    o_done = sem(name + "_o_done")
    o_added = sem(name + "_o_added")
    O_CREDIT = 2
    last = k0 > 0

    def beside(engine, eng, point, plain=True):
        if plain and engine in extra:
            extra[engine](eng, point, o_added, O_CREDIT)

    with nc.Block() as block:
        @block.sync
        def _(sp):
            beside("sync", sp, "start")
            if chunks > 1:
                with sp.Fori(0, chunks - 1) as c:
                    sp.wait_ge(w1.lo_ready, c + k0 + 1)
                    w1.load(sp, io["w1"], c + chunk0 + 1)
                    sp.wait_ge(w2.lo_ready, c + k0 + 1)
                    w2.load(sp, io["w2"], c + chunk0 + 1)
            beside("sync", sp, "end")

        @block.gpsimd
        def _(gp):
            def stage(c, g, first=False, final=False):
                for m in range(HT):
                    hid.pool_lo(gp, c * GROUPS + g, m, g % 2)
                beside("gpsimd", gp, g, first or final)

            beside("gpsimd", gp, "start")
            rotated(gp, chunks, GROUPS, stage)
            beside("gpsimd", gp, "end")

        @block.scalar
        def _(act):
            def stage(c, g, first=False, final=False):
                n = c * GROUPS + g
                for m in range(HT):
                    hid.scalar_hi(act, n, m, g % 2)
                    if g == 1 and m == 0:
                        w2.split_hi(act, c + k0 if k0 else 0)
                if g == GROUPS - 1 and not (final and last):
                    w1.split_hi(act, c + k0 + 1, shared=k0 > 0)
                beside("scalar", act, g, first or final)

            beside("scalar", act, "start")
            rotated(act, chunks, GROUPS, stage)
            beside("scalar", act, "end")

        @block.tensor
        def _(pe):
            def output(c, n, g):
                if g == 0:
                    pe.wait_ge(w2.lo_ready, c + k0 + 1)
                pe.wait_ge(hid.lo_ready, HT * n + HT)
                for s in range(GT):
                    pe.wait_ge(o_added, GT * n + s + 1)
                    three_pass(pe, out_ps[s % 2][:, :], hid.terms(g % 2, s, w2)).then_inc(o_done, 1)

            def stage(c, g, first=False, final=False):
                n = c * GROUPS + g
                if g == 0:
                    pe.wait_ge(w1.lo_ready, c + k0 + 1)
                rows = slice(g * GROUP, (g + 1) * GROUP)
                for m in range(HT):
                    hid.product(pe, n, m, w1, lambda k: (xt_hi[:, k, rows], xt_lo[:, k, rows]), first)
                beside("tensor", pe, g, first or final)
                if not first:
                    output(c if g else c - 1, n - 1, (g - 1) % GROUPS)

            rotated(pe, chunks, GROUPS, stage)
            output(chunks - 1, chunks * GROUPS - 1, GROUPS - 1)
            beside("tensor", pe, "end")

        @block.vector
        def _(dve):
            def add(n, g):
                for s in range(GT):
                    dve.wait_ge(o_done, GT * n + s + 1)
                    dve.tensor_tensor(x[:, g * GT + s, :], out_ps[s % 2][:, :], x[:, g * GT + s, :], ALU.add).then_inc(o_added, 1)
                    beside("vector", dve, "step", chunks == 1)

            def stage(c, g, first=False, final=False):
                n = c * GROUPS + g
                if g == 0:
                    if not first:
                        dve.wait_ge(hid.relu_ready, HT * n)
                    dve.tensor_scalar(b1_now[:, :], b1_all[:, bass.ds(c + chunk0, 1), :].rearrange("p a n -> p (a n)"), 1.0, None, ALU.mult)\
                        .then_inc(now_ready, 1)
                    dve.wait_ge(now_ready, c + 1)
                for m in range(HT):
                    hid.vector_relu(dve, n, m, b1_now, first)
                    beside("vector", dve, "step", chunks == 1)
                    if g == 1 and m == 1:
                        w2.split_lo(dve, c + k0)
                if g == GROUPS - 1 and not (final and last):
                    w1.split_lo(dve, c + k0 + 1)
                if not first:
                    add(n - 1, (g - 1) % GROUPS)
                beside("vector", dve, g, first or final)

            dve.sem_inc(o_added, O_CREDIT)
            beside("vector", dve, "start")
            rotated(dve, chunks, GROUPS, stage)
            add(chunks * GROUPS - 1, GROUPS - 1)
            beside("vector", dve, "end")


def block_d(nc, sb, pb, sem, io, x, ident, xt_hi, xt_lo):
    w1, w2 = weights = Weights(sb, sem, "w1"), Weights(sb, sem, "w2")
    b1_all = sb("b1_all", [P, CHUNKS, HT])
    gate_all = sb("gate_all", [P, TILES, 2])
    second = sb("takes_second", [P, TILES])
    slots = sb("slots", [P, TILES], U32)
    is_second = sb("is_second", [P, SLOT_GROUPS, 2])
    w_index = sb("w_index", [P, SLOT_GROUPS, CHUNKS_PER_EXPERT], U32)
    b1_slots = sb("b1_slots", [P, SLOT_GROUPS, CHUNKS_PER_EXPERT, HT])
    idle = [pb("idle_out0", [P, D]), sb("idle_out1", [P, D])]
    free_f = sb("free_f", [P, GT])
    free_slots = sb("free_slots", [P, GT], U32)
    rows_now = sb("rows_now", [P, GT, D])

    norm_loaded = sem("d_loaded")
    gate_split = sem("gate_split")
    gate_done = sem("gate_done")
    gate_read = sem("gate_read")
    gate_turned = sem("gate_turned")
    bias_step = sem("bias_step")
    xn_used = sem("xn_used")
    rows_stored = [sem(f"rows_stored{i}") for i in range(2)]
    score_step = sem("score_step")
    gate_exp = sem("gate_exp")
    rows_v = io["xn_rows"].rearrange("(t p) d -> p t d", p=P)
    slots_v = io["xn_slots"].rearrange("(t p) d -> p t d", p=P)
    out_slots_v = io["out_slots"].rearrange("(t p) d -> p t d", p=P)

    with ExitStack() as part:
        def psb(name, shape, dt=F32):
            return part.enter_context(nc.sbuf_tensor(name, shape, dt))

        def ppb(name, shape, dt=F32):
            return part.enter_context(nc.psum_tensor(name, shape, dt))

        norm = Norm("n3", psb, ppb, sem, x, ident)
        gate_raw = psb("gate_raw", [P, KT, 2])
        gate_hi, gate_lo = psb("gate_hi", [P, KT, 2], F32R), psb("gate_lo", [P, KT, 2], F32R)
        bias2 = psb("bias2", [P, EXPERTS, D])
        gate_rows_ps = [ppb(f"gate_rows_ps{i}", [2, GROUP]) for i in range(2)]
        gate_rows = [psb(f"gate_rows{i}", [2, GROUP]) for i in range(2)]
        gate_ps = ppb("gate_ps", [P, TILES, 2])
        with nc.Block() as block:
            @block.sync
            def _(sp):
                sp.dma_start(gate_raw[:, :, :], io["gate"]).then_inc(norm_loaded, 16)
                sp.dma_start(bias2[:, :, :], io["b2"].partition_broadcast(P)).then_inc(norm_loaded, 16)
                sp.dma_start(b1_all[:, :, :], io["b1"]).then_inc(norm_loaded, 16)
                w1.load(sp, io["w1"], SHARED0)
                w2.load(sp, io["w2"], SHARED0)
                for g in range(GROUPS):
                    sp.wait_ge(norm.xn_ready, g + 1)
                    sp.dma_start(rows_v[:, g * GT:(g + 1) * GT, :], norm.xn[g % 2][:, :, :]).then_inc(rows_stored[g % 2], 16)
                for i in range(2):
                    sp.wait_ge(rows_stored[i], 16 * GROUPS // 2)
                sp.wait_ge(norm_loaded, 16 * 3)

            @block.gpsimd
            def _(gp):
                gp.wait_ge(norm_loaded, 16 * 3)
                gp.tensor_tensor(bias2[:, 0, :], bias2[:, 0, :], bias2[:, 1, :], ALU.add).then_inc(bias_step, 1)
                gp.wait_ge(bias_step, 1)
                gp.tensor_tensor(bias2[:, 0, :], bias2[:, 0, :], bias2[:, 2, :], ALU.add).then_inc(bias_step, 1)
                gp.wait_ge(bias_step, 2)
                w1.split_lo(gp, 0)
                for g in range(GROUPS):
                    gp.wait_ge(norm.xn_ready, g + 1)
                    rows = x[:, g * GT:(g + 1) * GT, :]
                    gp.tensor_tensor(rows, rows, bias2[:, 0, :].unsqueeze(1).broadcast_to([P, GT, D]), ALU.add).then_inc(xn_used, 1)

            @block.scalar
            def _(act):
                act.wait_ge(norm_loaded, 16 * 3)
                act.activation(gate_hi[:, :, :], gate_raw[:, :, :], ACT.Copy).then_inc(gate_split, 1)
                act.wait_ge(norm.eps_set, 1)

                def read_gate(g):
                    act.wait_ge(gate_done, g + 1)
                    if g >= 2:
                        act.wait_ge(gate_turned, g - 1)
                    act.activation(gate_rows[g % 2][:, :], gate_rows_ps[g % 2][:, :], ACT.Copy).then_inc(gate_read, 1)

                norm.scalar_sd(act, 0)
                w1.split_hi(act, 0)
                for g in range(GROUPS):
                    if g + 1 < GROUPS:
                        norm.scalar_sd(act, g + 1)
                    if g >= 2:
                        read_gate(g - 2)
                    norm.scalar_hi(act, g, lambda s: xt_hi[:, :, g * GROUP + s * P:g * GROUP + (s + 1) * P])
                read_gate(GROUPS - 2)
                read_gate(GROUPS - 1)

            @block.tensor
            def _(pe):
                def gate(g):
                    pe.wait_ge(norm.lo_ready, g * GT + GT)
                    cols = slice(g * GROUP, (g + 1) * GROUP)
                    three_pass(pe, gate_rows_ps[g % 2][:, :], [((gate_hi[:, k, :], gate_lo[:, k, :]),
                                                                (xt_hi[:, k, cols], xt_lo[:, k, cols])) for k in range(KT)])\
                        .then_inc(gate_done, 1)

                def turn_gate(g):
                    pe.wait_ge(gate_read, g + 1)
                    for s in range(GT):
                        mm = pe.transpose(gate_ps[:, g * GT + s, :], gate_rows[g % 2][:, s * P:(s + 1) * P], ident[0:2, 0:2])
                    mm.then_inc(gate_turned, 1)

                for g in range(GROUPS):
                    norm.tensor_turn(pe, g)
                    if g == 1:
                        pe.wait_ge(gate_split, 2)
                    if g:
                        gate(g - 1)
                    if g >= 2:
                        turn_gate(g - 2)
                gate(GROUPS - 1)
                turn_gate(GROUPS - 2)
                turn_gate(GROUPS - 1)

            @block.vector
            def _(dve):
                norm.start(dve)
                norm.vector_stats(dve, 0)
                dve.wait_ge(gate_split, 1)
                dve.tensor_tensor(gate_lo[:, :, :], gate_raw[:, :, :], f32(gate_hi[:, :, :]), ALU.subtract).then_inc(gate_split, 1)
                for g in range(GROUPS):
                    if g + 1 < GROUPS:
                        if g >= 1:
                            dve.wait_ge(rows_stored[(g + 1) % 2], 16)
                        norm.vector_stats(dve, g + 1)
                    norm.vector_lo(dve, g, lambda s: xt_hi[:, :, g * GROUP + s * P:g * GROUP + (s + 1) * P],
                                   lambda s: xt_lo[:, :, g * GROUP + s * P:g * GROUP + (s + 1) * P])
                dve.wait_ge(gate_turned, GROUPS)
                dve.tensor_copy(gate_all[:, :, :], gate_ps[:, :, :]).then_inc(score_step, 1)

    with ExitStack() as part:
        def psb(name, shape, dt=F32):
            return part.enter_context(nc.sbuf_tensor(name, shape, dt))

        def ppb(name, shape, dt=F32):
            return part.enter_context(nc.psum_tensor(name, shape, dt))

        idle_w2 = psb("idle_w2", [P, HT, D])
        idle_acc = [psb(f"idle_acc{e}", [P, D]) for e in range(2)]
        consts = psb("d_consts", [P, SLOT_CONSTS])
        triangle, ones = psb("d_triangle", [P, P]), psb("d_ones", [P, P])
        gate_max = psb("gate_max", [P, TILES])
        takes1 = [psb(f"takes1_{i}", [P, TILES + 1]) for i in range(2)]
        slot_f = psb("slot_f", [P, TILES])
        rank = psb("rank", [P, TILES + 1])
        w_index_f = psb("w_index_f", [P, SLOT_GROUPS, CHUNKS_PER_EXPERT])
        relu_b1 = psb("relu_b1", [P, CHUNKS, HT])
        rank_ps = ppb("rank_ps", [P, TILES + 1])
        idle_ps = [idle[0], ppb("idle_ps1", [P, D])]
        slot_consts_loaded = sem("slot_consts_loaded")
        sums_ready = sem("sums_ready")
        rank_done = sem("rank_done")
        slots_ready = sem("slots_ready")
        dispatch_loaded = sem("dispatch_loaded")
        scattered = sem("scattered")
        idle_loaded = [sem(f"idle_loaded{m}") for m in range(HT)]
        idle_step = sem("idle_step")
        idle_done = sem("idle_done")
        idle_read = sem("idle_read")
        rows_loaded = sem("rows_loaded")
        IDLE_TILES = 2 * CHUNKS_PER_EXPERT * HT
        idle_tiles = iter(range(IDLE_TILES))

        def sync_beside(sp, point, o_added, credit):
            if point == "start":
                sp.dma_start(consts[:, :], io["slot_consts"]).then_inc(slot_consts_loaded, 16)
                sp.dma_start(triangle[:, :], io["triangle"]).then_inc(slot_consts_loaded, 16)
                return
            for i in range(IDLE_TILES):
                if i >= HT:
                    sp.wait_ge(idle_step, i - HT + 2)
                sp.dma_start(idle_w2[:, i % HT, :], io["w2"][i // HT, :, i % HT, :]).then_inc(idle_loaded[i % HT], 16)
            sp.wait_ge(scattered, 16 * (TILES + GT))
            sp.dma_start(rows_now[:, :, :], slots_v[:, 0:GT, :]).then_inc(rows_loaded, 16)

        def pool_beside(gp, point, o_added, credit):
            def load(g):
                gp.dma_start(rows_now[:, :, :], rows_v[:, g * GT:(g + 1) * GT, :]).then_inc(dispatch_loaded, 16)

            if point == "start":
                gp.memset(ones[:, :], 1.0).then_inc(slot_consts_loaded, 16)
                load(0)
            if point == 0:
                gp.wait_ge(slots_ready, 1)
                gp.wait_ge(w1.lo_ready, 1)
                w1.gather(gp, io["w1"], w_index[:, 0, 0:1])
            if point in range(GROUPS):
                gp.wait_ge(dispatch_loaded, 16 * (point + 1))
                for s in range(GT):
                    t = point * GT + s
                    gp.indirect_dma_start(io["xn_slots"], bass.IndirectOffsetOnAxis(slots[:, t:t + 1], 0), rows_now[:, s, :], None)\
                        .then_inc(scattered, 16)
                if point + 1 < GROUPS:
                    gp.wait_ge(scattered, 16 * GT * (point + 1))
                    load(point + 1)
                else:
                    for s in range(GT):
                        gp.indirect_dma_start(io["xn_slots"], bass.IndirectOffsetOnAxis(free_slots[:, s:s + 1], 0), rows_now[:, s, :], None)\
                            .then_inc(scattered, 16)
            if point == "end":
                gp.wait_ge(w1.lo_ready, 2)
                w1.gather(gp, io["w1"], w_index[:, 0, 1:2])

        def scalar_beside(act, point, o_added, credit):
            if point == "start":
                act.wait_ge(score_step, 2)
                act.activation(gate_all[:, :, :], gate_all[:, :, :], ACT.Exp).then_inc(gate_exp, 1)
            if point == "end":
                act.wait_ge(idle_done, 2)
                act.activation(idle[1][:, :], idle_ps[1][:, :], ACT.Copy).then_inc(idle_read, 1)

        def tensor_beside(pe, point, o_added, credit):
            if point == 0:
                pe.wait_ge(slot_consts_loaded, 48)
                pe.wait_ge(sums_ready, 1)
                pe.matmul(rank_ps[:, :], triangle[:, :], takes1[0][:, :], start=True, stop=False)
                pe.matmul(rank_ps[:, :], ones[:, :], takes1[1][:, :], start=False, stop=True).then_inc(rank_done, 1)
            if point == "end":
                pe.wait_ge(idle_step, IDLE_TILES + 1)
                for e in range(2):
                    pe.matmul(idle_ps[e][:, :], ones[:, :], idle_acc[e][:, :], start=True, stop=True).then_inc(idle_done, 1)

        def vector_beside(dve, point, o_added, credit):
            steps = [0]

            def chained(ins):
                steps[0] += 1
                ins.then_inc(own_step, 1)
                dve.wait_ge(own_step, own_base + steps[0])

            def idle_sum(i):
                e, tile = divmod(i, CHUNKS_PER_EXPERT * HT)
                dve.wait_ge(idle_loaded[i % HT], 16 * (i // HT + 1))
                scale = relu_b1[:, i // HT, i % HT:i % HT + 1]
                if tile == 0:
                    ins = dve.tensor_scalar(idle_acc[e][:, :], idle_w2[:, i % HT, :], scale, None, ALU.mult)
                else:
                    dve.wait_ge(idle_step, i + 1)
                    ins = dve.scalar_tensor_tensor(idle_acc[e][:, :], idle_w2[:, i % HT, :], scale, idle_acc[e][:, :],
                                                   ALU.mult, ALU.add)
                ins.then_inc(idle_step, 1)

            if point == "step":
                idle_sum(next(idle_tiles))
            own_step, own_base = own_start, 0
            if point == "start":
                chained(dve.tensor_tensor(gate_max[:, :], gate_all[:, :, 0], gate_all[:, :, 1], ALU.max))
                dve.tensor_tensor(gate_all[:, :, :], gate_all[:, :, :], gate_max[:, :].unsqueeze(2).broadcast_to([P, TILES, 2]),
                                  ALU.subtract).then_inc(score_step, 1)
                dve.wait_ge(gate_exp, 1)
                chained(dve.tensor_tensor(second[:, :], gate_all[:, :, 1], gate_all[:, :, 0], ALU.is_gt))
                dve.memset(takes1[0][:, 0:1], 0.0)
                chained(dve.tensor_copy(takes1[0][:, 1:TILES + 1], second[:, :]))
                now = 0
                for d in (1, 2, 4, 8, 16):
                    old, new = takes1[now], takes1[1 - now]
                    dve.tensor_copy(new[:, 0:d], old[:, 0:d])
                    chained(dve.tensor_tensor(new[:, d:TILES + 1], old[:, d:TILES + 1], old[:, 0:TILES + 1 - d], ALU.add))
                    now = 1 - now
                dve.memset(takes1[0][:, TILES:TILES + 1], 0.0)
                dve.tensor_copy(takes1[0][:, 0:TILES], second[:, :]).then_inc(sums_ready, 1)
                dve.tensor_scalar(relu_b1[:, :, :], b1_all[:, :, :], 0.0, None, ALU.max).then_inc(idle_step, 1)
                dve.wait_ge(idle_step, 1)
            if point == 0:
                own_step = own_slots
                token, above, least, w_base = (consts[:, a:b] for a, b in SLOT_CONST_COLS)
                dve.wait_ge(slot_consts_loaded, 48)
                dve.wait_ge(rank_done, 1)
                chained(dve.tensor_copy(rank[:, :], rank_ps[:, :]))
                dve.tensor_tensor(is_second[:, :, 0], rank[:, TILES:TILES + 1].broadcast_to([P, SLOT_GROUPS]), least, ALU.is_ge)
                chained(dve.tensor_tensor(slot_f[:, :], second[:, :], above, ALU.mult))
                dve.tensor_scalar(is_second[:, :, 1], is_second[:, :, 0], -1.0, 1.0, ALU.mult, ALU.add)
                chained(dve.tensor_tensor(slot_f[:, :], slot_f[:, :], token, ALU.add))
                chained(dve.tensor_tensor(slot_f[:, :], slot_f[:, :], rank[:, 0:TILES], ALU.subtract))
                dve.tensor_scalar(free_f[:, :], token[:, 0:GT], rank[:, TILES:TILES + 1], float(TOKENS), ALU.subtract, ALU.add)
                chained(dve.tensor_copy(slots[:, :], slot_f[:, :]))
                dve.tensor_copy(free_slots[:, :], free_f[:, :])
                chained(dve.tensor_scalar(w_index_f[:, :, :], is_second[:, :, 0:1].broadcast_to([P, SLOT_GROUPS, CHUNKS_PER_EXPERT]),
                                          float(CHUNKS_PER_EXPERT * P), None, ALU.mult))
                chained(dve.tensor_tensor(w_index_f[:, :, :], w_index_f[:, :, :],
                                          w_base.unsqueeze(1).broadcast_to([P, SLOT_GROUPS, CHUNKS_PER_EXPERT]), ALU.add))
                dve.tensor_copy(w_index[:, :, :], w_index_f[:, :, :]).then_inc(slots_ready, 1)
                for g in range(SLOT_GROUPS):
                    ins = dve.tensor_scalar(b1_slots[:, g, :, :], b1_all[:, 0:CHUNKS_PER_EXPERT, :], is_second[:, g, 1:2],
                                            None, ALU.mult)
                chained(ins)
                for g in range(SLOT_GROUPS):
                    ins = dve.scalar_tensor_tensor(b1_slots[:, g, :, :], b1_all[:, CHUNKS_PER_EXPERT:2 * CHUNKS_PER_EXPERT, :],
                                                   is_second[:, g, 0:1], b1_slots[:, g, :, :], ALU.mult, ALU.add)
                chained(ins)

        own_start, own_slots = sem("own_start"), sem("own_slots")

        extra = {"sync": sync_beside, "gpsimd": pool_beside, "scalar": scalar_beside, "tensor": tensor_beside,
                 "vector": vector_beside}
        shared_ffn(nc, psb, ppb, sem, "s0", x, xt_hi, xt_lo, b1_all, weights, io, 0, SHARED0, 1, extra)

    with ExitStack() as part:
        def psb(name, shape, dt=F32):
            return part.enter_context(nc.sbuf_tensor(name, shape, dt))

        def ppb(name, shape, dt=F32):
            return part.enter_context(nc.psum_tensor(name, shape, dt))

        hid = Hidden("r", psb, ppb, sem)
        C = CHUNKS_PER_EXPERT
        STAGES = SLOT_GROUPS * C
        xs = psb("xs_hi", [P, KT, GROUP], F32R), psb("xs_lo", [P, KT, GROUP], F32R)
        b1_now = [psb(f"r_b1_now{i}", [P, HT]) for i in range(2)]
        index_now = [psb(f"index_now{i}", [P, 1], U32) for i in range(2)]
        expert_now = psb("expert_now", [P, 2])
        turned = ppb("r_turned", [P, KT, P])
        out_ps = [ppb(f"r_out_ps{i}", [P, D]) for i in range(GT)]
        turn_done = sem("r_turn_done")
        xs_hi_ready = sem("xs_hi_ready")
        xs_lo_ready = sem("xs_lo_ready")
        b1_ready = sem("r_b1_ready")
        index_ready = [sem(f"index_ready{i}") for i in range(2)]
        o_done = sem("r_o_done")
        o_read = sem("r_o_read")
        READ_CREDIT = GT
        idle_chain = sem("idle_chain")
        out_stored = sem("out_stored")
        gather_turn = sem("gather_turn")
        last_but_one = sem("last_but_one")

        with nc.Block() as block:
            @block.sync
            def _(sp):
                def store(g):
                    sp.wait_ge(idle_chain, g * 2 + 2)
                    sp.dma_start(out_slots_v[:, bass.ds(g * GT, GT), :], rows_now[:, :, :]).then_inc(out_stored, 16)

                def load(g):
                    sp.dma_start(rows_now[:, :, :], slots_v[:, bass.ds(g * GT, GT), :]).then_inc(rows_loaded, 16)

                sp.wait_ge(turn_done, GT)
                load(1)
                with sp.Fori(0, SLOT_GROUPS - 2) as g:
                    store(g)
                    sp.wait_ge(out_stored, g * 16 + 16)
                    load(g + 2)
                store(SLOT_GROUPS - 2)
                sp.wait_ge(w1.lo_ready, STAGES + 1)
                w1.load(sp, io["w1"], SHARED0 + 1)
                sp.wait_ge(w2.lo_ready, STAGES + 1)
                w2.load(sp, io["w2"], SHARED0 + 1)
                store(SLOT_GROUPS - 1)

            @block.gpsimd
            def _(gp):
                def stage(g, c, first=False, final=False):
                    n = g * C + c
                    for m in range(HT):
                        hid.pool_lo(gp, n, m, c % 2)
                        if m == 1:
                            gp.wait_ge(index_ready[1], n + 1)
                            gp.sem_inc(gather_turn, 1)
                            w2.gather(gp, io["w2"], index_now[1][:, :])
                    if not (final and c >= C - 2):
                        gp.wait_ge(index_ready[0], n + 1)
                        gp.sem_inc(gather_turn, 1)
                        w1.gather(gp, io["w1"], index_now[0][:, :])

                rotated(gp, SLOT_GROUPS, C, stage)

            @block.scalar
            def _(act):
                def slots_hi(g, tiles):
                    for s in tiles:
                        act.wait_ge(turn_done, g * GT + s + 1)
                        act.activation(xs[0][:, :, s * P:(s + 1) * P], turned[:, :, :], ACT.Copy).then_inc(xs_hi_ready, 1)

                def stage(g, c, first=False, final=False):
                    n = g * C + c
                    for m in range(HT):
                        hid.scalar_hi(act, n, m, c % 2)
                        if m == 0 and not first:
                            w2.split_hi(act, n, shared=False)
                    turning = c == C - 1 and not final
                    if turning:
                        slots_hi(g + 1, [0])
                    w1.split_hi(act, n + 2, shared=final and c == C - 1)
                    if turning:
                        slots_hi(g + 1, range(1, GT))

                slots_hi(0, range(GT))
                rotated(act, SLOT_GROUPS, C, stage)
                act.wait_ge(last_but_one, 1)
                w2.split_hi(act, STAGES, shared=False)

            @block.tensor
            def _(pe):
                def turn(g, s, first=False):
                    if not first or s:
                        pe.wait_ge(xs_lo_ready, g * GT + s)
                    for k in range(KT):
                        mm = pe.transpose(turned[:, k, :], rows_now[:, s, k * P:(k + 1) * P], ident[:, :])
                    mm.then_inc(turn_done, 1)

                def output(n, g, c, turning=False, mark=False):
                    pe.wait_ge(w2.lo_ready, n + 2)
                    pe.wait_ge(hid.lo_ready, HT * n + HT)
                    if turning:
                        pe.wait_ge(rows_loaded, 16 * (g + 2))
                    for s in range(GT):
                        if turning:
                            turn(g + 1, s)
                        if c == 0:
                            pe.wait_ge(o_read, GT * g + s + 1)
                        mm = three_pass(pe, out_ps[s][:, :], hid.terms(c % 2, s, w2), start=c == 0, stop=c == C - 1)
                        if c == C - 1:
                            mm.then_inc(o_done, 1)
                    if mark:
                        mm.then_inc(last_but_one, 1)

                def stage(g, c, first=False, final=False):
                    n = g * C + c
                    pe.wait_ge(w1.lo_ready, n + 2)
                    if c == 0:
                        pe.wait_ge(xs_lo_ready, g * GT + GT)
                    for m in range(HT):
                        hid.product(pe, n, m, w1, lambda k: (xs[0][:, k, :], xs[1][:, k, :]), first)
                    if not first:
                        output(n - 1, g if c else g - 1, (c - 1) % C, turning=c == C - 1 and not final,
                               mark=c == C - 1 and final)

                pe.wait_ge(rows_loaded, 16)
                for s in range(GT):
                    turn(0, s, first=True)
                rotated(pe, SLOT_GROUPS, C, stage)
                output(STAGES - 1, SLOT_GROUPS - 1, C - 1)

            @block.vector
            def _(dve):
                def slots_lo(g, tiles):
                    for s in tiles:
                        dve.wait_ge(xs_hi_ready, g * GT + s + 1)
                        dve.tensor_tensor(xs[1][:, :, s * P:(s + 1) * P], turned[:, :, :],
                                          f32(xs[0][:, :, s * P:(s + 1) * P]), ALU.subtract).then_inc(xs_lo_ready, 1)

                def biases(n, g, c):
                    dve.tensor_scalar(b1_now[c % 2][:, :], b1_slots[:, bass.ds(g, 1), c, :].rearrange("p a n -> p (a n)"), 1.0, None, ALU.mult)\
                        .then_inc(b1_ready, 1)

                def index(i, g, c):
                    dve.tensor_scalar(index_now[i][:, :], w_index[:, bass.ds(g, 1), c], 1.0, None, ALU.mult).then_inc(index_ready[i], 1)

                def evacuate(g):
                    dve.tensor_copy(expert_now[:, :], is_second[:, bass.ds(g, 1), :].rearrange("p a n -> p (a n)"))\
                        .then_inc(idle_chain, 1)
                    dve.wait_ge(idle_chain, g * 2 + 1)
                    for s in range(GT):
                        dve.wait_ge(o_done, g * GT + s + 1)
                        dve.scalar_tensor_tensor(rows_now[:, s, :], idle[1][:, :], expert_now[:, 1:2], out_ps[s][:, :],
                                                 ALU.mult, ALU.add).then_inc(o_read, 1)
                    dve.wait_ge(o_read, g * GT + GT + READ_CREDIT)
                    for s in range(GT):
                        ins = dve.scalar_tensor_tensor(rows_now[:, s, :], idle[0][:, :], expert_now[:, 0:1], rows_now[:, s, :],
                                                       ALU.mult, ALU.add)
                    ins.then_inc(idle_chain, 1)

                def stage(g, c, first=False, final=False):
                    n = g * C + c
                    dve.wait_ge(b1_ready, n + 1)
                    for m in range(HT):
                        hid.vector_relu(dve, n, m, b1_now[c % 2], first)
                        if m == 1:
                            if not first:
                                w2.split_lo(dve, n)
                                dve.wait_ge(w2.lo_ready, n + 1)
                            index(1, g, c)
                    turning = c == C - 1 and not final
                    if turning:
                        slots_lo(g + 1, [0])
                    w1.split_lo(dve, n + 2)
                    dve.wait_ge(w1.lo_ready, n + 3)
                    if not (final and c >= C - 2):
                        index(0, g + (c + 2) // C, (c + 2) % C)
                    if not (final and c == C - 1):
                        biases(n + 1, g + (c + 1) // C, (c + 1) % C)
                    if turning:
                        slots_lo(g + 1, range(1, GT))
                    if c == 0 and not first:
                        evacuate(g - 1)

                dve.sem_inc(o_read, READ_CREDIT)
                biases(0, 0, 0)
                slots_lo(0, range(GT))
                rotated(dve, SLOT_GROUPS, C, stage)
                w2.split_lo(dve, STAGES)
                dve.wait_ge(out_stored, 16 * (SLOT_GROUPS - 1))
                evacuate(SLOT_GROUPS - 1)

    routed_in = [rows_now, sb("routed_in", [P, GT, D])]
    fetched = [sem(f"fetched{i}") for i in range(2)]
    routed_added = sem("routed_added")
    stored = sem("stored")
    out_v = io["out"].rearrange("(t p) d -> p t d", p=P)
    rest = CHUNKS_PER_EXPERT - 1

    def sync_last(sp, point, o_added, credit):
        if point == "start":
            return
        for g in range(GROUPS):
            sp.wait_ge(routed_added, GT * (g + 1))
            sp.wait_ge(o_added, GT * (GROUPS * (rest - 1) + g + 1) + credit)
            sp.dma_start(out_v[:, g * GT:(g + 1) * GT, :], x[:, g * GT:(g + 1) * GT, :]).then_inc(stored, 16)
        sp.wait_ge(stored, 16 * GROUPS)

    def pool_last(gp, point, o_added, credit):
        groups = {"start": (0, 1), 1: (2,), 2: (3,)}.get(point, ())
        for g in groups:
            if g == 0:
                gp.wait_ge(out_stored, 16 * SLOT_GROUPS)
            if g >= 2:
                gp.wait_ge(routed_added, GT * (g - 1))
            for s in range(GT):
                t = g * GT + s
                gp.indirect_dma_start(routed_in[g % 2][:, s, :], None, io["out_slots"], bass.IndirectOffsetOnAxis(slots[:, t:t + 1], 0))\
                    .then_inc(fetched[g % 2], 16)

    def vector_last(dve, point, o_added, credit):
        groups = {1: (0, 1), 2: (2,), 3: (3,)}.get(point, ())
        if groups:
            dve.wait_ge(o_added, GT * (GROUPS * (rest - 1) + point) + credit)
        for g in groups:
            for s in range(GT):
                if s == 0:
                    dve.wait_ge(fetched[g % 2], 16 * GT * (g // 2 + 1))
                rows = x[:, g * GT + s, :]
                dve.tensor_tensor(rows, routed_in[g % 2][:, s, :], rows, ALU.add).then_inc(routed_added, 1)
            dve.wait_ge(routed_added, GT * (g + 1))

    shared_ffn(nc, sb, pb, sem, "s1", x, xt_hi, xt_lo, b1_all, weights, io, 1 + STAGES, SHARED0 + 1, rest,
               {"sync": sync_last, "gpsimd": pool_last, "vector": vector_last})


def slot_constants():
    import numpy as np
    p = np.arange(P)[:, None]
    token = np.arange(TILES)[None, :] * P + p
    least = np.broadcast_to(TOKENS - GROUP * np.arange(SLOT_GROUPS)[None, :], (P, SLOT_GROUPS))
    rows = np.arange(CHUNKS_PER_EXPERT)[None, :] * P + p
    return np.concatenate([token, SLOTS - 1 - token, least, rows], 1).astype(np.float32)


def build(nc, io):
    with ExitStack() as ctx:
        def sem(name):
            return ctx.enter_context(nc.semaphore(name))

        def cross_sem(name):
            cross_sems.append(nc.alloc_semaphore(name))
            return cross_sems[-1]

        cross_sems = []

        def scope():
            stack = ctx.enter_context(ExitStack())

            def sb(name, shape, dt=F32):
                return stack.enter_context(nc.sbuf_tensor(name, shape, dt))

            def pb(name, shape, dt=F32):
                return stack.enter_context(nc.psum_tensor(name, shape, dt))

            return stack, sb, pb

        _, sb, pb = scope()
        x = sb("x_res", [P, TILES, D])
        ident = sb("ident", [P, P])
        const_loaded = cross_sem("const_loaded")

        cross, csb, cpb = scope()
        cos_k, sin_k = csb("cos_k", [P, TK]), csb("sin_k", [P, TK])
        key_last, value_last = csb("key_last", [P, KT, BATCH]), csb("value_last", [P, KT, BATCH])
        ctx_raw = [csb(f"ctx_raw{i}", [P, KT, 2 * TKM]) for i in range(2)]
        ctx_loaded = [cross_sem(f"ctx_loaded{i}") for i in range(2)]
        weights = [(csb(n + "_hi", [P, KT, D], F32R), csb(n + "_lo", [P, KT, D], F32R)) for n in ("wk", "wv", "wo")]
        with nc.Block() as block:
            @block.sync
            def _(sp):
                sp.dma_start(ident[:, :], io["ident"]).then_inc(const_loaded, 16)
                sp.dma_start(cos_k[:, :], io["cos"]).then_inc(const_loaded, 16)
                sp.dma_start(sin_k[:, :], io["sin"]).then_inc(const_loaded, 16)
        stack, asb, apb = scope()
        block_a(nc, asb, apb, cross_sem, io, x, ident, cos_k, sin_k, key_last, value_last, weights, const_loaded,
                ctx_raw, ctx_loaded)
        stack.close()
        stack, bsb, bpb = scope()
        block_b(nc, bsb, bpb, cross_sem, io, x, ident, cos_k, sin_k, key_last, value_last, weights, ctx_raw, ctx_loaded)
        stack.close()
        cross.close()
        nc.clear_and_free_semaphores(cross_sems)
        nc.all_engine_barrier()

        _, sb, pb = scope()
        xt_hi, xt_lo = sb("x_t_hi", [P, KT, TOKENS], F32R), sb("x_t_lo", [P, KT, TOKENS], F32R)
        stack, csb, cpb = scope()
        block_c(nc, csb, cpb, sem, io, x, ident, xt_hi, xt_lo)
        stack.close()
        stack, dsb, dpb = scope()
        block_d(nc, dsb, dpb, sem, io, x, ident, xt_hi, xt_lo)
        stack.close()


def kernel(**inputs):
    import ml_dtypes
    import numpy as np
    import concourse.bacc as bacc
    from concourse.bass_utils import run_bass_kernel_spmd

    a = {n: np.asarray(v) for n, v in inputs.items()}
    half = X_HEAD // 2
    inv_freq = (1.0 / np.float32(10000.0) ** (np.arange(0, X_HEAD, 2, dtype=np.float32) / np.float32(X_HEAD))).astype(np.float32)
    angle = np.outer(np.arange(TK, dtype=np.float32), inv_freq).astype(np.float32).T
    cos, sin = np.cos(angle), np.sin(angle)
    wq, wk, wv = (a[f"L0_attn_{n}"].reshape(HEADS, 2, DH, KT, P) for n in ("Wq", "Wk", "Wv"))
    w_qk = np.concatenate([wq, wk], 1).transpose(0, 4, 3, 1, 2).reshape(HEADS, P, KT, 4 * DH)
    w_v = wv.transpose(0, 4, 3, 1, 2).reshape(HEADS, P, KT, 2 * DH)
    w_o = a["L0_attn_Wo"].reshape(D, HEADS, 2, DH).transpose(1, 3, 2, 0)
    w1 = np.concatenate([a["L0_ffn_w1"], a["L0_ffn_sw1"][None]]).reshape(EXPERTS, KT, P, CHUNKS_PER_EXPERT, HC)
    w2 = np.concatenate([a["L0_ffn_w2"], a["L0_ffn_sw2"][None]]).reshape(CHUNKS, HT, P, D)
    b1 = np.concatenate([a["L0_ffn_b1"], a["L0_ffn_sb1"][None]]).reshape(CHUNKS, HT, P)
    b2 = np.concatenate([a["L0_ffn_b2"], a["L0_ffn_sb2"][None]])
    same = np.arange(4)[:, None] == np.arange(P)[None, :] // TQ
    arrays = {
        "x": a["x"].reshape(TOKENS, D),
        "ctx_main": a["ctx_1024"][:, :TKM].reshape(BATCH * TKM, D).T,
        "ctx_last": a["ctx_1024"][:, TKM].T,
        "Wq": a["L0_xattn_Wq"].T, "Wk": a["L0_xattn_Wk"].T, "Wv": a["L0_xattn_Wv"].T, "Wo": a["L0_xattn_Wo"].T,
        "ident": np.eye(P, dtype=np.float32),
        "cos": np.tile(cos, (P // half, 1)),
        "sin": np.tile(np.concatenate([-sin, sin]), (P // X_HEAD, 1)),
        "lq1": a["L0_attn_lambda_q1"], "lk1": a["L0_attn_lambda_k1"],
        "lq2": a["L0_attn_lambda_q2"], "lk2": a["L0_attn_lambda_k2"],
        "rms": a["L0_attn_rms_scale"].reshape(2, DH).T,
        "mask_rows": same.astype(ml_dtypes.bfloat16),
        "mask_cols": np.tile(np.where(same, 0.0, MASKED), (1, D // P)).astype(ml_dtypes.bfloat16),
        "w_qk": w_qk, "w_v": w_v, "w_o": w_o,
        "gate": a["L0_ffn_gate_w"].reshape(2, KT, P).transpose(2, 1, 0),
        "w1": w1.transpose(0, 3, 2, 1, 4).reshape(CHUNKS, P, KT, HC),
        "w2": w2.transpose(0, 2, 1, 3),
        "b1": b1.transpose(2, 0, 1),
        "b2": b2,
        "slot_consts": slot_constants(),
        "triangle": np.triu(np.ones((P, P), np.float32), 1),
    }
    nc = bacc.Bacc("TRN2", target_bir_lowering=False, num_devices=1)
    feeds, io = {}, {}
    for name, v in arrays.items():
        v = np.ascontiguousarray(v)
        feeds[f"in_{name}_dram"] = v
        io[name] = nc.dram_tensor(f"in_{name}_dram", v.shape, mybir.dt.from_np(v.dtype), kind="ExternalInput").ap()
    io["queries"] = nc.dram_tensor("queries_dram", (P, KT, TOKENS), F32, kind="Internal").ap()
    for name, rows in (("xn_rows", TOKENS), ("xn_slots", SLOTS), ("out_slots", SLOTS)):
        io[name] = nc.dram_tensor(name + "_dram", (rows, D), F32, kind="Internal").ap()
    io["out"] = nc.dram_tensor("out_0_dram", (TOKENS, D), F32, kind="ExternalOutput").ap()
    build(nc, io)
    r = run_bass_kernel_spmd(nc, [feeds], core_ids=[0])
    return np.asarray(r.results[0]["out_0_dram"]).reshape(BATCH, TQ, D)
```
